# Optimizing a Trainium2 kernel written in Bass

```python
import numpy as np
import jax
import jax.numpy as jnp

def _softmax(x, axis=-1):
    return jax.nn.softmax(x, axis=axis)

def _gelu(x):
    return jax.nn.gelu(x, approximate=True)

def _silu(x):
    return jax.nn.silu(x)

def _sigmoid(x):
    return jax.nn.sigmoid(x)

def _layernorm(x, axis=-1, eps=1e-05):
    m = jnp.mean(x, axis=axis, keepdims=True)
    v = jnp.var(x, axis=axis, keepdims=True)
    return (x - m) / jnp.sqrt(v + eps)

def _scatter_add(tgt, idx, src, axis=0):
    return tgt.at[idx].add(src)

def _segment_sum(src, seg, n):
    return jax.ops.segment_sum(src, seg, n)
kernel_name = 'mk_adaln_d1_jaxref_r4_cf851a'

def setup_inputs(seed: int=0):
    np.random.seed(seed)
    _w = jnp.asarray

    def _L0_attn_setup():
        import jax, jax.numpy as jnp
        import numpy as np
        B, SQ, H = (2, 512, 512)
        NH = 16
        HN = H // NH
        key = jax.random.key(seed)
        ks = jax.random.split(key, 6)
        query = jax.random.normal(ks[0], (B, SQ, H), dtype=jnp.float32)
        k_in = jax.random.normal(ks[1], (B, SQ, H), dtype=jnp.float32)
        v_in = jax.random.normal(ks[2], (B, SQ, H), dtype=jnp.float32)
        Wqkv = jax.random.normal(ks[3], (3 * H, H), dtype=jnp.float32) * (1.0 / np.sqrt(H))
        Wproj = jax.random.normal(ks[4], (H, H), dtype=jnp.float32) * (1.0 / np.sqrt(H))
        bproj = jnp.zeros((H,), dtype=jnp.float32)
        return {'query': query, 'key': k_in, 'value': v_in, 'Wqkv': Wqkv, 'Wproj': Wproj, 'bproj': bproj}
    _L0_attn_in = _L0_attn_setup()

    def _L0_ffn_setup():
        import jax, jax.numpy as jnp
        import numpy as np
        B, S, D, H = (4, 512, 512, 2048)

        def fwht(x):
            orig_shape = x.shape
            n = orig_shape[-1]
            x = x.reshape(-1, n)
            h = 1
            while h < n:
                xb = x.reshape(-1, n // (2 * h), 2, h)
                a = xb[:, :, 0, :]
                b = xb[:, :, 1, :]
                x = jnp.stack([a + b, a - b], axis=2).reshape(-1, n)
                h *= 2
            scale = jnp.asarray(1.0 / np.sqrt(n), dtype=x.dtype)
            return (x * scale).reshape(orig_shape)
        key = jax.random.key(seed)
        kx, k1, k2, k3 = jax.random.split(key, 4)
        x = jax.random.normal(kx, (B, S, D), dtype=jnp.float32)
        W1 = jax.random.normal(k1, (H, D), dtype=jnp.float32) * (1.0 / np.sqrt(D))
        W2 = jax.random.normal(k2, (D, H), dtype=jnp.float32) * (1.0 / np.sqrt(H))
        W3 = jax.random.normal(k3, (H, D), dtype=jnp.float32) * (1.0 / np.sqrt(D))
        return {'x': x, 'W1': W1, 'W2': W2, 'W3': W3}
    _L0_ffn_in = _L0_ffn_setup()
    _L0_c = _w((lambda *s: np.random.randn(*s).astype(np.float32) * 0.05)(2, 512))
    _L0_wmod = _w((lambda *s: np.random.randn(*s).astype(np.float32) * 0.05)(512, 6 * 512) * 512 ** (-0.5))
    _d = {'L0_attn_query': _L0_attn_in['query'], 'L0_attn_key': _L0_attn_in['key'], 'L0_attn_value': _L0_attn_in['value'], 'L0_attn_Wqkv': _L0_attn_in['Wqkv'], 'L0_attn_Wproj': _L0_attn_in['Wproj'], 'L0_attn_bproj': _L0_attn_in['bproj'], 'L0_ffn_W1': _L0_ffn_in['W1'], 'L0_ffn_W2': _L0_ffn_in['W2'], 'L0_ffn_W3': _L0_ffn_in['W3'], 'L0_c': _L0_c, 'L0_wmod': _L0_wmod}
    _x0 = _d['L0_attn_query']
    _d['L0_attn_query'] = jax.random.normal(jax.random.fold_in(jax.random.key(seed), 1), (2, 2048, 512), dtype=_x0.dtype)
    del _x0
    return _d

def reference(L0_attn_query, L0_attn_key, L0_attn_value, L0_attn_Wqkv, L0_attn_Wproj, L0_attn_bproj, L0_ffn_W1, L0_ffn_W2, L0_ffn_W3, L0_c, L0_wmod):

    def _L0_attn_ref(query, key, value, Wqkv, Wproj, bproj):
        import jax, jax.numpy as jnp
        import numpy as np
        B, SQ, H = (2, 512, 512)
        NH = 16
        HN = H // NH
        b, sq, h = query.shape
        nh, hn = (NH, HN)
        norm = 1.0 / jnp.sqrt(jnp.asarray(hn, query.dtype))
        x = jnp.transpose(query, (1, 0, 2)).reshape(sq * b, h)
        mixed = x @ Wqkv.T
        mixed = mixed.reshape(sq, b, nh, 3, hn)
        q = mixed[..., 0, :]
        k = mixed[..., 1, :]
        v = mixed[..., 2, :]
        q = q.reshape(sq, b * nh, hn).transpose(1, 0, 2)
        k = k.reshape(sq, b * nh, hn).transpose(1, 0, 2)
        v = v.reshape(sq, b * nh, hn).transpose(1, 0, 2)
        attn = jnp.einsum('gqd,gkd->gqk', q, k) * norm
        attn = jax.nn.softmax(attn, axis=-1)
        ctx = jnp.einsum('gqk,gkd->gqd', attn, v)
        ctx = ctx.reshape(nh, b, sq, hn)
        ctx = jnp.transpose(ctx, (2, 1, 0, 3)).reshape(sq * b, h)
        out = ctx @ Wproj.T + bproj
        out = out.reshape(sq, b, h)
        return jnp.transpose(out, (1, 0, 2))

    def _L0_ffn_ref(x, W1, W2, W3):
        import jax, jax.numpy as jnp
        import numpy as np
        B, S, D, H = (4, 512, 512, 2048)

        def fwht(x):
            orig_shape = x.shape
            n = orig_shape[-1]
            x = x.reshape(-1, n)
            h = 1
            while h < n:
                xb = x.reshape(-1, n // (2 * h), 2, h)
                a = xb[:, :, 0, :]
                b = xb[:, :, 1, :]
                x = jnp.stack([a + b, a - b], axis=2).reshape(-1, n)
                h *= 2
            scale = jnp.asarray(1.0 / np.sqrt(n), dtype=x.dtype)
            return (x * scale).reshape(orig_shape)
        up_gate = jnp.einsum('bsd,hd->bsh', x, W1)
        up_lin = jnp.einsum('bsd,hd->bsh', x, W3)
        hidden = jax.nn.silu(up_gate) * up_lin
        hidden = fwht(hidden)
        out = jnp.einsum('bsh,dh->bsd', hidden, W2)
        return out
    x = L0_attn_query
    mod = (_silu(L0_c) @ L0_wmod).reshape(L0_c.shape[0], 6, 1, -1)
    sa, ca, ga, sb, cb, gb = (mod[:, 0], mod[:, 1], mod[:, 2], mod[:, 3], mod[:, 4], mod[:, 5])
    ga = (2 * (ga >= 0) - 1) * jnp.maximum(jnp.abs(ga), 0.25)
    gb = (2 * (gb >= 0) - 1) * jnp.maximum(jnp.abs(gb), 0.25)
    h = _layernorm(x, axis=-1) * (1 + ca) + sa
    x = x + ga * _L0_attn_ref(h, L0_attn_key, L0_attn_value, L0_attn_Wqkv, L0_attn_Wproj, L0_attn_bproj)
    h = _layernorm(x, axis=-1) * (1 + cb) + sb
    x = x + gb * _L0_ffn_ref(h, L0_ffn_W1, L0_ffn_W2, L0_ffn_W3)
    return x

_drawn_inputs = setup_inputs


def setup_inputs(seed=0):
    import zlib

    import numpy as np

    out = dict(_drawn_inputs(seed))
    spreads = {'L0_attn_bproj': (0.0, 1.191)}
    factors = {'L0_attn_Wqkv': 3.951, 'L0_attn_Wproj': 3.93}
    for name, (base, spread) in spreads.items():
        noise = np.random.default_rng([zlib.crc32(name.encode()), seed]).standard_normal(out[name].shape)
        drawn = base * np.exp(spread * noise) if base else spread * noise
        out[name] = jnp.asarray(drawn.astype(out[name].dtype))
    for name, factor in factors.items():
        out[name] = (out[name] * factor).astype(out[name].dtype)
    return out
```

```python
from contextlib import ExitStack

import concourse.bass as bass
from concourse import mybir

ALU = mybir.AluOpType
ACT = mybir.ActivationFunctionType
X = mybir.AxisListType.X
F32 = mybir.dt.float32
F32R = mybir.dt.float32r

P = 128
B, S, D = 2, 2048, 512
NH, HD = 16, 32
HID = 2048
DC = D // P
HC = HID // P
TK = 4
TOK = TK * P
ST = S // TOK
TILES = B * ST
HEADS = B * NH
KT = S // P
QJ = S // TOK
EPS = 1e-5
HI, LO = 0, 1
TERMS = ((HI, HI), (HI, LO), (LO, HI))
SA, CA, SB, CB, GA, GB = range(6)
COLUMN = (0, 1, 2, 3, 4, 5)
WMOD_AT = {SA: 0, CA: 1, GA: 2, SB: 3, CB: 4, GB: 5}


def raw(ap):
    return ap.bitcast(F32)


def split_product(pe, out, stationary, moving, chunks, start=True, stop=True):
    last = None
    n = len(chunks) * len(TERMS)
    i = 0
    for c in chunks:
        for a, b in TERMS:
            last = pe.matmul(out, stationary(a, c), moving(b, c),
                             start=start and i == 0, stop=stop and i == n - 1)
            i += 1
    return last


def prepare(nc, ins, keep, scratch):
    ident, wqk, wv, wp, shift, scale1, gains = (keep[k] for k in ("ident", "wqk", "wv", "wp", "shift", "scale1", "gains"))
    NAT, OB, BANKS = 4, 4, 4
    SHIFTS = [SA, CA, SB, CB]
    jobs = [("rows", "q", j) for j in range(4)] + [("rows", "k", j) for j in range(4)]
    jobs += [("rows", "v", j) for j in range(4)] + [("rows", "p", j) for j in range(4)]
    jobs += [("mod", k, 0) for k in SHIFTS] + [("gain", k, b) for k in (GA, GB) for b in range(B)]
    jobs += [("w2", "t", c) for c in range(HC)]
    jobs += [("rows", "w1", j) for j in range(HC)] + [("rows", "w3", j) for j in range(HC)]
    jobs += [("had", "w2", c) for c in range(HC)]
    row_jobs = [n for n, j in enumerate(jobs) if j[0] == "rows"]
    store_jobs = [n for n, j in enumerate(jobs) if j[1] in ("w1", "w3") or j[0] == "had"]
    first_w1 = next(n for n, j in enumerate(jobs) if j[1] == "w1")
    last_w2t = first_w1 - 1
    kinds = SHIFTS + [GA, GB]
    kind_last_job = {k: max(n for n, j in enumerate(jobs) if j[0] in ("mod", "gain") and j[1] == k) for k in kinds}

    with ExitStack() as ctx:
        def sb(name, shape, dt=F32):
            return ctx.enter_context(nc.sbuf_tensor(name, shape, dt))

        def sem(name):
            return ctx.enter_context(nc.semaphore(name))

        had = sb("had", [P, P])
        nat = sb("nat", [P, NAT, D])
        w2a = sb("w2a", [P, HC, D])
        w2b = sb("w2b", [P, HC * D])
        wm = sb("wm", [P, 2, DC, D])
        ob = sb("ob", [P, OB, 2, D], F32R)
        ct = sb("ct", [P, DC, B])
        sc = sb("sc", [P, DC, B])
        scb = sb("scb", [P, B, DC, P])
        zero = sb("zero", [P, P])
        gtmp = sb("gtmp", [P, 2, D])
        graw = sb("graw", [P, D])
        bpb = sb("bpb", [P, D])
        mark = sb("mark", [P, 2])
        ps = ctx.enter_context(nc.psum_tensor("ps_prep", [P, BANKS, D], F32))

        const_in = sem("p_const_in")
        nat_in = [sem(f"p_nat_in{i}") for i in range(NAT)]
        w2_in = sem("p_w2_in")
        wm_in = [sem(f"p_wm_in{i}") for i in range(2)]
        job_pe = sem("p_job_pe")
        job_act = sem("p_job_act")
        job_dve = sem("p_job_dve")
        silu_done = sem("p_silu")
        scb_done = sem("p_scb")
        chain = sem("p_chain")
        fly = sem("p_butterfly")
        ob_out = [sem(f"p_ob_out{i}") for i in range(OB)]

        def rows_of(name, j):
            if name in "qkv":
                part = "qkv".index(name)
                return [(ins["wqkv"][(4 * j + h) * 3 * HD + part * HD:][:HD, :], h * HD, HD) for h in range(4)]
            w = {"p": ins["wproj"], "w1": ins["w1"], "w3": ins["w3"]}[name]
            return [(w[j * P:(j + 1) * P, :], 0, P)]

        def target(n):
            kind, name, j = jobs[n]
            if name in ("q", "k"):
                return [wqk[:, j + 4 * (name == "k"), s, :, :] for s in (HI, LO)]
            if name in ("v", "p") :
                w = wv if name == "v" else wp
                return [w[:, s, :, j * P:(j + 1) * P] for s in (HI, LO)]
            slot = store_jobs.index(n) % OB
            if kind == "had":
                return [ob[:, slot, s, :] for s in (HI, LO)]
            return [ob[:, slot, s, :].rearrange("p (c m) -> p c m", c=DC) for s in (HI, LO)]

        def bank(n, kind):
            v = ps[:, n % BANKS, :]
            return v.rearrange("p (c m) -> p c m", c=DC) if kind == "rows" else v

        def ob_free(eng, n):
            if n in store_jobs:
                m = store_jobs.index(n)
                if m >= OB:
                    eng.wait_ge(ob_out[m % OB], 16 * (m // OB))

        with nc.Block() as block:

            @block.sync
            def _(sp):
                sp.dma_start(ident[:, :], ins["identity"]).then_inc(const_in, 16)
                sp.dma_start(had[:, :], ins["hadamard"]).then_inc(const_in, 16)
                with nc.allow_non_contiguous_dma("c is 1024 numbers"):
                    for b in range(B):
                        sp.dma_start(ct[:, :, b], ins["c"][b].rearrange("(k p) -> p k", p=P)).then_inc(const_in, 16)
                sp.dma_start(bpb[:, :], ins["bproj"].partition_broadcast(P)).then_inc(const_in, 16)

                def load_rows(m):
                    n = row_jobs[m]
                    if m >= NAT:
                        sp.wait_ge(job_pe, row_jobs[m - NAT] + 1)
                    for src, p0, k in rows_of(jobs[n][1], jobs[n][2]):
                        sp.dma_start(nat[p0:p0 + k, m % NAT, :], src).then_inc(nat_in[m % NAT], 16)

                def load_mod(m):
                    k = kinds[m]
                    if m >= 2:
                        sp.wait_ge(job_pe, kind_last_job[kinds[m - 2]] + 1)
                    sp.dma_start(wm[:, m % 2, :, :], ins["wmod"].rearrange("(k p) n -> p k n", p=P)[
                        :, :, WMOD_AT[k] * D:(WMOD_AT[k] + 1) * D]).then_inc(wm_in[m % 2], 16)

                for m in range(4):
                    load_rows(m)
                load_mod(0)
                load_mod(1)
                sp.dma_start(w2b[:, :].rearrange("p (t n) -> p t n", t=DC),
                             ins["w2"].rearrange("(t p) n -> p t n", p=P)).then_inc(w2_in, 16)
                for m in range(4, 16):
                    load_rows(m)
                for m in range(2, 6):
                    load_mod(m)
                for m in range(16, len(row_jobs)):
                    load_rows(m)

            @block.tensor
            def _(pe):
                pe.wait_ge(const_in, 16 * 5)
                arrivals = [0] * NAT
                row = 0
                for n, (kind, name, j) in enumerate(jobs):
                    if n >= BANKS:
                        pe.wait_ge(job_act, n - BANKS + 1)
                        pe.wait_ge(job_dve, n - BANKS + 1)
                    if kind == "rows":
                        slot = row % NAT
                        arrivals[slot] += 16 * len(rows_of(name, j))
                        pe.wait_ge(nat_in[slot], arrivals[slot])
                        for c in range(DC):
                            last = pe.transpose(ps[:, n % BANKS, c * P:(c + 1) * P],
                                                nat[:, slot, c * P:(c + 1) * P], ident[:, :])
                        row += 1
                    elif kind == "w2":
                        if j == 0:
                            pe.wait_ge(w2_in, 16)
                        for t in range(DC):
                            last = pe.transpose(ps[:, n % BANKS, t * P:(t + 1) * P],
                                                w2b[:, t * HID + j * P:t * HID + (j + 1) * P], ident[:, :])
                    elif kind == "had":
                        if j == 0:
                            pe.wait_ge(fly, 8)
                        last = pe.matmul(ps[:, n % BANKS, :], had[:, :], w2a[:, j, :], start=True, stop=True)
                    else:
                        m = kinds.index(name)
                        pe.wait_ge(wm_in[m % 2], 16 * (m // 2 + 1))
                        if kind == "mod":
                            pe.wait_ge(silu_done, 1)
                            for c in range(DC):
                                for k in range(DC):
                                    last = pe.matmul(ps[:, n % BANKS, B * c:B * c + B],
                                                     wm[:, m % 2, k, c * P:(c + 1) * P], sc[:, k, :],
                                                     start=(k == 0), stop=(k == DC - 1))
                        else:
                            pe.wait_ge(scb_done, B * DC)
                            for k in range(DC):
                                last = pe.matmul(ps[:, n % BANKS, :], scb[:, j, k, :], wm[:, m % 2, k, :],
                                                 start=(k == 0), stop=(k == DC - 1))
                    last.then_inc(job_pe, 1)

            @block.scalar
            def _(act):
                act.wait_ge(const_in, 16 * 5)
                act.activation(sc[:, :, :], ct[:, :, :], ACT.Silu).then_inc(silu_done, 1)
                for n, (kind, name, j) in enumerate(jobs):
                    act.wait_ge(job_pe, n + 1)
                    ob_free(act, n)
                    src = bank(n, kind)
                    if kind == "rows":
                        op = act.activation(target(n)[HI], src, ACT.Copy)
                    elif kind == "had":
                        op = act.activation(target(n)[HI], src, ACT.Copy, scale=HID ** -0.5)
                    elif kind == "w2":
                        if j % 2:
                            act.wait_ge(job_act, n)
                        op = (act.activation(mark[:, 0:1], ident[:, 0:1], ACT.Copy) if j % 2
                              else act.activation(w2a[:, j, :], src, ACT.Copy))
                    elif kind == "mod":
                        op = act.activation(shift[:, name, :], src[:, 0:DC * B], ACT.Copy)
                    else:
                        if name != GA or j:
                            act.wait_ge(job_dve, n)
                        op = act.activation(graw[:, :], src, ACT.Copy)
                    op.then_inc(job_act, 1)

            @block.vector
            def _(dve):
                links = [0]

                def link(op):
                    links[0] += 1
                    op.then_inc(chain, 1)
                    dve.wait_ge(chain, links[0])

                link(dve.memset(zero[:, :], 0.0))
                dve.wait_ge(silu_done, 1)
                for b in range(B):
                    for k in range(DC):
                        dve.tensor_scalar(scb[:, b, k, :], zero[:, :], sc[:, k, b:b + 1], None,
                                          ALU.add).then_inc(scb_done, 1)

                def butterfly(m):
                    stage, minus = m // 2, m % 2
                    h = 1 << stage
                    src, dst = (w2a[:, :, :].rearrange("p c n -> p (c n)"), w2b[:, :])
                    if stage % 2:
                        src, dst = dst, src
                    src = src.rearrange("p (n t w) -> p t n w", t=2, w=h * D)
                    dst = dst.rearrange("p (n t w) -> p t n w", t=2, w=h * D)
                    if m:
                        dve.wait_ge(fly, m)
                    dve.tensor_tensor(dst[:, minus], src[:, 0], src[:, 1],
                                      ALU.subtract if minus else ALU.add).then_inc(fly, 1)

                flies = 0
                for n, (kind, name, j) in enumerate(jobs):
                    dve.wait_ge(job_pe, n + 1)
                    src = bank(n, kind)
                    if kind in ("rows", "had"):
                        ob_free(dve, n)
                        dve.wait_ge(job_act, n + 1)
                        hi, lo = target(n)
                    if kind == "rows":
                        dve.tensor_tensor(lo, src, hi, ALU.subtract).then_inc(job_dve, 1)
                    elif kind == "had":
                        dve.scalar_tensor_tensor(out=lo, in0=src, scalar=HID ** -0.5, in1=hi, op0=ALU.mult,
                                                 op1=ALU.subtract).then_inc(job_dve, 1)
                    elif kind == "w2":
                        if j % 2 == 0:
                            dve.wait_ge(job_dve, n)
                        (dve.tensor_copy(w2a[:, j, :], src) if j % 2
                         else dve.memset(mark[:, 1:2], 0.0)).then_inc(job_dve, 1)
                    elif kind == "mod":
                        dve.wait_ge(job_act, n + 1)
                        dve.tensor_scalar(scale1[:, name, :], src[:, 0:DC * B], 1.0, None,
                                          ALU.add).then_inc(job_dve, 1)
                    else:
                        dve.wait_ge(job_act, n + 1)
                        link(dve.tensor_scalar(gtmp[:, 0, :], graw[:, :], 0.0, 2.0, ALU.is_ge, ALU.mult))
                        link(dve.scalar_tensor_tensor(out=gtmp[:, 1, :], in0=gtmp[:, 0, :], scalar=-1.0,
                                                      in1=graw[:, :], op0=ALU.add, op1=ALU.mult))
                        link(dve.tensor_scalar(gtmp[:, 1, :], gtmp[:, 1, :], 0.25, None, ALU.max))
                        out = gains[:, 0, j, :] if name == GA else keep["gain_out"][:, j, :]
                        op = dve.scalar_tensor_tensor(out=out, in0=gtmp[:, 0, :], scalar=-1.0, in1=gtmp[:, 1, :],
                                                      op0=ALU.add, op1=ALU.mult)
                        if name == GA:
                            link(op)
                            op = dve.tensor_tensor(gains[:, 1, j, :], out, bpb[:, :], ALU.mult)
                        op.then_inc(job_dve, 1)
                    if n == last_w2t:
                        dve.wait_ge(job_act, n + 1)
                        dve.wait_ge(job_dve, n + 1)
                    if n >= first_w1 and (n - first_w1) % 4 == 3 and flies < 8:
                        butterfly(flies)
                        flies += 1
                while flies < 8:
                    butterfly(flies)
                    flies += 1

            @block.gpsimd
            def _(pool):
                for m, n in enumerate(store_jobs):
                    kind, name, j = jobs[n]
                    pool.wait_ge(job_act, n + 1)
                    pool.wait_ge(job_dve, n + 1)
                    pool.dma_start(scratch["w2" if kind == "had" else name][j],
                                   raw(ob[:, m % OB, :, :])).then_inc(ob_out[m % OB], 16)
                for i in range(OB):
                    pool.wait_ge(ob_out[i], 16 * len(range(i, len(store_jobs), OB)))


LINKS = 4


def norm_stats(dve, chain, rooted, t, x, st, mv, dev, rstd, nmr):
    base = LINKS * t
    for k in range(TK):
        last = dve.bn_stats(st[:, k, :], x[:, k, :])
    last.then_inc(chain, 1)
    dve.wait_ge(chain, base + 1)
    dve.memset(dev, 0.0)
    for k in range(TK):
        last = dve.bn_aggr(mv[:, k, :], st[:, k, :])
    last.then_inc(chain, 1)
    dve.wait_ge(chain, base + 2)
    dve.tensor_scalar(dev, mv[:, :, 1], EPS, None, ALU.add).then_inc(chain, 1)
    dve.wait_ge(rooted, t + 1)
    dve.reciprocal(rstd, dev).then_inc(chain, 1)
    dve.wait_ge(chain, base + 4)
    return dve.scalar_tensor_tensor(out=nmr, in0=mv[:, :, 0], scalar=-1.0, in1=rstd, op0=ALU.mult, op1=ALU.mult)


def project_qkv(nc, ins, keep, scratch):
    ident, wqk, wv, shift, scale1 = (keep[k] for k in ("ident", "wqk", "wv", "shift", "scale1"))
    NQK = 8
    NJ = NQK + TK
    MID = 5
    BANKS = 4
    OB = 4
    with ExitStack() as ctx:
        def sb(name, shape, dt=F32):
            return ctx.enter_context(nc.sbuf_tensor(name, shape, dt))

        def sem(name):
            return ctx.enter_context(nc.semaphore(name))

        xin = sb("xin", [P, 2, TK, D])
        xn = sb("xn", [P, 2, TK, D])
        ht = sb("ht", [P, 2, 2, DC, TOK], F32R)
        full = sb("full", [P, DC, TOK])
        st = sb("st", [P, TK, 6])
        mv = sb("mv", [P, TK, 2])
        dev = sb("dev", [P, TK])
        mark = sb("mark2", [P, 1])
        rstd = sb("rstd", [P, 2, TK])
        nmr = sb("nmr", [P, 2, TK])
        ob = sb("obq", [P, OB, 2, TOK], F32R)
        vst = sb("vst", [P, 2, NH, TK, HD])
        ps = ctx.enter_context(nc.psum_tensor("ps_qkv", [P, BANKS, TOK], F32))
        pt = ctx.enter_context(nc.psum_tensor("ps_ht", [P, DC, TOK], F32))

        x_in = [sem(f"a_x_in{i}") for i in range(2)]
        chain = sem("a_chain")
        rooted = sem("a_rooted")
        stats = sem("a_stats")
        normed = sem("a_normed")
        turned = sem("a_turned")
        h_hi = sem("a_h_hi")
        h_full = sem("a_h_full")
        h_lo = sem("a_h_lo")
        mm = sem("a_mm")
        out_hi = sem("a_out_hi")
        out_lo = sem("a_out_lo")
        ob_out = [sem(f"a_ob_out{i}") for i in range(OB)]
        v_out = [sem(f"a_v_out{i}") for i in range(2)]


        with nc.Block() as block:

            @block.sync
            def _(sp):
                def load(s, b, fresh=False):
                    if not fresh:
                        sp.wait_ge(normed, TK * (2 * s + b - 1))
                    sp.dma_start(xin[:, b, :, :], ins["x"][b].rearrange("(t k p) d -> t p k d", k=TK, p=P)[
                        bass.ds(s, 1)].rearrange("o p k d -> (o p) k d")).then_inc(x_in[b], 16)

                def store(s, b):
                    for j in range(NQK):
                        sp.wait_ge(out_lo, NJ * (2 * s + b) + j + 1)
                        dst = scratch["q" if j < 4 else "k"]
                        r0 = b * NH * HD + (j % 4) * P
                        sp.dma_start(dst[:, r0:r0 + P, bass.ds(s * TOK, TOK)].rearrange("l r n -> r l n"),
                                     raw(ob[:, j % OB, :, :])).then_inc(ob_out[j % OB], 16)
                    sp.wait_ge(out_hi, NJ * (2 * s + b + 1))
                    sp.dma_start(scratch["v"][b * NH:(b + 1) * NH, :, bass.ds(s * TK * HD, TK * HD)].rearrange(
                        "g p n -> p g n"), vst[:, b, :, :, :].rearrange("p h k d -> p h (k d)")).then_inc(v_out[b], 16)

                load(0, 0, True)
                load(0, 1, True)
                with sp.Fori(0, ST - 1) as s:
                    load(s + 1, 0)
                    store(s, 0)
                    load(s + 1, 1)
                    store(s, 1)
                store(ST - 1, 0)
                store(ST - 1, 1)
                for i in range(OB):
                    sp.wait_ge(ob_out[i], 16 * 2 * TILES)
                for b in range(2):
                    sp.wait_ge(v_out[b], 16 * ST)

            @block.tensor
            def _(pe):
                def turn(s, b, fresh=False):
                    t = 2 * s + b
                    pe.wait_ge(normed, TK * (t + 1))
                    if not fresh:
                        pe.wait_ge(h_hi, DC * t)
                        pe.wait_ge(h_full, DC * t)
                    for c in range(DC):
                        for k in range(TK):
                            last = pe.transpose(pt[:, c, k * P:(k + 1) * P], xn[:, b, k, c * P:(c + 1) * P],
                                                ident[:, :])
                        last.then_inc(turned, 1)

                def results(s, b, j, fresh=False):
                    n = NJ * (2 * s + b) + j
                    if j == 0:
                        pe.wait_ge(h_hi, DC * (2 * s + b + 1))
                        pe.wait_ge(h_lo, DC * (2 * s + b + 1))
                    if not (fresh and j < BANKS):
                        pe.wait_ge(out_hi, n - BANKS + 1)
                        pe.wait_ge(out_lo, n - BANKS + 1)
                    if j < NQK:
                        last = split_product(pe, ps[:, j % BANKS, :], lambda a, c: wqk[:, j, a, c, :],
                                             lambda a, c: ht[:, b, a, c, :], range(DC))
                    else:
                        k = j - NQK
                        last = split_product(pe, ps[:, j % BANKS, :],
                                             lambda a, c: ht[:, b, a, c, k * P:(k + 1) * P],
                                             lambda a, c: wv[:, a, c, :], range(DC))
                    last.then_inc(mm, 1)

                def tile(s, b, nxt, fresh=False):
                    for j in range(NJ):
                        results(s, b, j, fresh)
                        if j == MID and nxt:
                            turn(*nxt)

                turn(0, 0, True)
                tile(0, 0, (0, 1), True)
                tile(0, 1, (1, 0))
                with pe.Fori(1, ST - 1) as s:
                    tile(s, 0, (s, 1))
                    tile(s, 1, (s + 1, 0))
                tile(ST - 1, 0, (ST - 1, 1))
                tile(ST - 1, 1, None)

            @block.scalar
            def _(act):
                def normalise(s, b, fresh=False):
                    t = 2 * s + b
                    act.wait_ge(chain, LINKS * t + 3)
                    act.activation(dev[:, :], dev[:, :], ACT.Sqrt).then_inc(rooted, 1)
                    act.wait_ge(stats, t + 1)
                    act.wait_ge(x_in[b], 16 * (s + 1))
                    if not fresh:
                        act.wait_ge(turned, DC * (t - 1))
                    for k in range(TK):
                        act.activation(xn[:, b, k, :], xin[:, b, k, :], ACT.Identity, bias=nmr[:, b, k:k + 1],
                                       scale=rstd[:, b, k:k + 1]).then_inc(normed, 1)

                def high_parts(s, b, fresh=False):
                    t = 2 * s + b
                    if not fresh:
                        act.wait_ge(mm, NJ * (t - 1))
                    for c in range(DC):
                        act.wait_ge(turned, DC * t + c + 1)
                        act.activation(ht[:, b, HI, c, :], pt[:, c, :], ACT.Identity,
                                       bias=shift[:, SA, B * c + b:B * c + b + 1],
                                       scale=scale1[:, CA, B * c + b:B * c + b + 1]).then_inc(h_hi, 1)

                def tile(s, b, nxt, fresh=False):
                    if nxt:
                        normalise(*nxt, fresh and b == 0)
                    for j in range(NJ):
                        n = NJ * (2 * s + b) + j
                        act.wait_ge(mm, n + 1)
                        if j < NQK:
                            if not (fresh and b == 0 and j < OB):
                                act.wait_ge(ob_out[j % OB], 16 * (2 * (2 * s + b) + j // OB))
                            act.activation(ob[:, j % OB, HI, :], ps[:, j % BANKS, :], ACT.Copy).then_inc(out_hi, 1)
                        else:
                            if j == NQK and not fresh:
                                act.wait_ge(v_out[b], 16 * s)
                            act.activation(vst[:, b, :, j - NQK, :],
                                           ps[:, j % BANKS, :].rearrange("p (h d) -> p h d", h=NH),
                                           ACT.Copy).then_inc(out_hi, 1)
                        if j == MID + 1 and nxt:
                            high_parts(*nxt, fresh and b == 0)

                normalise(0, 0, True)
                high_parts(0, 0, True)
                tile(0, 0, (0, 1), True)
                tile(0, 1, (1, 0), True)
                with act.Fori(1, ST - 1) as s:
                    tile(s, 0, (s, 1))
                    tile(s, 1, (s + 1, 0))
                tile(ST - 1, 0, (ST - 1, 1))
                tile(ST - 1, 1, None)

            @block.vector
            def _(dve):
                def measure(s, b, fresh=False):
                    t = 2 * s + b
                    dve.wait_ge(x_in[b], 16 * (s + 1))
                    if not fresh:
                        dve.wait_ge(normed, TK * (t - 1))
                    norm_stats(dve, chain, rooted, t, xin[:, b, :, :], st, mv, dev[:, :], rstd[:, b, :],
                               nmr[:, b, :]).then_inc(stats, 1)

                def low_parts(s, b, fresh=False):
                    t = 2 * s + b
                    for c in range(DC):
                        dve.wait_ge(h_hi, DC * t + c + 1)
                        dve.tensor_scalar(full[:, c, :], pt[:, c, :], scale1[:, CA, B * c + b:B * c + b + 1],
                                          shift[:, SA, B * c + b:B * c + b + 1], ALU.mult,
                                          ALU.add).then_inc(h_full, 1)
                    for c in range(DC):
                        dve.wait_ge(h_full, DC * t + c + 1)
                        dve.tensor_tensor(ht[:, b, LO, c, :], full[:, c, :], ht[:, b, HI, c, :],
                                          ALU.subtract).then_inc(h_lo, 1)

                def tile(s, b, nxt, fresh=False):
                    if nxt:
                        measure(*nxt, fresh and b == 0)
                    for j in range(NJ):
                        n = NJ * (2 * s + b) + j
                        dve.wait_ge(out_hi, n + 1)
                        if j < NQK:
                            dve.tensor_tensor(ob[:, j % OB, LO, :], ps[:, j % BANKS, :], ob[:, j % OB, HI, :],
                                              ALU.subtract).then_inc(out_lo, 1)
                        else:
                            dve.wait_ge(out_lo, n)
                            dve.memset(mark[:, :], 0.0).then_inc(out_lo, 1)
                        if j == MID + 1 and nxt:
                            low_parts(*nxt)

                measure(0, 0, True)
                low_parts(0, 0)
                tile(0, 0, (0, 1), True)
                tile(0, 1, (1, 0), True)
                with dve.Fori(1, ST - 1) as s:
                    tile(s, 0, (s, 1))
                    tile(s, 1, (s + 1, 0))
                tile(ST - 1, 0, (ST - 1, 1))
                tile(ST - 1, 1, None)


DIRECT = (13, 14, 15)
GROUPS = ((0, 1, 2), (3, 4, 5), (6, 7, 8), (9, 10, 11, 12))
ADDS = sum(len(g) - 1 for g in GROUPS)
UNITS = len(GROUPS) + len(DIRECT)


def adds_until(kt):
    n = 0
    for g in GROUPS:
        for i, k in enumerate(g):
            n += i > 0
            if k == kt:
                return n + (i == 0)
    raise ValueError(kt)


def attend(nc, keep, scratch):
    ident = keep["ident"]
    SLOTS, RING, KR = 4, 8, 3 * HD
    NM = KT * QJ
    PER = [5] * 8 + [4] * 6 + [0, 0]
    assert sum(PER) == NM
    SCALE = HD ** -0.5
    HALF = S // 2
    LOADS = 16 * 7
    with ExitStack() as ctx:
        def sb(name, shape, dt=F32):
            return ctx.enter_context(nc.sbuf_tensor(name, shape, dt))

        def sem(name):
            return ctx.enter_context(nc.semaphore(name))

        qst = sb("qst", [KR + 2, SLOTS, S], F32R)
        kst = sb("kst", [KR + 2, SLOTS, S], F32R)
        v = sb("v", [P, SLOTS, KT, HD])
        prob = sb("prob", [P, RING, S])
        gsum = sb("gsum", [P, 2, S])
        ctxo = sb("ctxo", [P, 2, TOK])
        sumo = sb("sumo", [P, 2, TOK])
        mxp = sb("mxp", [P, KT, QJ])
        mx = sb("mx", [P, KT])
        mrow = sb("mrow", [KT, 2, P], F32R)
        ones = sb("ones", [P, HD])
        mark = sb("mark3", [P, 8])
        pexp = ctx.enter_context(nc.psum_tensor("pexp", [P, 2, HALF], F32))
        pmax = ctx.enter_context(nc.psum_tensor("pmax", [P, 2, TOK], F32))
        pctx = ctx.enter_context(nc.psum_tensor("pctx", [P, TOK], F32))
        psum = ctx.enter_context(nc.psum_tensor("psums", [P, TOK], F32))

        const = sem("b_const")
        loaded = [sem(f"b_loaded{i}") for i in range(SLOTS)]
        scores = sem("b_scores")
        exp_done = sem("b_exp_done")
        mm_max = sem("b_mm_max")
        mx_done = sem("b_mx_done")
        mx_all = sem("b_mx_all")
        mx_turned = sem("b_mx_turned")
        m_split = sem("b_m_split")
        m_row = sem("b_m_row")
        pv_done = sem("b_pv_done")
        unit_done = sem("b_unit_done")
        add_done = sem("b_add_done")
        ctx_read = sem("b_ctx_read")
        sum_read = sem("b_sum_read")
        out_done = [sem(f"b_out_done{i}") for i in range(2)]
        OUTS = 16 * 5

        def heads(eng, step):
            with eng.Fori(0, HEADS // SLOTS - 1) as i:
                for r in range(SLOTS):
                    step(i * SLOTS + r, i, r, False)
            i = HEADS // SLOTS - 1
            for r in range(SLOTS):
                step(i * SLOTS + r, i, r, r == SLOTS - 1)

        with nc.Block() as block:

            @block.sync
            def _(sp):
                def load(g, slot):
                    rows = bass.ds(g * HD, HD)
                    q, k = scratch["q"], scratch["k"]
                    for r, part in enumerate((HI, LO, HI)):
                        sp.dma_start(raw(qst[r * HD:(r + 1) * HD, slot, :]), q[part, rows, :]).then_inc(loaded[slot], 16)
                    for r, part in enumerate((HI, HI, LO)):
                        sp.dma_start(raw(kst[r * HD:(r + 1) * HD, slot, :]), k[part, rows, :]).then_inc(loaded[slot], 16)
                    sp.dma_start(v[:, slot, :, :].rearrange("p k d -> p (k d)"),
                                 scratch["v"][bass.ds(g, 1)].rearrange("o p n -> (o p) n")).then_inc(loaded[slot], 16)

                def max_row(g, slot):
                    sp.wait_ge(m_split, 2 * (g + 1))
                    for part in (HI, LO):
                        r = KR + part
                        sp.dma_start(raw(qst[r:r + 1, slot, :]).rearrange("o (t n) -> o t n", t=KT),
                                     raw(mrow[:, part, :])).then_inc(m_row, 16)

                def step(g, i, r, last):
                    if not isinstance(g, int) or g + 3 < HEADS:
                        sp.wait_ge(pv_done, RING + KT * g)
                        load(g + 3, (r + 3) % SLOTS)
                    if not last:
                        max_row(g + 1, (r + 1) % SLOTS)
                    par = r % 2
                    pair = i * 2 + r // 2
                    sp.wait_ge(ctx_read, g + 2)
                    for j in range(QJ):
                        sp.dma_start(scratch["ctx"][par, bass.ds(pair * HD, HD), j * TOK:(j + 1) * TOK],
                                     ctxo[j * HD:(j + 1) * HD, par, :]).then_inc(out_done[par], 16)
                    sp.wait_ge(sum_read, g + 2)
                    sp.dma_start(scratch["sum"][par, bass.ds(pair, 1), :].rearrange("o (j n) -> (o j) n", j=QJ),
                                 sumo[0:P:HD, par, :]).then_inc(out_done[par], 16)

                for g in range(3):
                    load(g, g)
                max_row(0, 0)
                heads(sp, step)
                for par in range(2):
                    sp.wait_ge(out_done[par], 16 + OUTS * HEADS // 2)

            @block.tensor
            def _(pe):
                def maximum(g, slot, u, fresh=False):
                    qt, kc = u // QJ, u % QJ
                    if not (fresh and u < 2):
                        pe.wait_ge(mx_done, g * NM + u - 1)
                    if u == 0 and not fresh:
                        pe.wait_ge(m_split, 2 * g)
                    pe.matmul(pmax[:, u % 2, :], qst[0:KR, slot, qt * P:(qt + 1) * P],
                              kst[0:KR, slot, kc * TOK:(kc + 1) * TOK], start=True, stop=True).then_inc(mm_max, 1)

                def turn_max(g):
                    pe.wait_ge(mx_all, g + 1)
                    pe.transpose(pmax[0:KT, 0, 0:P], mx[:, :], ident[:, :]).then_inc(mx_turned, 1)

                def score(g, slot, kt, half):
                    if kt == 0 and half == 0:
                        pe.wait_ge(m_row, 32 * (g + 1))
                    pe.wait_ge(exp_done, 2 * KT * g + 2 * kt + half + 1)
                    for j in range(2):
                        q0 = half * HALF + j * TOK
                        last = pe.matmul(pexp[:, half, j * TOK:(j + 1) * TOK], kst[:, slot, kt * P:(kt + 1) * P],
                                         qst[:, slot, q0:q0 + TOK], start=True, stop=True)
                    last.then_inc(scores, 1)

                def weigh(g, slot, kt):
                    pe.wait_ge(exp_done, 2 * KT * g + 2 * kt + 4)
                    if kt == 0:
                        pe.wait_ge(ctx_read, g + 1)
                    for j in range(QJ):
                        last = pe.matmul(pctx[j * HD:(j + 1) * HD, :], v[:, slot, kt, :],
                                         prob[:, kt % RING, j * TOK:(j + 1) * TOK], start=(kt == 0), stop=(kt == KT - 1))
                    last.then_inc(pv_done, 1)

                def unit(g, n, src):
                    if n == 0:
                        pe.wait_ge(sum_read, g + 1)
                    for j in range(QJ):
                        last = pe.matmul(psum[j * HD:(j + 1) * HD, :], ones[:, :], src[:, j * TOK:(j + 1) * TOK],
                                         start=(n == 0), stop=(n == UNITS - 1))
                    last.then_inc(unit_done, 1)

                def group(g, n, k):
                    pe.wait_ge(add_done, ADDS + ADDS * g + adds_until(GROUPS[k][-1]))
                    unit(g, n, gsum[:, k % 2, :])

                def step(g, i, r, last):
                    u = 0

                    def some(n):
                        nonlocal u
                        for _ in range(n):
                            maximum(g + 1, (r + 1) % SLOTS, u)
                            u += 1

                    if not last:
                        nxt = (r + 1) % SLOTS
                        pe.wait_ge(loaded[nxt], LOADS * (i + 1 + (r + 1) // SLOTS))
                    for kt in range(KT):
                        n = 0 if last else PER[kt]
                        score(g, r, kt, 0)
                        some(n // 4 + (n == 5))
                        if kt:
                            weigh(g, r, kt - 1)
                        some((n >= 4))
                        score(g, r, kt, 1)
                        some(n and n - 1 - (n // 4 + (n == 5)))
                        if kt == KT - 2 and not last:
                            turn_max(g + 1)
                        if kt in (6, 9, 12):
                            group(g, (kt - 6) // 3, (kt - 6) // 3)
                        if kt == KT - 1:
                            unit(g, 3, prob[:, 13 % RING, :])
                            unit(g, 4, prob[:, 14 % RING, :])
                    group(g, 5, 3)
                    weigh(g, r, KT - 1)
                    unit(g, 6, prob[:, 15 % RING, :])

                pe.wait_ge(const, 2)
                pe.wait_ge(loaded[0], LOADS)
                for u in range(NM):
                    maximum(0, 0, u, True)
                turn_max(0)
                heads(pe, step)

            @block.scalar
            def _(act):
                def step(g, i, r, last):
                    par = r % 2
                    for kt in range(KT):
                        act.wait_ge(pv_done, KT * g + kt + 1)
                        old = (kt - RING) % KT
                        back = 0 if kt >= RING else 1
                        if old in DIRECT:
                            done = {13: 4, 14: 5, 15: 7}[old]
                            act.wait_ge(unit_done, UNITS + UNITS * g - UNITS * back + done)
                        else:
                            act.wait_ge(add_done, ADDS + ADDS * g - ADDS * back + adds_until(old))
                        for half in range(2):
                            act.wait_ge(scores, 2 * KT * g + 2 * kt + half + 1)
                            act.activation(prob[:, kt % RING, half * HALF:(half + 1) * HALF], pexp[:, half, :],
                                           ACT.Exp, scale=SCALE).then_inc(exp_done, 1)
                    act.wait_ge(out_done[par], 16 + OUTS * (2 * i + r // 2))
                    act.wait_ge(pv_done, RING + KT * (g + 1))
                    act.activation(ctxo[:, par, :], pctx[:, :], ACT.Copy).then_inc(ctx_read, 1)
                    act.wait_ge(unit_done, UNITS + UNITS * (g + 1))
                    act.activation(sumo[:, par, :], psum[:, :], ACT.Copy).then_inc(sum_read, 1)

                heads(act, step)

            @block.vector
            def _(dve):
                dve.memset(ones[:, :], 1.0).then_inc(const, 1)
                dve.memset(kst[KR:KR + 2, :, :].bitcast(F32), 1.0).then_inc(const, 1)
                credits = ((exp_done, 2), (pv_done, RING), (unit_done, UNITS), (add_done, ADDS), (ctx_read, 1),
                           (sum_read, 1), (out_done[0], 16), (out_done[1], 16))
                for i, (free, n) in enumerate(credits):
                    dve.memset(mark[:, i:i + 1], 0.0).then_inc(free, n)

                def maxima(g):
                    for u in range(NM):
                        dve.wait_ge(mm_max, g * NM + u + 1)
                        dve.tensor_reduce(mxp[:, u // QJ, u % QJ:u % QJ + 1], pmax[:, u % 2, :], X,
                                          ALU.max).then_inc(mx_done, 1)
                    dve.wait_ge(mx_done, (g + 1) * NM)
                    dve.tensor_reduce(mx[:, :], mxp[:, :, :], X, ALU.max).then_inc(mx_all, 1)
                    dve.wait_ge(mx_turned, g + 1)
                    dve.wait_ge(m_row, 32 * g)
                    dve.tensor_scalar(mrow[:, HI, :], pmax[0:KT, 0, 0:P], -1.0, None, ALU.mult).then_inc(m_split, 1)
                    dve.wait_ge(m_split, 2 * g + 1)
                    dve.scalar_tensor_tensor(out=mrow[:, LO, :], in0=pmax[0:KT, 0, 0:P], scalar=-1.0,
                                             in1=mrow[:, HI, :], op0=ALU.mult, op1=ALU.subtract).then_inc(m_split, 1)

                maxima(0)
                with dve.Fori(1, HEADS) as g:
                    maxima(g)

            @block.gpsimd
            def _(pool):
                def head(g):
                    n = 0
                    before = (3, 6, 1, 2)
                    for k, grp in enumerate(GROUPS):
                        dst = gsum[:, k % 2, :]
                        pool.wait_ge(unit_done, UNITS * g + before[k] + (UNITS if k >= 2 else 0))
                        for m, kt in enumerate(grp[1:]):
                            pool.wait_ge(exp_done, 2 * KT * g + 2 * kt + 4)
                            a = prob[:, grp[0] % RING, :] if m == 0 else dst
                            if m:
                                pool.wait_ge(add_done, ADDS + ADDS * g + n)
                            pool.tensor_tensor(dst, a, prob[:, kt % RING, :], ALU.add).then_inc(add_done, 1)
                            n += 1

                with pool.Fori(0, HEADS) as g:
                    head(g)


def project_out(nc, ins, keep, scratch):
    ident, wp, shift, scale1, gains = (keep[k] for k in ("ident", "wp", "shift", "scale1", "gains"))
    with ExitStack() as ctx:
        def sb(name, shape, dt=F32):
            return ctx.enter_context(nc.sbuf_tensor(name, shape, dt))

        def sem(name):
            return ctx.enter_context(nc.semaphore(name))

        sums = sb("sums", [P, HEADS * S // P])
        rec = sb("rec", [P, HEADS * S // P])
        cin = sb("cin", [P, 2, DC, TOK])
        rin = sb("rin", [P, 2, DC, TOK])
        cn = sb("cn", [P, DC, TOK])
        cs = sb("cs", [P, 2, 2, DC, TOK], F32R)
        xin = sb("xin2", [P, 2, TK, D])
        x2 = sb("x2", [P, 2, TK, D])
        xn = sb("xn2", [P, TK, D])
        h2 = sb("h2", [P, 2, 2, DC, TOK], F32R)
        full = sb("full2", [P, DC, TOK])
        st = sb("st2", [P, TK, 6])
        mv = sb("mv2", [P, TK, 2])
        dev = sb("dev2", [P, TK])
        rstd = sb("rstd2", [P, TK])
        nmr = sb("nmr2", [P, TK])
        po = ctx.enter_context(nc.psum_tensor("po", [P, TK, D], F32))
        pt = ctx.enter_context(nc.psum_tensor("pt2", [P, DC, TOK], F32))

        s_in = sem("c_sums_in")
        s_rec = sem("c_rec")
        s_out = sem("c_rec_out")
        tile_in = [sem(f"c_tile_in{i}") for i in range(2)]
        c_norm = sem("c_ctx_normed")
        c_hi = sem("c_ctx_hi")
        c_lo = sem("c_ctx_lo")
        x_bias = sem("c_x_bias")
        mm = sem("c_mm")
        scaled = sem("c_scaled")
        resid = sem("c_resid")
        chain = sem("c_chain")
        rooted = sem("c_rooted")
        stats = sem("c_stats")
        normed = sem("c_normed")
        turned = sem("c_turned")
        h_hi = sem("c_h_hi")
        h_full = sem("c_h_full")
        h_lo = sem("c_h_lo")
        tile_out = [sem(f"c_tile_out{i}") for i in range(2)]


        with nc.Block() as block:

            @block.sync
            def _(sp):
                sp.dma_start(sums[:, :], scratch["sum"].rearrange("b h s -> (b h s)").rearrange(
                    "(p n) -> p n", p=P)).then_inc(s_in, 16)
                sp.wait_ge(s_rec, 1)
                sp.dma_start(scratch["rec"].rearrange("b h s -> (b h s)").rearrange("(p n) -> p n", p=P),
                             rec[:, :]).then_inc(s_out, 16)
                sp.wait_ge(s_out, 16)

                def load(s, b, fresh=False):
                    if not fresh:
                        sp.wait_ge(c_norm, DC * (2 * s + b - 1))
                        sp.wait_ge(resid, TK * (2 * s + b - 1))
                    tok = bass.ds(s * TOK, TOK)
                    sp.dma_start(cin[:, b, :, :], scratch["ctx"][b].rearrange("(c p) n -> p c n", p=P)[
                        :, :, tok]).then_inc(tile_in[b], 16)
                    for h in range(4):
                        src = scratch["rec"][b].rearrange("(c h) n -> h c n", h=4)[h][:, tok]
                        sp.dma_start(rin[h * HD:(h + 1) * HD, b, :, :],
                                     src.partition_broadcast(HD)).then_inc(tile_in[b], 16)
                    sp.dma_start(xin[:, b, :, :], ins["x"][b].rearrange("(t k p) d -> t p k d", k=TK, p=P)[
                        bass.ds(s, 1)].rearrange("o p k d -> (o p) k d")).then_inc(tile_in[b], 16)

                def store(s, b):
                    t = 2 * s + b
                    sp.wait_ge(resid, TK * (t + 1))
                    sp.dma_start(scratch["x2"][bass.ds(t, 1)].rearrange("o p n -> (o p) n"),
                                 x2[:, b, :, :].rearrange("p k d -> p (k d)")).then_inc(tile_out[b], 16)
                    sp.wait_ge(h_lo, DC * (t + 1))
                    sp.dma_start(scratch["h2"][bass.ds(t, 1)].rearrange("o p n -> (o p) n"),
                                 raw(h2[:, b, :, :, :]).rearrange("p l c n -> p (l c n)")).then_inc(tile_out[b], 16)

                load(0, 0, True)
                load(0, 1, True)
                with sp.Fori(0, ST - 1) as s:
                    load(s + 1, 0)
                    store(s, 0)
                    load(s + 1, 1)
                    store(s, 1)
                store(ST - 1, 0)
                store(ST - 1, 1)
                for b in range(2):
                    sp.wait_ge(tile_out[b], 16 + 32 * ST)

            @block.tensor
            def _(pe):
                def project(s, b):
                    t = 2 * s + b
                    pe.wait_ge(c_hi, DC * (t + 1))
                    pe.wait_ge(c_lo, DC * (t + 1))
                    for k in range(TK):
                        pe.wait_ge(scaled, TK * t + k + 1 - TK) if not isinstance(t, int) or t else None
                        split_product(pe, po[:, k, :], lambda a, c: cs[:, b, a, c, k * P:(k + 1) * P],
                                      lambda a, c: wp[:, a, c, :], range(DC)).then_inc(mm, 1)

                def turn(s, b):
                    t = 2 * s + b
                    pe.wait_ge(normed, TK * (t + 1))
                    pe.wait_ge(h_hi, DC * t)
                    pe.wait_ge(h_full, DC * t)
                    for c in range(DC):
                        for k in range(TK):
                            last = pe.transpose(pt[:, c, k * P:(k + 1) * P], xn[:, k, c * P:(c + 1) * P], ident[:, :])
                        last.then_inc(turned, 1)

                project(0, 0)
                project(0, 1)
                turn(0, 0)
                with pe.Fori(1, ST) as s:
                    project(s, 0)
                    turn(s - 1, 1)
                    project(s, 1)
                    turn(s, 0)
                turn(ST - 1, 1)

            @block.gpsimd
            def _(pool):
                def tile(s, b):
                    t = 2 * s + b
                    pool.wait_ge(tile_in[b], 16 * 6 * (s + 1))
                    pool.wait_ge(c_hi, DC * t)
                    pool.wait_ge(c_lo, DC * t)
                    for c in range(DC):
                        pool.tensor_tensor(cn[:, c, :], cin[:, b, c, :], rin[:, b, c, :],
                                           ALU.mult).then_inc(c_norm, 1)
                    for k in range(TK):
                        pool.tensor_tensor(xin[:, b, k, :], xin[:, b, k, :], gains[:, 1, b, :],
                                           ALU.add).then_inc(x_bias, 1)

                tile(0, 0)
                tile(0, 1)
                with pool.Fori(1, ST) as s:
                    tile(s, 0)
                    tile(s, 1)

            @block.scalar
            def _(act):
                def ctx_high(s, b, fresh=False):
                    t = 2 * s + b
                    if not fresh:
                        act.wait_ge(mm, TK * (t - 1))
                    for c in range(DC):
                        act.wait_ge(c_norm, DC * t + c + 1)
                        act.activation(cs[:, b, HI, c, :], cn[:, c, :], ACT.Copy).then_inc(c_hi, 1)

                def normalise(s, b):
                    t = 2 * s + b
                    act.wait_ge(chain, LINKS * t + 3)
                    act.activation(dev[:, :], dev[:, :], ACT.Sqrt).then_inc(rooted, 1)
                    act.wait_ge(stats, t + 1)
                    act.wait_ge(turned, DC * t)
                    for k in range(TK):
                        act.activation(xn[:, k, :], x2[:, b, k, :], ACT.Identity, bias=nmr[:, k:k + 1],
                                       scale=rstd[:, k:k + 1]).then_inc(normed, 1)

                def high_parts(s, b):
                    t = 2 * s + b
                    act.wait_ge(tile_out[b], 16 + 32 * s)
                    for c in range(DC):
                        act.wait_ge(turned, DC * t + c + 1)
                        act.activation(h2[:, b, HI, c, :], pt[:, c, :], ACT.Identity,
                                       bias=shift[:, SB, B * c + b:B * c + b + 1],
                                       scale=scale1[:, CB, B * c + b:B * c + b + 1]).then_inc(h_hi, 1)

                ctx_high(0, 0, True)
                ctx_high(0, 1, True)
                normalise(0, 0)
                high_parts(0, 0)
                with act.Fori(1, ST) as s:
                    ctx_high(s, 0)
                    normalise(s - 1, 1)
                    high_parts(s - 1, 1)
                    ctx_high(s, 1)
                    normalise(s, 0)
                    high_parts(s, 0)
                normalise(ST - 1, 1)
                high_parts(ST - 1, 1)

            @block.vector
            def _(dve):
                for b in range(2):
                    dve.memset(nmr[:, b:b + 1], 0.0).then_inc(tile_out[b], 16)
                dve.wait_ge(s_in, 16)
                dve.reciprocal(rec[:, :], sums[:, :]).then_inc(s_rec, 1)

                def ctx_low(s, b):
                    t = 2 * s + b
                    for c in range(DC):
                        dve.wait_ge(c_hi, DC * t + c + 1)
                        dve.tensor_tensor(cs[:, b, LO, c, :], cn[:, c, :], cs[:, b, HI, c, :],
                                          ALU.subtract).then_inc(c_lo, 1)

                def residual(s, b):
                    t = 2 * s + b
                    dve.wait_ge(tile_out[b], 16 + 32 * s)
                    for k in range(TK):
                        dve.wait_ge(mm, TK * t + k + 1)
                        dve.tensor_tensor(x2[:, b, k, :], po[:, k, :], gains[:, 0, b, :],
                                          ALU.mult).then_inc(scaled, 1)
                    for k in range(TK):
                        dve.wait_ge(scaled, TK * t + k + 1)
                        dve.wait_ge(x_bias, TK * t + k + 1)
                        dve.tensor_tensor(x2[:, b, k, :], x2[:, b, k, :], xin[:, b, k, :],
                                          ALU.add).then_inc(resid, 1)
                    dve.wait_ge(resid, TK * (t + 1))
                    dve.wait_ge(normed, TK * t)
                    norm_stats(dve, chain, rooted, t, x2[:, b, :, :], st, mv, dev[:, :], rstd[:, :], nmr[:, :]).then_inc(stats, 1)

                def low_parts(s, b):
                    t = 2 * s + b
                    for c in range(DC):
                        dve.wait_ge(h_hi, DC * t + c + 1)
                        dve.tensor_scalar(full[:, c, :], pt[:, c, :], scale1[:, CB, B * c + b:B * c + b + 1],
                                          shift[:, SB, B * c + b:B * c + b + 1], ALU.mult,
                                          ALU.add).then_inc(h_full, 1)
                    for c in range(DC):
                        dve.wait_ge(h_full, DC * t + c + 1)
                        dve.tensor_tensor(h2[:, b, LO, c, :], full[:, c, :], h2[:, b, HI, c, :],
                                          ALU.subtract).then_inc(h_lo, 1)

                ctx_low(0, 0)
                ctx_low(0, 1)
                residual(0, 0)
                low_parts(0, 0)
                with dve.Fori(1, ST) as s:
                    ctx_low(s, 0)
                    residual(s - 1, 1)
                    low_parts(s - 1, 1)
                    ctx_low(s, 1)
                    residual(s, 0)
                    low_parts(s, 0)
                residual(ST - 1, 1)
                low_parts(ST - 1, 1)


def feed_forward(nc, keep, scratch, out):
    gain = keep["gain_out"]
    W2R = 4
    with ExitStack() as ctx:
        def sb(name, shape, dt=F32):
            return ctx.enter_context(nc.sbuf_tensor(name, shape, dt))

        def sem(name):
            return ctx.enter_context(nc.semaphore(name))

        w1 = sb("w1", [P, HC, 2, DC, P], F32R)
        w3 = sb("w3", [P, HC, 2, DC, P], F32R)
        w2 = sb("w2", [P, W2R, 2, D], F32R)
        h2 = sb("h2f", [P, 2, 2, DC, TOK], F32R)
        x2 = sb("x2f", [P, TK, D])
        sil = sb("sil", [P, TOK])
        hid = sb("hid", [P, TOK])
        gs = sb("gs", [P, 2, 2, TOK], F32R)
        fin = sb("fin", [P, 2, D])
        pg = ctx.enter_context(nc.psum_tensor("pg", [P, 2, TOK], F32))
        pl = ctx.enter_context(nc.psum_tensor("pl", [P, 2, TOK], F32))
        po = ctx.enter_context(nc.psum_tensor("pof", [P, TK, D], F32))

        w_in = [sem(f"f_w_in{h}") for h in range(HC)]
        w2_in = [sem(f"f_w2_in{i}") for i in range(W2R)]
        h_in = [sem(f"f_h_in{i}") for i in range(2)]
        x_in = sem("f_x_in")
        gate = sem("f_gate")
        lin = sem("f_lin")
        silu = sem("f_silu")
        prod = sem("f_prod")
        g_hi = sem("f_g_hi")
        g_lo = sem("f_g_lo")
        down = sem("f_down")
        scaled = sem("f_scaled")
        summed = sem("f_summed")
        stored = sem("f_stored")

        with nc.Block() as block:

            @block.sync
            def _(sp):
                def load_h(s, b, fresh=False):
                    if not fresh:
                        sp.wait_ge(lin, HC * (2 * s + b - 1))
                    sp.dma_start(raw(h2[:, b, :, :, :]).rearrange("p l c n -> p (l c n)"),
                                 scratch["h2"][bass.ds(2 * s + b, 1)].rearrange("o p n -> (o p) n")
                                 ).then_inc(h_in[b], 16)

                def load_w2(n, h, fresh=False):
                    if not fresh:
                        sp.wait_ge(down, n - W2R + 1)
                    sp.dma_start(raw(w2[:, h % W2R, :, :]), scratch["w2"][h]).then_inc(w2_in[h % W2R], 16)

                load_h(0, 0, True)
                for h in range(HC):
                    sp.dma_start(raw(w1[:, h, :, :, :]).rearrange("p l c n -> p (l c n)"),
                                 scratch["w1"][h].rearrange("p l n -> p (l n)")).then_inc(w_in[h], 16)
                    sp.dma_start(raw(w3[:, h, :, :, :]).rearrange("p l c n -> p (l c n)"),
                                 scratch["w3"][h].rearrange("p l n -> p (l n)")).then_inc(w_in[h], 16)
                    if h < W2R:
                        load_w2(h, h, True)
                load_h(0, 1, True)

                def store(s, b):
                    sp.wait_ge(summed, TK * (2 * s + b + 1))
                    sp.dma_start(out[b].rearrange("(t k p) d -> t p k d", k=TK, p=P)[bass.ds(s, 1)].rearrange(
                        "o p k d -> (o p) k d"), x2[:, :, :]).then_inc(stored, 16)

                def tile(s, b, fresh=False, last=False):
                    t = 2 * s + b
                    for h in range(HC):
                        if not (fresh and h < W2R):
                            load_w2(HC * t + h, h)
                        if h == 2 + W2R and not fresh:
                            store(s - 1 + b, 1 - b)
                        if h == 3 + W2R:
                            if not fresh:
                                sp.wait_ge(stored, 16 * t)
                            sp.dma_start(x2[:, :, :].rearrange("p k d -> p (k d)"),
                                         scratch["x2"][bass.ds(t, 1)].rearrange("o p n -> (o p) n")
                                         ).then_inc(x_in, 16)
                        if h == 3 and not fresh and not last:
                            load_h(s + b, 1 - b)

                tile(0, 0, True)
                tile(0, 1)
                with sp.Fori(1, ST - 1) as s:
                    tile(s, 0)
                    tile(s, 1)
                tile(ST - 1, 0)
                tile(ST - 1, 1, last=True)
                store(ST - 1, 1)
                sp.wait_ge(stored, 16 * TILES)

            @block.tensor
            def _(pe):
                def up(t, s, b, h, fresh=False):
                    n = HC * t + h
                    if h == 0:
                        pe.wait_ge(h_in[b], 16 * (s + 1))
                    if fresh:
                        pe.wait_ge(w_in[h], 32)
                    if not (fresh and h < 2):
                        pe.wait_ge(silu, n - 1)
                        pe.wait_ge(prod, n - 1)
                    split_product(pe, pg[:, h % 2, :], lambda a, c: w1[:, h, a, c, :],
                                  lambda a, c: h2[:, b, a, c, :], range(DC)).then_inc(gate, 1)
                    split_product(pe, pl[:, h % 2, :], lambda a, c: w3[:, h, a, c, :],
                                  lambda a, c: h2[:, b, a, c, :], range(DC)).then_inc(lin, 1)

                def into_out(t, h):
                    n = HC * t + h
                    pe.wait_ge(g_hi, n + 1)
                    pe.wait_ge(g_lo, n + 1)
                    pe.wait_ge(w2_in[h % W2R], 16 * (HC // W2R * t + h // W2R + 1))
                    for k in range(TK):
                        if h == 0:
                            pe.wait_ge(scaled, TK * t - TK + k + 1) if not isinstance(t, int) or t else None
                        last = split_product(pe, po[:, k, :], lambda a, c: gs[:, h % 2, a, k * P:(k + 1) * P],
                                             lambda a, c: w2[:, h % W2R, a, :], range(1),
                                             start=(h == 0), stop=(h == HC - 1))
                    last.then_inc(down, 1)

                def tile(s, b, fresh=False, last=False):
                    t = 2 * s + b
                    for h in range(1, HC):
                        up(t, s, b, h, fresh)
                        into_out(t, h - 1)
                    if not last:
                        up(t + 1, s + b, 1 - b, 0)
                    into_out(t, HC - 1)

                up(0, 0, 0, 0, True)
                tile(0, 0, True)
                tile(0, 1)
                with pe.Fori(1, ST - 1) as s:
                    tile(s, 0)
                    tile(s, 1)
                tile(ST - 1, 0)
                tile(ST - 1, 1, last=True)

            @block.scalar
            def _(act):
                def tile(s, b, fresh=False):
                    t = 2 * s + b
                    for h in range(HC):
                        n = HC * t + h
                        act.wait_ge(gate, n + 1)
                        act.wait_ge(prod, n)
                        act.activation(sil[:, :], pg[:, h % 2, :], ACT.Silu).then_inc(silu, 1)
                        act.wait_ge(prod, n + 1)
                        if not (fresh and h < 2):
                            act.wait_ge(down, n - 1)
                        act.activation(gs[:, h % 2, HI, :], hid[:, :], ACT.Copy).then_inc(g_hi, 1)

                tile(0, 0, True)
                tile(0, 1)
                with act.Fori(1, ST) as s:
                    tile(s, 0)
                    tile(s, 1)

            @block.vector
            def _(dve):
                def finish(s, b):
                    t = 2 * s + b
                    dve.wait_ge(down, HC * (t + 1))
                    dve.wait_ge(x_in, 16 * (t + 1))
                    dve.wait_ge(g_lo, HC * (t + 1))
                    for k in range(TK):
                        dve.tensor_tensor(tmp(k), po[:, k, :], gain[:, b, :], ALU.mult).then_inc(scaled, 1)
                        dve.wait_ge(scaled, TK * t + k + 1)
                        dve.tensor_tensor(x2[:, k, :], tmp(k), x2[:, k, :], ALU.add).then_inc(summed, 1)

                def tmp(k):
                    return fin[:, k % 2, :]

                def tile(s, b, first=False):
                    t = 2 * s + b
                    for h in range(HC):
                        n = HC * t + h
                        dve.wait_ge(lin, n + 1)
                        dve.wait_ge(silu, n + 1)
                        dve.wait_ge(g_hi, n)
                        dve.wait_ge(g_lo, n)
                        dve.tensor_tensor(hid[:, :], sil[:, :], pl[:, h % 2, :], ALU.mult).then_inc(prod, 1)
                        dve.wait_ge(g_hi, n + 1)
                        dve.tensor_tensor(gs[:, h % 2, LO, :], hid[:, :], gs[:, h % 2, HI, :],
                                          ALU.subtract).then_inc(g_lo, 1)
                        if h == 0 and not first:
                            finish(s - 1 + b, 1 - b)

                tile(0, 0, True)
                tile(0, 1)
                with dve.Fori(1, ST) as s:
                    tile(s, 0)
                    tile(s, 1)
                finish(ST - 1, 1)


def program(nc, x, wqkv, wproj, bproj, w1, w2, w3, c, wmod, identity, hadamard, out):
    ins = dict(x=x, wqkv=wqkv, wproj=wproj, bproj=bproj, w1=w1, w2=w2, w3=w3, c=c, wmod=wmod,
               identity=identity, hadamard=hadamard)

    def dram(name, shape, dt=F32):
        return nc.dram_tensor(name, shape, dt, kind="Internal").ap()

    scratch = {
        "q": dram("q_scratch", [2, HEADS * HD, S]),
        "k": dram("k_scratch", [2, HEADS * HD, S]),
        "v": dram("v_scratch", [HEADS, P, KT * HD]),
        "ctx": dram("ctx_scratch", [B, D, S]),
        "sum": dram("sum_scratch", [B, NH, S]),
        "rec": dram("rec_scratch", [B, NH, S]),
        "w1": dram("w1_scratch", [HC, P, 2, D]),
        "w3": dram("w3_scratch", [HC, P, 2, D]),
        "w2": dram("w2_scratch", [HC, P, 2, D]),
        "h2": dram("h2_scratch", [TILES, P, 2 * DC * TOK]),
        "x2": dram("x2_scratch", [TILES, P, TK * D]),
    }
    with ExitStack() as whole:
        keep = {}

        def sb(stack, name, shape, dt=F32):
            keep[name] = stack.enter_context(nc.sbuf_tensor(name, shape, dt))

        sb(whole, "ident", [P, P])
        sb(whole, "gain_out", [P, B, D])
        with ExitStack() as most:
            sb(most, "gains", [P, 2, B, D])
            sb(most, "wp", [P, 2, DC, D], F32R)
            sb(most, "shift", [P, 4, DC * B])
            sb(most, "scale1", [P, 4, DC * B])
            with ExitStack() as early:
                sb(early, "wqk", [P, 8, 2, DC, P], F32R)
                sb(early, "wv", [P, 2, DC, D], F32R)
                prepare(nc, ins, keep, scratch)
                project_qkv(nc, ins, keep, scratch)
            attend(nc, keep, scratch)
            project_out(nc, ins, keep, scratch)
        feed_forward(nc, keep, scratch, out)


_INS = ["L0_attn_query", "L0_attn_Wqkv", "L0_attn_Wproj", "L0_attn_bproj", "L0_ffn_W1", "L0_ffn_W2", "L0_ffn_W3",
        "L0_c", "L0_wmod"]


def kernel(**inputs):
    import numpy as _np
    import concourse.bacc as _bacc
    from concourse import mybir as _mybir
    from concourse.bass_utils import run_bass_kernel_spmd as _run

    nc = _bacc.Bacc("TRN2", target_bir_lowering=False, num_devices=1)
    arrays, args = {}, []
    given = [(n, inputs[n]) for n in _INS]
    n = _np.arange(128)
    bits = _np.array([[bin(i & j).count("1") & 1 for j in range(128)] for i in range(128)])
    given += [("identity", _np.eye(128, dtype=_np.float32)), ("hadamard", (1 - 2 * bits).astype(_np.float32))]
    for name, a in given:
        a = _np.ascontiguousarray(a)
        arrays[f"in_{name}_dram"] = a
        args.append(nc.dram_tensor(f"in_{name}_dram", a.shape, _mybir.dt.from_np(a.dtype), kind="ExternalInput").ap())
    out = nc.dram_tensor("out_0_dram", (2, 2048, 512), _mybir.dt.float32, kind="ExternalOutput").ap()
    program(nc, *args, out)
    r = _run(nc, [arrays], core_ids=[0])
    return r.results[0]["out_0_dram"]
```

```python
from contextlib import ExitStack

import concourse.bass as bass
from concourse import mybir

ALU = mybir.AluOpType
ACT = mybir.ActivationFunctionType
X = mybir.AxisListType.X
F32 = mybir.dt.float32
F32R = mybir.dt.float32r

P = 128
B, S, D = 2, 2048, 512
NH, HD = 16, 32
HID = 2048
DC = D // P
HC = HID // P
TK = 4
TOK = TK * P
ST = S // TOK
TILES = B * ST
HEADS = B * NH
KT = S // P
QJ = S // TOK
EPS = 1e-5
HI, LO = 0, 1
TERMS = ((HI, HI), (HI, LO), (LO, HI))
SA, CA, SB, CB, GA, GB = range(6)
COLUMN = (0, 1, 2, 3, 4, 5)
WMOD_AT = {SA: 0, CA: 1, GA: 2, SB: 3, CB: 4, GB: 5}


def raw(ap):
    return ap.bitcast(F32)


def split_product(pe, out, stationary, moving, chunks, start=True, stop=True):
    last = None
    n = len(chunks) * len(TERMS)
    i = 0
    for c in chunks:
        for a, b in TERMS:
            last = pe.matmul(out, stationary(a, c), moving(b, c),
                             start=start and i == 0, stop=stop and i == n - 1)
            i += 1
    return last


def prepare(nc, ins, keep, scratch):
    ident, wqk, wv, wp, shift, scale1, gains = (keep[k] for k in ("ident", "wqk", "wv", "wp", "shift", "scale1", "gains"))
    NAT, OB, BANKS = 4, 4, 4
    SHIFTS = [SA, CA, SB, CB]
    jobs = [("rows", "q", j) for j in range(4)] + [("rows", "k", j) for j in range(4)]
    jobs += [("rows", "v", j) for j in range(4)] + [("rows", "p", j) for j in range(4)]
    jobs += [("mod", k, 0) for k in SHIFTS] + [("gain", k, b) for k in (GA, GB) for b in range(B)]
    jobs += [("w2", "t", c) for c in range(HC)]
    jobs += [("rows", "w1", j) for j in range(HC)] + [("rows", "w3", j) for j in range(HC)]
    jobs += [("had", "w2", c) for c in range(HC)]
    row_jobs = [n for n, j in enumerate(jobs) if j[0] == "rows"]
    store_jobs = [n for n, j in enumerate(jobs) if j[1] in ("w1", "w3") or j[0] == "had"]
    first_w1 = next(n for n, j in enumerate(jobs) if j[1] == "w1")
    last_w2t = first_w1 - 1
    kinds = SHIFTS + [GA, GB]
    kind_last_job = {k: max(n for n, j in enumerate(jobs) if j[0] in ("mod", "gain") and j[1] == k) for k in kinds}

    with ExitStack() as ctx:
        def sb(name, shape, dt=F32):
            return ctx.enter_context(nc.sbuf_tensor(name, shape, dt))

        def sem(name):
            return ctx.enter_context(nc.semaphore(name))

        had = sb("had", [P, P])
        nat = sb("nat", [P, NAT, D])
        w2a = sb("w2a", [P, HC, D])
        w2b = sb("w2b", [P, HC * D])
        wm = sb("wm", [P, 2, DC, D])
        ob = sb("ob", [P, OB, 2, D], F32R)
        ct = sb("ct", [P, DC, B])
        sc = sb("sc", [P, DC, B])
        scb = sb("scb", [P, B, DC, P])
        zero = sb("zero", [P, P])
        gtmp = sb("gtmp", [P, 2, D])
        graw = sb("graw", [P, D])
        bpb = sb("bpb", [P, D])
        mark = sb("mark", [P, 2])
        ps = ctx.enter_context(nc.psum_tensor("ps_prep", [P, BANKS, D], F32))

        const_in = sem("p_const_in")
        nat_in = [sem(f"p_nat_in{i}") for i in range(NAT)]
        w2_in = sem("p_w2_in")
        wm_in = [sem(f"p_wm_in{i}") for i in range(2)]
        job_pe = sem("p_job_pe")
        job_act = sem("p_job_act")
        job_dve = sem("p_job_dve")
        silu_done = sem("p_silu")
        scb_done = sem("p_scb")
        chain = sem("p_chain")
        fly = sem("p_butterfly")
        ob_out = [sem(f"p_ob_out{i}") for i in range(OB)]

        def rows_of(name, j):
            if name in "qkv":
                part = "qkv".index(name)
                return [(ins["wqkv"][(4 * j + h) * 3 * HD + part * HD:][:HD, :], h * HD, HD) for h in range(4)]
            w = {"p": ins["wproj"], "w1": ins["w1"], "w3": ins["w3"]}[name]
            return [(w[j * P:(j + 1) * P, :], 0, P)]

        def target(n):
            kind, name, j = jobs[n]
            if name in ("q", "k"):
                return [wqk[:, j + 4 * (name == "k"), s, :, :] for s in (HI, LO)]
            if name in ("v", "p") :
                w = wv if name == "v" else wp
                return [w[:, s, :, j * P:(j + 1) * P] for s in (HI, LO)]
            slot = store_jobs.index(n) % OB
            if kind == "had":
                return [ob[:, slot, s, :] for s in (HI, LO)]
            return [ob[:, slot, s, :].rearrange("p (c m) -> p c m", c=DC) for s in (HI, LO)]

        def bank(n, kind):
            v = ps[:, n % BANKS, :]
            return v.rearrange("p (c m) -> p c m", c=DC) if kind == "rows" else v

        def ob_free(eng, n):
            if n in store_jobs:
                m = store_jobs.index(n)
                if m >= OB:
                    eng.wait_ge(ob_out[m % OB], 16 * (m // OB))

        with nc.Block() as block:

            @block.sync
            def _(sp):
                sp.dma_start(ident[:, :], ins["identity"]).then_inc(const_in, 16)
                sp.dma_start(had[:, :], ins["hadamard"]).then_inc(const_in, 16)
                with nc.allow_non_contiguous_dma("c is 1024 numbers"):
                    for b in range(B):
                        sp.dma_start(ct[:, :, b], ins["c"][b].rearrange("(k p) -> p k", p=P)).then_inc(const_in, 16)
                sp.dma_start(bpb[:, :], ins["bproj"].partition_broadcast(P)).then_inc(const_in, 16)

                def load_rows(m):
                    n = row_jobs[m]
                    if m >= NAT:
                        sp.wait_ge(job_pe, row_jobs[m - NAT] + 1)
                    for src, p0, k in rows_of(jobs[n][1], jobs[n][2]):
                        sp.dma_start(nat[p0:p0 + k, m % NAT, :], src).then_inc(nat_in[m % NAT], 16)

                def load_mod(m):
                    k = kinds[m]
                    if m >= 2:
                        sp.wait_ge(job_pe, kind_last_job[kinds[m - 2]] + 1)
                    sp.dma_start(wm[:, m % 2, :, :], ins["wmod"].rearrange("(k p) n -> p k n", p=P)[
                        :, :, WMOD_AT[k] * D:(WMOD_AT[k] + 1) * D]).then_inc(wm_in[m % 2], 16)

                for m in range(4):
                    load_rows(m)
                load_mod(0)
                load_mod(1)
                sp.dma_start(w2b[:, :].rearrange("p (t n) -> p t n", t=DC),
                             ins["w2"].rearrange("(t p) n -> p t n", p=P)).then_inc(w2_in, 16)
                for m in range(4, 16):
                    load_rows(m)
                for m in range(2, 6):
                    load_mod(m)
                for m in range(16, len(row_jobs)):
                    load_rows(m)

            @block.tensor
            def _(pe):
                pe.wait_ge(const_in, 16 * 5)
                arrivals = [0] * NAT
                row = 0
                for n, (kind, name, j) in enumerate(jobs):
                    if n >= BANKS:
                        pe.wait_ge(job_act, n - BANKS + 1)
                        pe.wait_ge(job_dve, n - BANKS + 1)
                    if kind == "rows":
                        slot = row % NAT
                        arrivals[slot] += 16 * len(rows_of(name, j))
                        pe.wait_ge(nat_in[slot], arrivals[slot])
                        for c in range(DC):
                            last = pe.transpose(ps[:, n % BANKS, c * P:(c + 1) * P],
                                                nat[:, slot, c * P:(c + 1) * P], ident[:, :])
                        row += 1
                    elif kind == "w2":
                        if j == 0:
                            pe.wait_ge(w2_in, 16)
                        for t in range(DC):
                            last = pe.transpose(ps[:, n % BANKS, t * P:(t + 1) * P],
                                                w2b[:, t * HID + j * P:t * HID + (j + 1) * P], ident[:, :])
                    elif kind == "had":
                        if j == 0:
                            pe.wait_ge(fly, 8)
                        last = pe.matmul(ps[:, n % BANKS, :], had[:, :], w2a[:, j, :], start=True, stop=True)
                    else:
                        m = kinds.index(name)
                        pe.wait_ge(wm_in[m % 2], 16 * (m // 2 + 1))
                        if kind == "mod":
                            pe.wait_ge(silu_done, 1)
                            for c in range(DC):
                                for k in range(DC):
                                    last = pe.matmul(ps[:, n % BANKS, B * c:B * c + B],
                                                     wm[:, m % 2, k, c * P:(c + 1) * P], sc[:, k, :],
                                                     start=(k == 0), stop=(k == DC - 1))
                        else:
                            pe.wait_ge(scb_done, B * DC)
                            for k in range(DC):
                                last = pe.matmul(ps[:, n % BANKS, :], scb[:, j, k, :], wm[:, m % 2, k, :],
                                                 start=(k == 0), stop=(k == DC - 1))
                    last.then_inc(job_pe, 1)

            @block.scalar
            def _(act):
                act.wait_ge(const_in, 16 * 5)
                act.activation(sc[:, :, :], ct[:, :, :], ACT.Silu).then_inc(silu_done, 1)
                for n, (kind, name, j) in enumerate(jobs):
                    act.wait_ge(job_pe, n + 1)
                    ob_free(act, n)
                    src = bank(n, kind)
                    if kind == "rows":
                        op = act.activation(target(n)[HI], src, ACT.Copy)
                    elif kind == "had":
                        op = act.activation(target(n)[HI], src, ACT.Copy, scale=HID ** -0.5)
                    elif kind == "w2":
                        if j % 2:
                            act.wait_ge(job_act, n)
                        op = (act.activation(mark[:, 0:1], ident[:, 0:1], ACT.Copy) if j % 2
                              else act.activation(w2a[:, j, :], src, ACT.Copy))
                    elif kind == "mod":
                        op = act.activation(shift[:, name, :], src[:, 0:DC * B], ACT.Copy)
                    else:
                        if name != GA or j:
                            act.wait_ge(job_dve, n)
                        op = act.activation(graw[:, :], src, ACT.Copy)
                    op.then_inc(job_act, 1)

            @block.vector
            def _(dve):
                links = [0]

                def link(op):
                    links[0] += 1
                    op.then_inc(chain, 1)
                    dve.wait_ge(chain, links[0])

                link(dve.memset(zero[:, :], 0.0))
                dve.wait_ge(silu_done, 1)
                for b in range(B):
                    for k in range(DC):
                        dve.tensor_scalar(scb[:, b, k, :], zero[:, :], sc[:, k, b:b + 1], None,
                                          ALU.add).then_inc(scb_done, 1)

                def butterfly(m):
                    stage, minus = m // 2, m % 2
                    h = 1 << stage
                    src, dst = (w2a[:, :, :].rearrange("p c n -> p (c n)"), w2b[:, :])
                    if stage % 2:
                        src, dst = dst, src
                    src = src.rearrange("p (n t w) -> p t n w", t=2, w=h * D)
                    dst = dst.rearrange("p (n t w) -> p t n w", t=2, w=h * D)
                    if m:
                        dve.wait_ge(fly, m)
                    dve.tensor_tensor(dst[:, minus], src[:, 0], src[:, 1],
                                      ALU.subtract if minus else ALU.add).then_inc(fly, 1)

                flies = 0
                for n, (kind, name, j) in enumerate(jobs):
                    dve.wait_ge(job_pe, n + 1)
                    src = bank(n, kind)
                    if kind in ("rows", "had"):
                        ob_free(dve, n)
                        dve.wait_ge(job_act, n + 1)
                        hi, lo = target(n)
                    if kind == "rows":
                        dve.tensor_tensor(lo, src, hi, ALU.subtract).then_inc(job_dve, 1)
                    elif kind == "had":
                        dve.scalar_tensor_tensor(out=lo, in0=src, scalar=HID ** -0.5, in1=hi, op0=ALU.mult,
                                                 op1=ALU.subtract).then_inc(job_dve, 1)
                    elif kind == "w2":
                        if j % 2 == 0:
                            dve.wait_ge(job_dve, n)
                        (dve.tensor_copy(w2a[:, j, :], src) if j % 2
                         else dve.memset(mark[:, 1:2], 0.0)).then_inc(job_dve, 1)
                    elif kind == "mod":
                        dve.wait_ge(job_act, n + 1)
                        dve.tensor_scalar(scale1[:, name, :], src[:, 0:DC * B], 1.0, None,
                                          ALU.add).then_inc(job_dve, 1)
                    else:
                        dve.wait_ge(job_act, n + 1)
                        link(dve.tensor_scalar(gtmp[:, 0, :], graw[:, :], 0.0, 2.0, ALU.is_ge, ALU.mult))
                        link(dve.scalar_tensor_tensor(out=gtmp[:, 1, :], in0=gtmp[:, 0, :], scalar=-1.0,
                                                      in1=graw[:, :], op0=ALU.add, op1=ALU.mult))
                        link(dve.tensor_scalar(gtmp[:, 1, :], gtmp[:, 1, :], 0.25, None, ALU.max))
                        out = gains[:, 0, j, :] if name == GA else keep["gain_out"][:, j, :]
                        op = dve.scalar_tensor_tensor(out=out, in0=gtmp[:, 0, :], scalar=-1.0, in1=gtmp[:, 1, :],
                                                      op0=ALU.add, op1=ALU.mult)
                        if name == GA:
                            link(op)
                            op = dve.tensor_tensor(gains[:, 1, j, :], out, bpb[:, :], ALU.mult)
                        op.then_inc(job_dve, 1)
                    if n == last_w2t:
                        dve.wait_ge(job_act, n + 1)
                        dve.wait_ge(job_dve, n + 1)
                    if n >= first_w1 and (n - first_w1) % 4 == 3 and flies < 8:
                        butterfly(flies)
                        flies += 1
                while flies < 8:
                    butterfly(flies)
                    flies += 1

            @block.gpsimd
            def _(pool):
                for m, n in enumerate(store_jobs):
                    kind, name, j = jobs[n]
                    pool.wait_ge(job_act, n + 1)
                    pool.wait_ge(job_dve, n + 1)
                    pool.dma_start(scratch["w2" if kind == "had" else name][j],
                                   raw(ob[:, m % OB, :, :])).then_inc(ob_out[m % OB], 16)
                for i in range(OB):
                    pool.wait_ge(ob_out[i], 16 * len(range(i, len(store_jobs), OB)))


LINKS = 4


def norm_stats(dve, chain, rooted, t, x, st, mv, dev, rstd, nmr):
    base = LINKS * t
    for k in range(TK):
        last = dve.bn_stats(st[:, k, :], x[:, k, :])
    last.then_inc(chain, 1)
    dve.wait_ge(chain, base + 1)
    dve.memset(dev, 0.0)
    for k in range(TK):
        last = dve.bn_aggr(mv[:, k, :], st[:, k, :])
    last.then_inc(chain, 1)
    dve.wait_ge(chain, base + 2)
    dve.tensor_scalar(dev, mv[:, :, 1], EPS, None, ALU.add).then_inc(chain, 1)
    dve.wait_ge(rooted, t + 1)
    dve.reciprocal(rstd, dev).then_inc(chain, 1)
    dve.wait_ge(chain, base + 4)
    return dve.scalar_tensor_tensor(out=nmr, in0=mv[:, :, 0], scalar=-1.0, in1=rstd, op0=ALU.mult, op1=ALU.mult)


def project_qkv(nc, ins, keep, scratch):
    ident, wqk, wv, shift, scale1 = (keep[k] for k in ("ident", "wqk", "wv", "shift", "scale1"))
    NQK = 8
    NJ = NQK + TK
    MID = 5
    BANKS = 4
    OB = 4
    with ExitStack() as ctx:
        def sb(name, shape, dt=F32):
            return ctx.enter_context(nc.sbuf_tensor(name, shape, dt))

        def sem(name):
            return ctx.enter_context(nc.semaphore(name))

        xin = sb("xin", [P, 2, TK, D])
        xn = sb("xn", [P, 2, TK, D])
        ht = sb("ht", [P, 2, 2, DC, TOK], F32R)
        full = sb("full", [P, DC, TOK])
        st = sb("st", [P, TK, 6])
        mv = sb("mv", [P, TK, 2])
        dev = sb("dev", [P, TK])
        mark = sb("mark2", [P, 1])
        rstd = sb("rstd", [P, 2, TK])
        nmr = sb("nmr", [P, 2, TK])
        ob = sb("obq", [P, OB, 2, TOK], F32R)
        vst = sb("vst", [P, 2, NH, TK, HD])
        ps = ctx.enter_context(nc.psum_tensor("ps_qkv", [P, BANKS, TOK], F32))
        pt = ctx.enter_context(nc.psum_tensor("ps_ht", [P, DC, TOK], F32))

        x_in = [sem(f"a_x_in{i}") for i in range(2)]
        chain = sem("a_chain")
        rooted = sem("a_rooted")
        stats = sem("a_stats")
        normed = sem("a_normed")
        turned = sem("a_turned")
        h_hi = sem("a_h_hi")
        h_full = sem("a_h_full")
        h_lo = sem("a_h_lo")
        mm = sem("a_mm")
        out_hi = sem("a_out_hi")
        out_lo = sem("a_out_lo")
        ob_out = [sem(f"a_ob_out{i}") for i in range(OB)]
        v_out = [sem(f"a_v_out{i}") for i in range(2)]


        with nc.Block() as block:

            @block.sync
            def _(sp):
                def load(s, b, fresh=False):
                    if not fresh:
                        sp.wait_ge(normed, TK * (2 * s + b - 1))
                    sp.dma_start(xin[:, b, :, :], ins["x"][b].rearrange("(t k p) d -> t p k d", k=TK, p=P)[
                        bass.ds(s, 1)].rearrange("o p k d -> (o p) k d")).then_inc(x_in[b], 16)

                def store(s, b):
                    for j in range(NQK):
                        sp.wait_ge(out_lo, NJ * (2 * s + b) + j + 1)
                        dst = scratch["q" if j < 4 else "k"]
                        r0 = b * NH * HD + (j % 4) * P
                        sp.dma_start(dst[:, r0:r0 + P, bass.ds(s * TOK, TOK)].rearrange("l r n -> r l n"),
                                     raw(ob[:, j % OB, :, :])).then_inc(ob_out[j % OB], 16)
                    sp.wait_ge(out_hi, NJ * (2 * s + b + 1))
                    sp.dma_start(scratch["v"][b * NH:(b + 1) * NH, :, bass.ds(s * TK * HD, TK * HD)].rearrange(
                        "g p n -> p g n"), vst[:, b, :, :, :].rearrange("p h k d -> p h (k d)")).then_inc(v_out[b], 16)

                load(0, 0, True)
                load(0, 1, True)
                with sp.Fori(0, ST - 1) as s:
                    load(s + 1, 0)
                    store(s, 0)
                    load(s + 1, 1)
                    store(s, 1)
                store(ST - 1, 0)
                store(ST - 1, 1)
                for i in range(OB):
                    sp.wait_ge(ob_out[i], 16 * 2 * TILES)
                for b in range(2):
                    sp.wait_ge(v_out[b], 16 * ST)

            @block.tensor
            def _(pe):
                def turn(s, b, fresh=False):
                    t = 2 * s + b
                    pe.wait_ge(normed, TK * (t + 1))
                    if not fresh:
                        pe.wait_ge(h_hi, DC * t)
                        pe.wait_ge(h_full, DC * t)
                    for c in range(DC):
                        for k in range(TK):
                            last = pe.transpose(pt[:, c, k * P:(k + 1) * P], xn[:, b, k, c * P:(c + 1) * P],
                                                ident[:, :])
                        last.then_inc(turned, 1)

                def results(s, b, j, fresh=False):
                    n = NJ * (2 * s + b) + j
                    if j == 0:
                        pe.wait_ge(h_hi, DC * (2 * s + b + 1))
                        pe.wait_ge(h_lo, DC * (2 * s + b + 1))
                    if not (fresh and j < BANKS):
                        pe.wait_ge(out_hi, n - BANKS + 1)
                        pe.wait_ge(out_lo, n - BANKS + 1)
                    if j < NQK:
                        last = split_product(pe, ps[:, j % BANKS, :], lambda a, c: wqk[:, j, a, c, :],
                                             lambda a, c: ht[:, b, a, c, :], range(DC))
                    else:
                        k = j - NQK
                        last = split_product(pe, ps[:, j % BANKS, :],
                                             lambda a, c: ht[:, b, a, c, k * P:(k + 1) * P],
                                             lambda a, c: wv[:, a, c, :], range(DC))
                    last.then_inc(mm, 1)

                def tile(s, b, nxt, fresh=False):
                    for j in range(NJ):
                        results(s, b, j, fresh)
                        if j == MID and nxt:
                            turn(*nxt)

                turn(0, 0, True)
                tile(0, 0, (0, 1), True)
                tile(0, 1, (1, 0))
                with pe.Fori(1, ST - 1) as s:
                    tile(s, 0, (s, 1))
                    tile(s, 1, (s + 1, 0))
                tile(ST - 1, 0, (ST - 1, 1))
                tile(ST - 1, 1, None)

            @block.scalar
            def _(act):
                def normalise(s, b, fresh=False):
                    t = 2 * s + b
                    act.wait_ge(chain, LINKS * t + 3)
                    act.activation(dev[:, :], dev[:, :], ACT.Sqrt).then_inc(rooted, 1)
                    act.wait_ge(stats, t + 1)
                    act.wait_ge(x_in[b], 16 * (s + 1))
                    if not fresh:
                        act.wait_ge(turned, DC * (t - 1))
                    for k in range(TK):
                        act.activation(xn[:, b, k, :], xin[:, b, k, :], ACT.Identity, bias=nmr[:, b, k:k + 1],
                                       scale=rstd[:, b, k:k + 1]).then_inc(normed, 1)

                def high_parts(s, b, fresh=False):
                    t = 2 * s + b
                    if not fresh:
                        act.wait_ge(mm, NJ * (t - 1))
                    for c in range(DC):
                        act.wait_ge(turned, DC * t + c + 1)
                        act.activation(ht[:, b, HI, c, :], pt[:, c, :], ACT.Identity,
                                       bias=shift[:, SA, B * c + b:B * c + b + 1],
                                       scale=scale1[:, CA, B * c + b:B * c + b + 1]).then_inc(h_hi, 1)

                def tile(s, b, nxt, fresh=False):
                    if nxt:
                        normalise(*nxt, fresh and b == 0)
                    for j in range(NJ):
                        n = NJ * (2 * s + b) + j
                        act.wait_ge(mm, n + 1)
                        if j < NQK:
                            if not (fresh and b == 0 and j < OB):
                                act.wait_ge(ob_out[j % OB], 16 * (2 * (2 * s + b) + j // OB))
                            act.activation(ob[:, j % OB, HI, :], ps[:, j % BANKS, :], ACT.Copy).then_inc(out_hi, 1)
                        else:
                            if j == NQK and not fresh:
                                act.wait_ge(v_out[b], 16 * s)
                            act.activation(vst[:, b, :, j - NQK, :],
                                           ps[:, j % BANKS, :].rearrange("p (h d) -> p h d", h=NH),
                                           ACT.Copy).then_inc(out_hi, 1)
                        if j == MID + 1 and nxt:
                            high_parts(*nxt, fresh and b == 0)

                normalise(0, 0, True)
                high_parts(0, 0, True)
                tile(0, 0, (0, 1), True)
                tile(0, 1, (1, 0), True)
                with act.Fori(1, ST - 1) as s:
                    tile(s, 0, (s, 1))
                    tile(s, 1, (s + 1, 0))
                tile(ST - 1, 0, (ST - 1, 1))
                tile(ST - 1, 1, None)

            @block.vector
            def _(dve):
                def measure(s, b, fresh=False):
                    t = 2 * s + b
                    dve.wait_ge(x_in[b], 16 * (s + 1))
                    if not fresh:
                        dve.wait_ge(normed, TK * (t - 1))
                    norm_stats(dve, chain, rooted, t, xin[:, b, :, :], st, mv, dev[:, :], rstd[:, b, :],
                               nmr[:, b, :]).then_inc(stats, 1)

                def low_parts(s, b, fresh=False):
                    t = 2 * s + b
                    for c in range(DC):
                        dve.wait_ge(h_hi, DC * t + c + 1)
                        dve.tensor_scalar(full[:, c, :], pt[:, c, :], scale1[:, CA, B * c + b:B * c + b + 1],
                                          shift[:, SA, B * c + b:B * c + b + 1], ALU.mult,
                                          ALU.add).then_inc(h_full, 1)
                    for c in range(DC):
                        dve.wait_ge(h_full, DC * t + c + 1)
                        dve.tensor_tensor(ht[:, b, LO, c, :], full[:, c, :], ht[:, b, HI, c, :],
                                          ALU.subtract).then_inc(h_lo, 1)

                def tile(s, b, nxt, fresh=False):
                    if nxt:
                        measure(*nxt, fresh and b == 0)
                    for j in range(NJ):
                        n = NJ * (2 * s + b) + j
                        dve.wait_ge(out_hi, n + 1)
                        if j < NQK:
                            dve.tensor_tensor(ob[:, j % OB, LO, :], ps[:, j % BANKS, :], ob[:, j % OB, HI, :],
                                              ALU.subtract).then_inc(out_lo, 1)
                        else:
                            dve.wait_ge(out_lo, n)
                            dve.memset(mark[:, :], 0.0).then_inc(out_lo, 1)
                        if j == MID + 1 and nxt:
                            low_parts(*nxt)

                measure(0, 0, True)
                low_parts(0, 0)
                tile(0, 0, (0, 1), True)
                tile(0, 1, (1, 0), True)
                with dve.Fori(1, ST - 1) as s:
                    tile(s, 0, (s, 1))
                    tile(s, 1, (s + 1, 0))
                tile(ST - 1, 0, (ST - 1, 1))
                tile(ST - 1, 1, None)


DIRECT = (13, 14, 15)
GROUPS = ((0, 1, 2), (3, 4, 5), (6, 7, 8), (9, 10, 11, 12))
ADDS = sum(len(g) - 1 for g in GROUPS)
UNIT_ORDER = (("group", 0), ("group", 1), ("group", 2), ("tile", 13), ("tile", 14), ("tile", 15), ("group", 3))
UNITS = len(UNIT_ORDER)
STEPS = (["qMqMUMqMqMUMUM", "qMqMUMUMqMqUMUM", "qMqMPqMq"] + ["qMqMPMqMq"] * 10 + ["qMqMPqMq", "qqPqqT", "qMqMPMqMq"])
LAG = 2
LEAD = 2


def adds_until(kt):
    n = 0
    for g in GROUPS:
        for i, k in enumerate(g):
            n += i > 0
            if k == kt:
                return n + (i == 0)
    raise ValueError(kt)


def attend(nc, keep, scratch):
    ident = keep["ident"]
    SLOTS, RING, KR = 4, 8, 3 * HD
    NM = KT * QJ
    EARLY = STEPS[KT - 1].count("M")
    assert sum(x.count("M") for x in STEPS) == NM and sum(x.count("U") for x in STEPS) == UNITS
    MR = 3
    TURN_BANK = NM % MR
    SCALE = HD ** -0.5
    HALF = S // 2
    LOADS = 16 * 7
    with ExitStack() as ctx:
        def sb(name, shape, dt=F32):
            return ctx.enter_context(nc.sbuf_tensor(name, shape, dt))

        def sem(name):
            return ctx.enter_context(nc.semaphore(name))

        qst = sb("qst", [KR + 2, SLOTS, S], F32R)
        kst = sb("kst", [KR + 2, SLOTS, S], F32R)
        v = sb("v", [P, SLOTS, KT, HD])
        prob = sb("prob", [P, RING, S])
        gsum = sb("gsum", [P, len(GROUPS), S])
        ctxo = sb("ctxo", [P, 2, TOK])
        sumo = sb("sumo", [P, TOK])
        recb = sb("recb", [P, TOK])
        sumc = sb("sumc", [P, S // P])
        recc = sb("recc", [P, S // P])
        mxp = sb("mxp", [P, KT, QJ])
        mx = sb("mx", [P, KT])
        mrow = sb("mrow", [KT, 2, P], F32R)
        ones = sb("ones", [P, HD])
        mark = sb("mark3", [P, 10])
        pexp = ctx.enter_context(nc.psum_tensor("pexp", [P, 2, HALF], F32))
        pmax = ctx.enter_context(nc.psum_tensor("pmax", [P, MR, TOK], F32))
        pctx = ctx.enter_context(nc.psum_tensor("pctx", [P, TOK], F32))

        const = sem("b_const")
        loaded = [sem(f"b_loaded{i}") for i in range(SLOTS)]
        scores = sem("b_scores")
        exp_done = sem("b_exp_done")
        mm_max = sem("b_mm_max")
        mx_done = sem("b_mx_done")
        mx_all = sem("b_mx_all")
        mx_turned = sem("b_mx_turned")
        m_split = sem("b_m_split")
        m_row = sem("b_m_row")
        pv_done = sem("b_pv_done")
        unit_done = sem("b_unit_done")
        add_done = sem("b_add_done")
        ctx_read = sem("b_ctx_read")
        sum_read = sem("b_sum_read")
        divided = sem("b_divided")
        sum_out = sem("b_sum_out")
        sum_in = sem("b_sum_in")
        inverted = sem("b_inverted")
        rec_out = sem("b_rec_out")
        rec_in = sem("b_rec_in")
        out_done = [sem(f"b_out_done{i}") for i in range(2)]
        OUTS = 16 * QJ

        def heads(eng, step):
            with eng.Fori(0, HEADS // SLOTS - 1) as i:
                for r in range(SLOTS):
                    step(i * SLOTS + r, i, r)
            i = HEADS // SLOTS - 1
            for r in range(SLOTS):
                step(i * SLOTS + r, i, r)

        def exists(g):
            return not isinstance(g, int) or g < HEADS

        with nc.Block() as block:

            @block.sync
            def _(sp):
                def load(g, slot):
                    rows = bass.ds(g * HD, HD)
                    q, k = scratch["q"], scratch["k"]
                    for r, part in enumerate((HI, LO, HI)):
                        sp.dma_start(raw(qst[r * HD:(r + 1) * HD, slot, :]), q[part, rows, :]).then_inc(loaded[slot], 16)
                    for r, part in enumerate((HI, HI, LO)):
                        sp.dma_start(raw(kst[r * HD:(r + 1) * HD, slot, :]), k[part, rows, :]).then_inc(loaded[slot], 16)
                    sp.dma_start(v[:, slot, :, :].rearrange("p k d -> p (k d)"),
                                 scratch["v"][bass.ds(g, 1)].rearrange("o p n -> (o p) n")).then_inc(loaded[slot], 16)

                def max_row(g, slot):
                    sp.wait_ge(m_split, 2 * (g + 1))
                    for part in (HI, LO):
                        r = KR + part
                        sp.dma_start(raw(qst[r:r + 1, slot, :]).rearrange("o (t n) -> o t n", t=KT),
                                     raw(mrow[:, part, :])).then_inc(m_row, 16)

                def invert(g):
                    sp.wait_ge(sum_read, g + 2)
                    sp.dma_start(scratch["sum"].rearrange("(j n) -> j n", j=QJ), sumo[0:P:HD, :]).then_inc(sum_out, 16)
                    sp.wait_ge(sum_out, 16 * (g + 2))
                    sp.dma_start(sumc[:, :], scratch["sum"].rearrange("(p n) -> p n", p=P)).then_inc(sum_in, 16)
                    sp.wait_ge(inverted, g + 1)
                    sp.dma_start(scratch["rec"].rearrange("(p n) -> p n", p=P), recc[:, :]).then_inc(rec_out, 16)
                    sp.wait_ge(rec_out, 16 * (g + 1))
                    sp.wait_ge(divided, g + 2)
                    for j in range(QJ):
                        sp.dma_start(recb[j * HD:(j + 1) * HD, :], scratch["rec"][j * TOK:(j + 1) * TOK]
                                     .partition_broadcast(HD)).then_inc(rec_in, 16)

                def store(g, par, pair):
                    sp.wait_ge(divided, g + 3)
                    for j in range(QJ):
                        sp.dma_start(scratch["ctx"][par, bass.ds(pair * HD, HD), j * TOK:(j + 1) * TOK],
                                     ctxo[j * HD:(j + 1) * HD, par, :]).then_inc(out_done[par], 16)

                def step(g, i, r):
                    static = isinstance(g, int)
                    par = r % 2
                    if not static or g + 3 < HEADS:
                        sp.wait_ge(pv_done, RING + KT * g)
                        load(g + 3, (r + 3) % SLOTS)
                    if not static or g >= 2:
                        store(g - 2, par, i * 2 + r // 2 - 1)
                    if not static or g >= 1:
                        invert(g - 1)
                    if not static or g + 1 < HEADS:
                        max_row(g + 1, (r + 1) % SLOTS)

                for g in range(3):
                    load(g, g)
                max_row(0, 0)
                for r in range(SLOTS):
                    step(r, 0, r)
                with sp.Fori(1, HEADS // SLOTS - 1) as i:
                    for r in range(SLOTS):
                        step(i * SLOTS + r, i, r)
                i = HEADS // SLOTS - 1
                for r in range(SLOTS):
                    step(i * SLOTS + r, i, r)
                store(HEADS - 2, 0, NH - 1)
                invert(HEADS - 1)
                store(HEADS - 1, 1, NH - 1)
                for par in range(2):
                    sp.wait_ge(out_done[par], 16 + OUTS * HEADS // 2)

            @block.tensor
            def _(pe):
                def maximum(g, slot, u, fresh=False):
                    qt, kc = u // QJ, u % QJ
                    if u >= MR:
                        pe.wait_ge(mx_done, g * NM + u - MR + 1)
                    elif not fresh:
                        pe.wait_ge(mx_done, g * NM)
                    if u == TURN_BANK and not fresh:
                        pe.wait_ge(m_split, 2 * g)
                    pe.matmul(pmax[:, u % MR, :], qst[0:KR, slot, qt * P:(qt + 1) * P],
                              kst[0:KR, slot, kc * TOK:(kc + 1) * TOK], start=True, stop=True).then_inc(mm_max, 1)

                def turn_max(g):
                    pe.wait_ge(mx_all, g + 1)
                    pe.transpose(pmax[0:KT, TURN_BANK, 0:P], mx[:, :], ident[:, :]).then_inc(mx_turned, 1)

                def score(g, slot, kt, half, j):
                    if j == 0:
                        if kt == 0 and half == 0:
                            pe.wait_ge(m_row, 32 * (g + 1))
                        pe.wait_ge(exp_done, 2 * KT * g + 2 * kt + half + 1)
                    q0 = half * HALF + j * TOK
                    pe.matmul(pexp[:, half, j * TOK:(j + 1) * TOK], kst[:, slot, kt * P:(kt + 1) * P],
                              qst[:, slot, q0:q0 + TOK], start=True, stop=True).then_inc(scores, 1)

                def weigh(g, slot, kt):
                    pe.wait_ge(exp_done, 2 * KT * g + 2 * kt + 4)
                    if kt == 0:
                        pe.wait_ge(sum_read, g + 1)
                    for j in range(QJ):
                        last = pe.matmul(pctx[j * HD:(j + 1) * HD, :], v[:, slot, kt, :],
                                         prob[:, kt % RING, j * TOK:(j + 1) * TOK], start=(kt == 0), stop=(kt == KT - 1))
                    last.then_inc(pv_done, 1)

                def unit(g, n):
                    kind, k = UNIT_ORDER[n]
                    if n == 0:
                        pe.wait_ge(ctx_read, g + 2)
                    if kind == "group":
                        pe.wait_ge(add_done, ADDS + ADDS * g + adds_until(GROUPS[k][-1]))
                    src = gsum[:, k, :] if kind == "group" else prob[:, k % RING, :]
                    for j in range(QJ):
                        last = pe.matmul(pctx[j * HD:(j + 1) * HD, :], ones[:, :], src[:, j * TOK:(j + 1) * TOK],
                                         start=(n == 0), stop=(n == UNITS - 1))
                    last.then_inc(unit_done, 1)

                def run(g, r, kts, ahead, far, closing):
                    u = sum(STEPS[kt].count("M") for kt in range(kts[0])) + EARLY
                    n = 0
                    for kt in kts:
                        q = v = 0
                        for x in STEPS[kt]:
                            if x == "q":
                                score(g, r, kt, q // 2, q % 2)
                                q += 1
                            elif x == "P":
                                weigh(g, r, kt - LAG)
                            elif x == "U" and closing:
                                unit(g - 1, n)
                                n += 1
                            elif x == "T" and ahead:
                                turn_max(g + 1)
                            elif x == "M" and kt == KT - 1 and far:
                                maximum(g + 2, (r + 2) % SLOTS, v)
                                v += 1
                            elif x == "M" and kt < KT - 1 and ahead:
                                maximum(g + 1, (r + 1) % SLOTS, u)
                                u += 1

                def step(g, i, r):
                    if exists(g + 2):
                        pe.wait_ge(loaded[(r + 2) % SLOTS], LOADS * (i + 1 + (r + 2) // SLOTS))
                    run(g, r, range(LEAD, KT), exists(g + 1), exists(g + 2), False)
                    weigh(g, r, KT - 2)
                    weigh(g, r, KT - 1)
                    if exists(g + 1):
                        run(g + 1, (r + 1) % SLOTS, range(LEAD), exists(g + 2), False, True)
                    else:
                        for n in range(UNITS):
                            unit(g, n)

                pe.wait_ge(const, 2)
                pe.wait_ge(loaded[0], LOADS)
                for u in range(NM):
                    maximum(0, 0, u, True)
                turn_max(0)
                pe.wait_ge(loaded[1], LOADS)
                for u in range(EARLY):
                    maximum(1, 1, u)
                run(0, 0, range(LEAD), True, False, False)
                heads(pe, step)

            @block.scalar
            def _(act):
                def exps(g, kts):
                    for kt in kts:
                        act.wait_ge(pv_done, KT * g + kt + 1)
                        old = (kt - RING) % KT
                        back = 0 if kt >= RING else 1
                        if old in DIRECT:
                            act.wait_ge(unit_done, UNITS + UNITS * g - UNITS * back + UNIT_ORDER.index(("tile", old)) + 1)
                        else:
                            act.wait_ge(add_done, ADDS + ADDS * g - ADDS * back + adds_until(old))
                        for half in range(2):
                            act.wait_ge(scores, QJ * (KT * g + kt) + 2 * half + 2)
                            act.activation(prob[:, kt % RING, half * HALF:(half + 1) * HALF], pexp[:, half, :],
                                           ACT.Exp, scale=SCALE).then_inc(exp_done, 1)

                def step(g, i, r):
                    par = r % 2
                    exps(g, range(LEAD, KT))
                    act.wait_ge(out_done[par], 16 + OUTS * (2 * i + r // 2))
                    act.wait_ge(pv_done, RING + KT * (g + 1))
                    act.activation(ctxo[:, par, :], pctx[:, :], ACT.Copy).then_inc(ctx_read, 1)
                    if exists(g + 1):
                        exps(g + 1, range(LEAD))
                    act.wait_ge(unit_done, UNITS + UNITS * (g + 1))
                    act.wait_ge(sum_out, 16 + 16 * g)
                    act.activation(sumo[:, :], pctx[:, :], ACT.Copy).then_inc(sum_read, 1)

                exps(0, range(LEAD))
                heads(act, step)

            @block.vector
            def _(dve):
                dve.memset(ones[:, :], 1.0).then_inc(const, 1)
                dve.memset(kst[KR:KR + 2, :, :].bitcast(F32), 1.0).then_inc(const, 1)
                credits = ((exp_done, 2), (pv_done, RING), (unit_done, UNITS), (add_done, ADDS), (ctx_read, 1),
                           (sum_read, 1), (divided, 2), (sum_out, 16), (out_done[0], 16), (out_done[1], 16))
                for i, (free, n) in enumerate(credits):
                    dve.memset(mark[:, i:i + 1], 0.0).then_inc(free, n)

                def invert(g):
                    dve.wait_ge(sum_in, 16 * (g + 1))
                    dve.wait_ge(rec_out, 16 * g)
                    dve.reciprocal(recc[:, :], sumc[:, :]).then_inc(inverted, 1)

                def maxima(g, old=None):
                    for u in range(NM):
                        if u == NM // 2 and old is not None:
                            invert(old)
                        dve.wait_ge(mm_max, g * NM + u + 1)
                        dve.tensor_reduce(mxp[:, u // QJ, u % QJ:u % QJ + 1], pmax[:, u % MR, :], X,
                                          ALU.max).then_inc(mx_done, 1)
                    dve.wait_ge(mx_done, (g + 1) * NM)
                    dve.tensor_reduce(mx[:, :], mxp[:, :, :], X, ALU.max).then_inc(mx_all, 1)
                    dve.wait_ge(mx_turned, g + 1)
                    dve.wait_ge(m_row, 32 * g)
                    dve.tensor_scalar(mrow[:, HI, :], pmax[0:KT, TURN_BANK, 0:P], -1.0, None, ALU.mult).then_inc(m_split, 1)
                    dve.wait_ge(m_split, 2 * g + 1)
                    dve.scalar_tensor_tensor(out=mrow[:, LO, :], in0=pmax[0:KT, TURN_BANK, 0:P], scalar=-1.0,
                                             in1=mrow[:, HI, :], op0=ALU.mult, op1=ALU.subtract).then_inc(m_split, 1)

                maxima(0)
                maxima(1)
                maxima(2, 0)
                with dve.Fori(3, HEADS) as g:
                    maxima(g, g - 2)
                invert(HEADS - 2)
                invert(HEADS - 1)

            @block.gpsimd
            def _(pool):
                def head(g):
                    n = 0
                    for k, grp in enumerate(GROUPS):
                        dst = gsum[:, k, :]
                        pool.wait_ge(unit_done, UNITS * g + UNIT_ORDER.index(("group", k)) + 1)
                        for m, kt in enumerate(grp[1:]):
                            pool.wait_ge(exp_done, 2 * KT * g + 2 * kt + 4)
                            a = prob[:, grp[0] % RING, :] if m == 0 else dst
                            if m:
                                pool.wait_ge(add_done, ADDS + ADDS * g + n)
                            pool.tensor_tensor(dst, a, prob[:, kt % RING, :], ALU.add).then_inc(add_done, 1)
                            n += 1

                def divide(g, n, par):
                    pool.wait_ge(rec_in, 16 * QJ * (g + 1))
                    pool.wait_ge(ctx_read, g + 2)
                    pool.tensor_tensor(ctxo[:, par, :], ctxo[:, par, :], recb[:, :], ALU.mult).then_inc(divided, 1)

                head(0)
                with pool.Fori(0, HEADS // 2 - 1) as n:
                    head(2 * n + 1)
                    divide(2 * n, n, 0)
                    head(2 * n + 2)
                    divide(2 * n + 1, n, 1)
                head(HEADS - 1)
                divide(HEADS - 2, HEADS // 2 - 1, 0)
                divide(HEADS - 1, HEADS // 2 - 1, 1)


def project_out(nc, ins, keep, scratch):
    ident, wp, shift, scale1, gains = (keep[k] for k in ("ident", "wp", "shift", "scale1", "gains"))
    with ExitStack() as ctx:
        def sb(name, shape, dt=F32):
            return ctx.enter_context(nc.sbuf_tensor(name, shape, dt))

        def sem(name):
            return ctx.enter_context(nc.semaphore(name))

        cin = sb("cin", [P, 2, DC, TOK])
        cs = sb("cs", [P, 2, 2, DC, TOK], F32R)
        xin = sb("xin2", [P, 2, TK, D])
        x2 = sb("x2", [P, 2, TK, D])
        xn = sb("xn2", [P, TK, D])
        h2 = sb("h2", [P, 2, DC, TOK])
        st = sb("st2", [P, TK, 6])
        mv = sb("mv2", [P, TK, 2])
        dev = sb("dev2", [P, TK])
        rstd = sb("rstd2", [P, TK])
        nmr = sb("nmr2", [P, TK])
        po = ctx.enter_context(nc.psum_tensor("po", [P, TK, D], F32))
        pt = ctx.enter_context(nc.psum_tensor("pt2", [P, DC, TOK], F32))

        tile_in = [sem(f"c_tile_in{i}") for i in range(2)]
        c_hi = sem("c_ctx_hi")
        c_lo = sem("c_ctx_lo")
        x_bias = sem("c_x_bias")
        mm = sem("c_mm")
        scaled = sem("c_scaled")
        resid = sem("c_resid")
        chain = sem("c_chain")
        rooted = sem("c_rooted")
        stats = sem("c_stats")
        normed = sem("c_normed")
        turned = sem("c_turned")
        h_done = sem("c_h_done")
        tile_out = [sem(f"c_tile_out{i}") for i in range(2)]


        with nc.Block() as block:

            @block.sync
            def _(sp):
                def load(s, b, fresh=False):
                    if not fresh:
                        sp.wait_ge(c_lo, DC * (2 * s + b - 1))
                        sp.wait_ge(resid, TK * (2 * s + b - 1))
                    tok = bass.ds(s * TOK, TOK)
                    sp.dma_start(cin[:, b, :, :], scratch["ctx"][b].rearrange("(c p) n -> p c n", p=P)[
                        :, :, tok]).then_inc(tile_in[b], 16)
                    sp.dma_start(xin[:, b, :, :], ins["x"][b].rearrange("(t k p) d -> t p k d", k=TK, p=P)[
                        bass.ds(s, 1)].rearrange("o p k d -> (o p) k d")).then_inc(tile_in[b], 16)

                def store(s, b):
                    t = 2 * s + b
                    sp.wait_ge(resid, TK * (t + 1))
                    sp.dma_start(scratch["x2"][bass.ds(t, 1)].rearrange("o p n -> (o p) n"),
                                 x2[:, b, :, :].rearrange("p k d -> p (k d)")).then_inc(tile_out[b], 16)
                    sp.wait_ge(h_done, DC * (t + 1))
                    sp.dma_start(scratch["h2"][bass.ds(t, 1)].rearrange("o p n -> (o p) n"),
                                 h2[:, b, :, :].rearrange("p c n -> p (c n)")).then_inc(tile_out[b], 16)

                load(0, 0, True)
                load(0, 1, True)
                with sp.Fori(0, ST - 1) as s:
                    load(s + 1, 0)
                    store(s, 0)
                    load(s + 1, 1)
                    store(s, 1)
                store(ST - 1, 0)
                store(ST - 1, 1)
                for b in range(2):
                    sp.wait_ge(tile_out[b], 16 + 32 * ST)

            @block.tensor
            def _(pe):
                def project(s, b):
                    t = 2 * s + b
                    pe.wait_ge(c_hi, DC * (t + 1))
                    pe.wait_ge(c_lo, DC * (t + 1))
                    for k in range(TK):
                        pe.wait_ge(scaled, TK * t + k + 1 - TK) if not isinstance(t, int) or t else None
                        split_product(pe, po[:, k, :], lambda a, c: cs[:, b, a, c, k * P:(k + 1) * P],
                                      lambda a, c: wp[:, a, c, :], range(DC)).then_inc(mm, 1)

                def turn(s, b):
                    t = 2 * s + b
                    pe.wait_ge(normed, TK * (t + 1))
                    pe.wait_ge(h_done, DC * t)
                    for c in range(DC):
                        for k in range(TK):
                            last = pe.transpose(pt[:, c, k * P:(k + 1) * P], xn[:, k, c * P:(c + 1) * P], ident[:, :])
                        last.then_inc(turned, 1)

                project(0, 0)
                project(0, 1)
                turn(0, 0)
                with pe.Fori(1, ST) as s:
                    project(s, 0)
                    turn(s - 1, 1)
                    project(s, 1)
                    turn(s, 0)
                turn(ST - 1, 1)

            @block.gpsimd
            def _(pool):
                def tile(s, b):
                    t = 2 * s + b
                    pool.wait_ge(tile_in[b], 32 * (s + 1))
                    for k in range(TK):
                        pool.tensor_tensor(xin[:, b, k, :], xin[:, b, k, :], gains[:, 1, b, :],
                                           ALU.add).then_inc(x_bias, 1)

                tile(0, 0)
                tile(0, 1)
                with pool.Fori(1, ST) as s:
                    tile(s, 0)
                    tile(s, 1)

            @block.scalar
            def _(act):
                def ctx_high(s, b, fresh=False):
                    t = 2 * s + b
                    if not fresh:
                        act.wait_ge(mm, TK * (t - 1))
                    act.wait_ge(tile_in[b], 32 * (s + 1))
                    for c in range(DC):
                        act.activation(cs[:, b, HI, c, :], cin[:, b, c, :], ACT.Copy).then_inc(c_hi, 1)

                def normalise(s, b):
                    t = 2 * s + b
                    act.wait_ge(chain, LINKS * t + 3)
                    act.activation(dev[:, :], dev[:, :], ACT.Sqrt).then_inc(rooted, 1)
                    act.wait_ge(stats, t + 1)
                    act.wait_ge(turned, DC * t)
                    for k in range(TK):
                        act.activation(xn[:, k, :], x2[:, b, k, :], ACT.Identity, bias=nmr[:, k:k + 1],
                                       scale=rstd[:, k:k + 1]).then_inc(normed, 1)

                def high_parts(s, b):
                    t = 2 * s + b
                    act.wait_ge(tile_out[b], 16 + 32 * s)
                    for c in range(DC):
                        act.wait_ge(turned, DC * t + c + 1)
                        act.activation(h2[:, b, c, :], pt[:, c, :], ACT.Identity,
                                       bias=shift[:, SB, B * c + b:B * c + b + 1],
                                       scale=scale1[:, CB, B * c + b:B * c + b + 1]).then_inc(h_done, 1)

                ctx_high(0, 0, True)
                ctx_high(0, 1, True)
                normalise(0, 0)
                high_parts(0, 0)
                with act.Fori(1, ST) as s:
                    ctx_high(s, 0)
                    normalise(s - 1, 1)
                    high_parts(s - 1, 1)
                    ctx_high(s, 1)
                    normalise(s, 0)
                    high_parts(s, 0)
                normalise(ST - 1, 1)
                high_parts(ST - 1, 1)

            @block.vector
            def _(dve):
                for b in range(2):
                    dve.memset(nmr[:, b:b + 1], 0.0).then_inc(tile_out[b], 16)

                def ctx_low(s, b):
                    t = 2 * s + b
                    for c in range(DC):
                        dve.wait_ge(c_hi, DC * t + c + 1)
                        dve.tensor_tensor(cs[:, b, LO, c, :], cin[:, b, c, :], cs[:, b, HI, c, :],
                                          ALU.subtract).then_inc(c_lo, 1)

                def residual(s, b):
                    t = 2 * s + b
                    dve.wait_ge(tile_out[b], 16 + 32 * s)
                    for k in range(TK):
                        dve.wait_ge(mm, TK * t + k + 1)
                        dve.tensor_tensor(x2[:, b, k, :], po[:, k, :], gains[:, 0, b, :],
                                          ALU.mult).then_inc(scaled, 1)
                    for k in range(TK):
                        dve.wait_ge(scaled, TK * t + k + 1)
                        dve.wait_ge(x_bias, TK * t + k + 1)
                        dve.tensor_tensor(x2[:, b, k, :], x2[:, b, k, :], xin[:, b, k, :],
                                          ALU.add).then_inc(resid, 1)
                    dve.wait_ge(resid, TK * (t + 1))
                    dve.wait_ge(normed, TK * t)
                    norm_stats(dve, chain, rooted, t, x2[:, b, :, :], st, mv, dev[:, :], rstd[:, :], nmr[:, :]).then_inc(stats, 1)

                ctx_low(0, 0)
                ctx_low(0, 1)
                residual(0, 0)
                with dve.Fori(1, ST) as s:
                    ctx_low(s, 0)
                    residual(s - 1, 1)
                    ctx_low(s, 1)
                    residual(s, 0)
                residual(ST - 1, 1)


def feed_forward(nc, keep, scratch, out):
    gain = keep["gain_out"]
    SPLIT_AT = 11
    W2R = 4
    with ExitStack() as ctx:
        def sb(name, shape, dt=F32):
            return ctx.enter_context(nc.sbuf_tensor(name, shape, dt))

        def sem(name):
            return ctx.enter_context(nc.semaphore(name))

        w1 = sb("w1", [P, HC, 2, DC, P], F32R)
        w3 = sb("w3", [P, HC, 2, DC, P], F32R)
        w2 = sb("w2", [P, W2R, 2, D], F32R)
        h2 = sb("h2f", [P, 2, 2, DC, TOK], F32R)
        x2 = sb("x2f", [P, TK, D])
        sil = sb("sil", [P, TOK])
        hid = sb("hid", [P, TOK])
        gs = sb("gs", [P, 2, 2, TOK], F32R)
        fin = sb("fin", [P, 2, D])
        pg = ctx.enter_context(nc.psum_tensor("pg", [P, 2, TOK], F32))
        pl = ctx.enter_context(nc.psum_tensor("pl", [P, 2, TOK], F32))
        po = ctx.enter_context(nc.psum_tensor("pof", [P, TK, D], F32))

        w_in = [sem(f"f_w_in{h}") for h in range(HC)]
        w2_in = [sem(f"f_w2_in{i}") for i in range(W2R)]
        h_in = [sem(f"f_h_in{i}") for i in range(2)]
        h_hi = sem("f_h_hi")
        h_lo = sem("f_h_lo")
        x_in = sem("f_x_in")
        gate = sem("f_gate")
        lin = sem("f_lin")
        silu = sem("f_silu")
        prod = sem("f_prod")
        g_hi = sem("f_g_hi")
        g_lo = sem("f_g_lo")
        down = sem("f_down")
        scaled = sem("f_scaled")
        summed = sem("f_summed")
        stored = sem("f_stored")

        with nc.Block() as block:

            @block.sync
            def _(sp):
                def load_h(s, b, fresh=False):
                    if not fresh:
                        sp.wait_ge(lin, HC * (2 * s + b - 1))
                    sp.dma_start(raw(h2[:, b, LO, :, :]).rearrange("p c n -> p (c n)"),
                                 scratch["h2"][bass.ds(2 * s + b, 1)].rearrange("o p n -> (o p) n")
                                 ).then_inc(h_in[b], 16)

                def load_w2(n, h, fresh=False):
                    if not fresh:
                        sp.wait_ge(down, n - W2R + 1)
                    sp.dma_start(raw(w2[:, h % W2R, :, :]), scratch["w2"][h]).then_inc(w2_in[h % W2R], 16)

                load_h(0, 0, True)
                for h in range(HC):
                    sp.dma_start(raw(w1[:, h, :, :, :]).rearrange("p l c n -> p (l c n)"),
                                 scratch["w1"][h].rearrange("p l n -> p (l n)")).then_inc(w_in[h], 16)
                    sp.dma_start(raw(w3[:, h, :, :, :]).rearrange("p l c n -> p (l c n)"),
                                 scratch["w3"][h].rearrange("p l n -> p (l n)")).then_inc(w_in[h], 16)
                    if h < W2R:
                        load_w2(h, h, True)
                load_h(0, 1, True)

                def store(s, b):
                    sp.wait_ge(summed, TK * (2 * s + b + 1))
                    sp.dma_start(out[b].rearrange("(t k p) d -> t p k d", k=TK, p=P)[bass.ds(s, 1)].rearrange(
                        "o p k d -> (o p) k d"), x2[:, :, :]).then_inc(stored, 16)

                def tile(s, b, fresh=False, last=False):
                    t = 2 * s + b
                    for h in range(HC):
                        if not (fresh and h < W2R):
                            load_w2(HC * t + h, h)
                        if h == 2 + W2R and not fresh:
                            store(s - 1 + b, 1 - b)
                        if h == 3 + W2R:
                            if not fresh:
                                sp.wait_ge(stored, 16 * t)
                            sp.dma_start(x2[:, :, :].rearrange("p k d -> p (k d)"),
                                         scratch["x2"][bass.ds(t, 1)].rearrange("o p n -> (o p) n")
                                         ).then_inc(x_in, 16)
                        if h == 3 and not fresh and not last:
                            load_h(s + b, 1 - b)

                tile(0, 0, True)
                tile(0, 1)
                with sp.Fori(1, ST - 1) as s:
                    tile(s, 0)
                    tile(s, 1)
                tile(ST - 1, 0)
                tile(ST - 1, 1, last=True)
                store(ST - 1, 1)
                sp.wait_ge(stored, 16 * TILES)

            @block.tensor
            def _(pe):
                def up(t, s, b, h, fresh=False):
                    n = HC * t + h
                    if h == 0:
                        pe.wait_ge(h_hi, t + 1)
                        pe.wait_ge(h_lo, t + 1)
                    if fresh:
                        pe.wait_ge(w_in[h], 32)
                    if not (fresh and h < 2):
                        pe.wait_ge(silu, n - 1)
                        pe.wait_ge(prod, n - 1)
                    split_product(pe, pg[:, h % 2, :], lambda a, c: w1[:, h, a, c, :],
                                  lambda a, c: h2[:, b, a, c, :], range(DC)).then_inc(gate, 1)
                    split_product(pe, pl[:, h % 2, :], lambda a, c: w3[:, h, a, c, :],
                                  lambda a, c: h2[:, b, a, c, :], range(DC)).then_inc(lin, 1)

                def into_out(t, h):
                    n = HC * t + h
                    pe.wait_ge(g_hi, n + 1)
                    pe.wait_ge(g_lo, n + 1)
                    pe.wait_ge(w2_in[h % W2R], 16 * (HC // W2R * t + h // W2R + 1))
                    for k in range(TK):
                        if h == 0:
                            pe.wait_ge(scaled, TK * t - TK + k + 1) if not isinstance(t, int) or t else None
                        last = split_product(pe, po[:, k, :], lambda a, c: gs[:, h % 2, a, k * P:(k + 1) * P],
                                             lambda a, c: w2[:, h % W2R, a, :], range(1),
                                             start=(h == 0), stop=(h == HC - 1))
                    last.then_inc(down, 1)

                def tile(s, b, fresh=False, last=False):
                    t = 2 * s + b
                    for h in range(1, HC):
                        up(t, s, b, h, fresh)
                        into_out(t, h - 1)
                    if not last:
                        up(t + 1, s + b, 1 - b, 0)
                    into_out(t, HC - 1)

                up(0, 0, 0, 0, True)
                tile(0, 0, True)
                tile(0, 1)
                with pe.Fori(1, ST - 1) as s:
                    tile(s, 0)
                    tile(s, 1)
                tile(ST - 1, 0)
                tile(ST - 1, 1, last=True)

            @block.scalar
            def _(act):
                def tile(s, b, fresh=False, last=False):
                    t = 2 * s + b
                    for h in range(HC):
                        n = HC * t + h
                        act.wait_ge(gate, n + 1)
                        act.wait_ge(prod, n)
                        act.activation(sil[:, :], pg[:, h % 2, :], ACT.Silu).then_inc(silu, 1)
                        act.wait_ge(prod, n + 1)
                        if not (fresh and h < 2):
                            act.wait_ge(down, n - 1)
                        act.activation(gs[:, h % 2, HI, :], hid[:, :], ACT.Copy).then_inc(g_hi, 1)
                        if h == SPLIT_AT and not last:
                            high_part(s + b, 1 - b)

                def high_part(s, b):
                    act.wait_ge(h_in[b], 16 * (s + 1))
                    act.activation(h2[:, b, HI, :, :], raw(h2[:, b, LO, :, :]), ACT.Copy).then_inc(h_hi, 1)

                high_part(0, 0)
                tile(0, 0, True)
                tile(0, 1)
                with act.Fori(1, ST - 1) as s:
                    tile(s, 0)
                    tile(s, 1)
                tile(ST - 1, 0)
                tile(ST - 1, 1, last=True)

            @block.vector
            def _(dve):
                def finish(s, b):
                    t = 2 * s + b
                    dve.wait_ge(down, HC * (t + 1))
                    dve.wait_ge(x_in, 16 * (t + 1))
                    dve.wait_ge(g_lo, HC * (t + 1))
                    for k in range(TK):
                        dve.tensor_tensor(tmp(k), po[:, k, :], gain[:, b, :], ALU.mult).then_inc(scaled, 1)
                        dve.wait_ge(scaled, TK * t + k + 1)
                        dve.tensor_tensor(x2[:, k, :], tmp(k), x2[:, k, :], ALU.add).then_inc(summed, 1)

                def tmp(k):
                    return fin[:, k % 2, :]

                def low_part(s, b):
                    dve.wait_ge(h_hi, 2 * s + b + 1)
                    dve.tensor_tensor(h2[:, b, LO, :, :], raw(h2[:, b, LO, :, :]), h2[:, b, HI, :, :],
                                      ALU.subtract).then_inc(h_lo, 1)

                def tile(s, b, first=False, last=False):
                    t = 2 * s + b
                    for h in range(HC):
                        n = HC * t + h
                        dve.wait_ge(lin, n + 1)
                        dve.wait_ge(silu, n + 1)
                        dve.wait_ge(g_hi, n)
                        dve.wait_ge(g_lo, n)
                        dve.tensor_tensor(hid[:, :], sil[:, :], pl[:, h % 2, :], ALU.mult).then_inc(prod, 1)
                        dve.wait_ge(g_hi, n + 1)
                        dve.tensor_tensor(gs[:, h % 2, LO, :], hid[:, :], gs[:, h % 2, HI, :],
                                          ALU.subtract).then_inc(g_lo, 1)
                        if h == 0 and not first:
                            finish(s - 1 + b, 1 - b)
                        if h == SPLIT_AT and not last:
                            low_part(s + b, 1 - b)

                low_part(0, 0)
                tile(0, 0, True)
                tile(0, 1)
                with dve.Fori(1, ST - 1) as s:
                    tile(s, 0)
                    tile(s, 1)
                tile(ST - 1, 0)
                tile(ST - 1, 1, last=True)
                finish(ST - 1, 1)


def program(nc, x, wqkv, wproj, bproj, w1, w2, w3, c, wmod, identity, hadamard, out):
    ins = dict(x=x, wqkv=wqkv, wproj=wproj, bproj=bproj, w1=w1, w2=w2, w3=w3, c=c, wmod=wmod,
               identity=identity, hadamard=hadamard)

    def dram(name, shape, dt=F32):
        return nc.dram_tensor(name, shape, dt, kind="Internal").ap()

    scratch = {
        "q": dram("q_scratch", [2, HEADS * HD, S]),
        "k": dram("k_scratch", [2, HEADS * HD, S]),
        "v": dram("v_scratch", [HEADS, P, KT * HD]),
        "ctx": dram("ctx_scratch", [B, D, S]),
        "sum": dram("sum_scratch", [S]),
        "rec": dram("rec_scratch", [S]),
        "w1": dram("w1_scratch", [HC, P, 2, D]),
        "w3": dram("w3_scratch", [HC, P, 2, D]),
        "w2": dram("w2_scratch", [HC, P, 2, D]),
        "h2": dram("h2_scratch", [TILES, P, DC * TOK]),
        "x2": dram("x2_scratch", [TILES, P, TK * D]),
    }
    with ExitStack() as whole:
        keep = {}

        def sb(stack, name, shape, dt=F32):
            keep[name] = stack.enter_context(nc.sbuf_tensor(name, shape, dt))

        sb(whole, "ident", [P, P])
        sb(whole, "gain_out", [P, B, D])
        with ExitStack() as most:
            sb(most, "gains", [P, 2, B, D])
            sb(most, "wp", [P, 2, DC, D], F32R)
            sb(most, "shift", [P, 4, DC * B])
            sb(most, "scale1", [P, 4, DC * B])
            with ExitStack() as early:
                sb(early, "wqk", [P, 8, 2, DC, P], F32R)
                sb(early, "wv", [P, 2, DC, D], F32R)
                prepare(nc, ins, keep, scratch)
                project_qkv(nc, ins, keep, scratch)
            attend(nc, keep, scratch)
            project_out(nc, ins, keep, scratch)
        feed_forward(nc, keep, scratch, out)


_INS = ["L0_attn_query", "L0_attn_Wqkv", "L0_attn_Wproj", "L0_attn_bproj", "L0_ffn_W1", "L0_ffn_W2", "L0_ffn_W3",
        "L0_c", "L0_wmod"]


def kernel(**inputs):
    import numpy as _np
    import concourse.bacc as _bacc
    from concourse import mybir as _mybir
    from concourse.bass_utils import run_bass_kernel_spmd as _run

    nc = _bacc.Bacc("TRN2", target_bir_lowering=False, num_devices=1)
    arrays, args = {}, []
    given = [(n, inputs[n]) for n in _INS]
    n = _np.arange(128)
    bits = _np.array([[bin(i & j).count("1") & 1 for j in range(128)] for i in range(128)])
    given += [("identity", _np.eye(128, dtype=_np.float32)), ("hadamard", (1 - 2 * bits).astype(_np.float32))]
    for name, a in given:
        a = _np.ascontiguousarray(a)
        arrays[f"in_{name}_dram"] = a
        args.append(nc.dram_tensor(f"in_{name}_dram", a.shape, _mybir.dt.from_np(a.dtype), kind="ExternalInput").ap())
    out = nc.dram_tensor("out_0_dram", (2, 2048, 512), _mybir.dt.float32, kind="ExternalOutput").ap()
    program(nc, *args, out)
    r = _run(nc, [arrays], core_ids=[0])
    return r.results[0]["out_0_dram"]
```

```python
from contextlib import ExitStack

import concourse.bass as bass
from concourse import mybir

ALU = mybir.AluOpType
ACT = mybir.ActivationFunctionType
X = mybir.AxisListType.X
F32 = mybir.dt.float32
F32R = mybir.dt.float32r

P = 128
B, S, D = 2, 2048, 512
NH, HD = 16, 32
HID = 2048
DC = D // P
HC = HID // P
TK = 4
TOK = TK * P
ST = S // TOK
TILES = B * ST
HEADS = B * NH
KT = S // P
QJ = S // TOK
EPS = 1e-5
HI, LO = 0, 1
TERMS = ((HI, HI), (HI, LO), (LO, HI))
SA, CA, SB, CB, GA, GB = range(6)
WMOD_AT = {SA: 0, CA: 1, GA: 2, SB: 3, CB: 4, GB: 5}


def raw(ap):
    return ap.bitcast(F32)


def split_product(pe, out, stationary, moving, chunks, start=True, stop=True):
    last = None
    n = len(chunks) * len(TERMS)
    i = 0
    for c in chunks:
        for a, b in TERMS:
            last = pe.matmul(out, stationary(a, c), moving(b, c),
                             start=start and i == 0, stop=stop and i == n - 1)
            i += 1
    return last


def prepare(nc, ins, keep, scratch):
    ident, wqk, wv, wp, shift, scale1 = (keep[k] for k in ("ident", "wqk", "wv", "wp", "shift", "scale1"))
    NAT, FULL, OB, BANKS, PIECES, STAGES = 4, 4, 4, 6, 4, 4
    SHIFTS = (SA, CA, SB, CB)
    jobs = [("w2", "t", c) for c in range(HC)]
    jobs += [("rows", name, j) for name in "qkvp" for j in range(DC)]
    jobs += [("turn", "mod", 0)]
    jobs += [("had", "w2", c) for c in range(HC)]
    row_jobs = [n for n, j in enumerate(jobs) if j[0] == "rows"]
    first_row, turn_job = row_jobs[0], row_jobs[-1] + 1
    first_had = turn_job + 1

    def act_reads(n):
        kind, _, c = jobs[n]
        return {"w2": 1 - c % 2, "rows": 2, "turn": len(SHIFTS), "had": 1 - c % 2}[kind]

    def dve_reads(n):
        kind, _, c = jobs[n]
        return {"w2": c % 2, "rows": 0, "turn": 0, "had": c % 2}[kind]

    def act_until(n):
        return sum(act_reads(m) for m in range(n + 1))

    def dve_until(n):
        return sum(dve_reads(m) for m in range(n + 1))

    with ExitStack() as ctx:
        def sb(name, shape, dt=F32):
            return ctx.enter_context(nc.sbuf_tensor(name, shape, dt))

        def sem(name):
            return ctx.enter_context(nc.semaphore(name))

        had = sb("had", [P, P])
        nat = sb("nat", [P, NAT, D])
        full = sb("fullw", [P, FULL, D])
        w2a = sb("w2a", [P, HC, D])
        w2b = sb("w2b", [P, HC * D])
        wm = sb("wm", [P, 2, 6 * D])
        ob = sb("ob", [P, OB, D])
        ct = sb("ct", [P, DC, B])
        sc = sb("sc", [P, DC, HD])
        one = sb("one", [P, 1])
        mod = sb("mod", [P, D])
        graw = sb("graw", [2 * HD, D])
        gsign = sb("gsign", [2 * HD, D])
        gain = sb("gain", [2 * HD, D])
        gbias = sb("gbias", [2 * HD, D])
        bpb = sb("bpb", [2 * HD, D])
        ps = ctx.enter_context(nc.psum_tensor("ps_prep", [P, BANKS, D], F32))
        pmod = ctx.enter_context(nc.psum_tensor("ps_mod", [P, 2, D], F32))

        const_in = sem("p_const_in")
        ident_in = sem("p_ident_in")
        nat_in = [sem(f"p_nat_in{i}") for i in range(NAT)]
        w2_in = [sem(f"p_w2_in{i}") for i in range(PIECES)]
        wm_in = [sem(f"p_wm_in{i}") for i in range(2)]
        job_pe = sem("p_job_pe")
        job_act = sem("p_job_act")
        job_dve = sem("p_job_dve")
        row_low = sem("p_row_low")
        set_up = sem("p_set_up")
        silu_done = sem("p_silu")
        mod_mm = sem("p_mod_mm")
        mod_read = sem("p_mod_read")
        chain = sem("p_chain")
        gains_done = sem("p_gains_done")
        gains_out = sem("p_gains_out")
        fly = sem("p_butterfly")
        ob_out = [sem(f"p_ob_out{i}") for i in range(OB)]

        def target(n):
            _, name, j = jobs[n]
            if name in ("q", "k"):
                return [wqk[:, j + 4 * (name == "k"), s, :, :] for s in (HI, LO)]
            w = wv if name == "v" else wp
            return [w[:, s, :, j * P:(j + 1) * P] for s in (HI, LO)]

        def by_chunk(v):
            return v.rearrange("p (c m) -> p c m", c=DC)

        def w2_piece(i):
            return w2b[:, :].rearrange("p (t n) -> p t n", t=DC)[:, :, i * HID // PIECES:(i + 1) * HID // PIECES]

        with nc.Block() as block:

            @block.sync
            def _(sp):
                sp.dma_start(ident[:, :], ins["identity"]).then_inc(ident_in, 16)
                for i in range(PIECES):
                    sp.dma_start(w2_piece(i), ins["w2"].rearrange("(t p) n -> p t n", p=P)[
                        :, :, i * HID // PIECES:(i + 1) * HID // PIECES]).then_inc(w2_in[i], 16)

                def load_rows(m):
                    _, name, j = jobs[row_jobs[m]]
                    if m >= NAT:
                        sp.wait_ge(job_pe, row_jobs[m - NAT] + 1)
                    if name == "p":
                        sp.dma_start(nat[:, m % NAT, :], ins["wproj"][j * P:(j + 1) * P, :]).then_inc(nat_in[m % NAT], 16)
                    else:
                        src = ins["wqkv"].rearrange("(j h t d) n -> j t h d n", h=TK, t=3, d=HD)
                        sp.dma_start(nat[:, m % NAT, :], src[j, "qkv".index(name)]).then_inc(nat_in[m % NAT], 16)

                def load_mod(k):
                    if k >= 2:
                        sp.wait_ge(mod_mm, k - 1)
                    sp.dma_start(wm[:, k % 2, :], ins["wmod"][k * P:(k + 1) * P, :]).then_inc(wm_in[k % 2], 16)

                for m in range(NAT):
                    load_rows(m)
                sp.dma_start(had[:, :], ins["hadamard"]).then_inc(const_in, 16)
                with nc.allow_non_contiguous_dma("c is 1024 numbers"):
                    for b in range(B):
                        sp.dma_start(ct[:, :, b], ins["c"][b].rearrange("(k p) -> p k", p=P)).then_inc(const_in, 16)
                sp.dma_start(bpb[:, :], ins["bproj"].partition_broadcast(2 * HD)).then_inc(const_in, 16)
                load_mod(0)
                load_mod(1)
                for m in range(NAT, len(row_jobs)):
                    load_rows(m)
                load_mod(2)
                load_mod(3)
                for b in range(2):
                    load_tokens(sp, ins, keep["xin"], 0, b).then_inc(keep["x_in"][b], 16)
                sp.wait_ge(gains_done, 1)
                for i, rows in enumerate((gain[0:B, :], gbias[0:B, :], gain[HD:HD + B, :])):
                    sp.dma_start(scratch["gain"][i], rows).then_inc(gains_out, 16)
                sp.wait_ge(gains_out, 16 * 3)

            @block.tensor
            def _(pe):
                pe.wait_ge(ident_in, 16)
                for n, (kind, name, j) in enumerate(jobs):
                    m = n - BANKS
                    if kind == "turn":
                        pe.wait_ge(silu_done, 1)
                        for k in range(DC):
                            pe.wait_ge(wm_in[k % 2], 16 * (k // 2 + 1))
                            for i, kinds in enumerate((SHIFTS, (GA, GB))):
                                for g, x in enumerate(kinds):
                                    last = pe.matmul(pmod[g * HD:(g + 1) * HD, i, :], sc[:, k, :],
                                                     wm[:, k % 2, WMOD_AT[x] * D:(WMOD_AT[x] + 1) * D],
                                                     start=(k == 0), stop=(k == DC - 1))
                            last.then_inc(mod_mm, 1)
                        pe.wait_ge(mod_read, 1)
                    if m >= 0:
                        if act_reads(m):
                            pe.wait_ge(job_act, act_until(m))
                        if dve_reads(m):
                            pe.wait_ge(job_dve, dve_until(m))
                    bank = ps[:, n % BANKS, :]
                    if kind == "w2":
                        if j % (HC // PIECES) == 0:
                            pe.wait_ge(w2_in[j * PIECES // HC], 16)
                        for t in range(DC):
                            last = pe.transpose(by_chunk(bank)[:, t, :],
                                                w2b[:, t * HID + j * P:t * HID + (j + 1) * P], ident[:, :])
                    elif kind == "rows":
                        r = row_jobs.index(n)
                        pe.wait_ge(nat_in[r % NAT], 16 * (r // NAT + 1))
                        for c in range(DC):
                            last = pe.transpose(by_chunk(bank)[:, c, :], nat[:, r % NAT, c * P:(c + 1) * P], ident[:, :])
                    elif kind == "turn":
                        for c in range(DC):
                            last = pe.transpose(by_chunk(bank)[:, c, :], mod[:, c * P:(c + 1) * P], ident[:, :])
                    else:
                        if j == 0:
                            pe.wait_ge(const_in, 16 * 4)
                            pe.wait_ge(fly, 8)
                        last = pe.matmul(bank, had[:, :], w2a[:, j, :], start=True, stop=True)
                    last.then_inc(job_pe, 1)

            def transformed(eng, j):
                eng.wait_ge(job_pe, first_had + j + 1)
                if j >= OB:
                    eng.wait_ge(ob_out[j % OB], 16 * (j // OB))

            @block.scalar
            def _(act):
                for n in range(0, HC, 2):
                    act.wait_ge(job_pe, n + 1)
                    act.activation(w2a[:, n, :], ps[:, n % BANKS, :], ACT.Copy).then_inc(job_act, 1)
                act.wait_ge(const_in, 16 * 4)
                act.wait_ge(set_up, 2)
                act.activation(sc[:, :, 0:B], ct[:, :, :], ACT.Silu).then_inc(silu_done, 1)
                for r, n in enumerate(row_jobs):
                    src = ps[:, n % BANKS, :]
                    act.wait_ge(job_pe, n + 1)
                    act.activation(target(n)[HI], by_chunk(src), ACT.Copy).then_inc(job_act, 1)
                    if r >= FULL:
                        act.wait_ge(row_low, r - FULL + 1)
                    act.activation(full[:, r % FULL, :], src, ACT.Copy).then_inc(job_act, 1)
                act.wait_ge(mod_mm, DC)
                act.activation(mod[:, :], pmod[:, 0, :], ACT.Copy).then_inc(mod_read, 1)
                act.activation(graw[:, :], pmod[0:2 * HD, 1, :], ACT.Copy).then_inc(mod_read, 1)
                act.wait_ge(job_pe, turn_job + 1)
                for g, x in enumerate(SHIFTS):
                    src = by_chunk(ps[:, turn_job % BANKS, :])[:, :, g * HD:g * HD + B]
                    scale = x in (CA, CB)
                    dst = (scale1 if scale else shift)[:, x, :].rearrange("p (c b) -> p c b", b=B)
                    if scale:
                        act.activation(dst, src, ACT.Identity, bias=one[:, 0:1]).then_inc(job_act, 1)
                    else:
                        act.activation(dst, src, ACT.Copy).then_inc(job_act, 1)
                for j in range(0, HC, 2):
                    transformed(act, j)
                    act.activation(ob[:, j % OB, :], ps[:, (first_had + j) % BANKS, :], ACT.Copy,
                                   scale=HID ** -0.5).then_inc(job_act, 1)
                take_root(act, keep["chain"], keep["rooted"], 0, keep["dev"][:, :])

            @block.vector
            def _(dve):
                links = [0]

                def link(op):
                    links[0] += 1
                    op.then_inc(chain, 1)
                    dve.wait_ge(chain, links[0])

                def butterfly(m):
                    stage, minus = m // 2, m % 2
                    h = 1 << stage
                    src, dst = (w2a[:, :, :].rearrange("p c n -> p (c n)"), w2b[:, :])
                    if stage % 2:
                        src, dst = dst, src
                    src = src.rearrange("p (n t w) -> p t n w", t=2, w=h * D)
                    dst = dst.rearrange("p (n t w) -> p t n w", t=2, w=h * D)
                    if m:
                        dve.wait_ge(fly, m)
                    dve.tensor_tensor(dst[:, minus], src[:, 0], src[:, 1],
                                      ALU.subtract if minus else ALU.add).then_inc(fly, 1)

                dve.memset(sc[:, :, :], 0.0).then_inc(set_up, 1)
                dve.memset(one[:, :], 1.0).then_inc(set_up, 1)
                for n in range(1, HC, 2):
                    dve.wait_ge(job_pe, n + 1)
                    dve.tensor_copy(w2a[:, n, :], ps[:, n % BANKS, :]).then_inc(job_dve, 1)
                dve.wait_ge(job_act, act_until(first_row - 1))
                dve.wait_ge(job_dve, dve_until(first_row - 1))
                for m in range(2 * STAGES):
                    butterfly(m)
                dve.wait_ge(mod_read, 2)
                dve.wait_ge(const_in, 16 * 4)
                link(dve.tensor_scalar(gsign[:, :], graw[:, :], 0.0, 2.0, ALU.is_ge, ALU.mult))
                link(dve.scalar_tensor_tensor(out=graw[:, :], in0=gsign[:, :], scalar=-1.0, in1=graw[:, :],
                                              op0=ALU.add, op1=ALU.mult))
                link(dve.tensor_scalar(graw[:, :], graw[:, :], 0.25, None, ALU.max))
                link(dve.scalar_tensor_tensor(out=gain[:, :], in0=gsign[:, :], scalar=-1.0, in1=graw[:, :],
                                              op0=ALU.add, op1=ALU.mult))
                dve.tensor_tensor(gbias[:, :], gain[:, :], bpb[:, :], ALU.mult).then_inc(gains_done, 1)
                for j in range(1, HC, 2):
                    transformed(dve, j)
                    dve.tensor_scalar(ob[:, j % OB, :], ps[:, (first_had + j) % BANKS, :], HID ** -0.5, None,
                                      ALU.mult).then_inc(job_dve, 1)
                dve.wait_ge(keep["x_in"][0], 16)
                norm_stats(dve, keep["chain"], keep["rooted"], 0, keep["xin"][:, 0, :, :], keep["st"], keep["mv"],
                           keep["dev"][:, :], keep["rstd"][:, 0, :], keep["nmr"][:, 0, :]).then_inc(keep["stats"], 1)

            @block.gpsimd
            def _(pool):
                for r, n in enumerate(row_jobs):
                    pool.wait_ge(job_act, act_until(n))
                    hi, lo = target(n)
                    pool.tensor_tensor(lo, by_chunk(full[:, r % FULL, :]), hi, ALU.subtract).then_inc(row_low, 1)
                for j in range(HC):
                    if j % 2:
                        pool.wait_ge(job_dve, dve_until(first_had + j))
                    else:
                        pool.wait_ge(job_act, act_until(first_had + j))
                    pool.dma_start(scratch["w2"][j], ob[:, j % OB, :]).then_inc(ob_out[j % OB], 16)
                for i in range(OB):
                    pool.wait_ge(ob_out[i], 16 * (HC // OB))


def load_tokens(sp, ins, xin, s, b):
    return sp.dma_start(xin[:, b, :, :], ins["x"][b].rearrange("(t k p) d -> t p k d", k=TK, p=P)[
        bass.ds(s, 1)].rearrange("o p k d -> (o p) k d"))


def take_root(act, chain, rooted, t, dev):
    act.wait_ge(chain, LINKS * t + 3)
    act.activation(dev, dev, ACT.Sqrt).then_inc(rooted, 1)


LINKS = 4


def norm_stats(dve, chain, rooted, t, x, st, mv, dev, rstd, nmr):
    base = LINKS * t
    for k in range(TK):
        last = dve.bn_stats(st[:, k, :], x[:, k, :])
    last.then_inc(chain, 1)
    dve.wait_ge(chain, base + 1)
    dve.memset(dev, 0.0)
    for k in range(TK):
        last = dve.bn_aggr(mv[:, k, :], st[:, k, :])
    last.then_inc(chain, 1)
    dve.wait_ge(chain, base + 2)
    dve.tensor_scalar(dev, mv[:, :, 1], EPS, None, ALU.add).then_inc(chain, 1)
    dve.wait_ge(rooted, t + 1)
    dve.reciprocal(rstd, dev).then_inc(chain, 1)
    dve.wait_ge(chain, base + 4)
    return dve.scalar_tensor_tensor(out=nmr, in0=mv[:, :, 0], scalar=-1.0, in1=rstd, op0=ALU.mult, op1=ALU.mult)


def project_qkv(nc, ins, keep, scratch):
    ident, wqk, wv, shift, scale1 = (keep[k] for k in ("ident", "wqk", "wv", "shift", "scale1"))
    xin, st, mv, dev, rstd, nmr = (keep[k] for k in ("xin", "st", "mv", "dev", "rstd", "nmr"))
    x_in, chain, rooted, stats = (keep[k] for k in ("x_in", "chain", "rooted", "stats"))
    NQK = 8
    NJ = NQK + TK
    MID = 5
    BANKS = 4
    OB = 4
    with ExitStack() as ctx:
        def sb(name, shape, dt=F32):
            return ctx.enter_context(nc.sbuf_tensor(name, shape, dt))

        def sem(name):
            return ctx.enter_context(nc.semaphore(name))

        xn = sb("xn", [P, 2, TK, D])
        ht = sb("ht", [P, 2, 2, DC, TOK], F32R)
        full = sb("full", [P, DC, TOK])
        mark = sb("mark2", [P, 1])
        ob = sb("obq", [P, OB, 2, TOK], F32R)
        vst = sb("vst", [P, 2, NH, TK, HD])
        ps = ctx.enter_context(nc.psum_tensor("ps_qkv", [P, BANKS, TOK], F32))
        pt = ctx.enter_context(nc.psum_tensor("ps_ht", [P, DC, TOK], F32))

        normed = sem("a_normed")
        turned = sem("a_turned")
        h_hi = sem("a_h_hi")
        h_full = sem("a_h_full")
        h_lo = sem("a_h_lo")
        mm = sem("a_mm")
        out_hi = sem("a_out_hi")
        out_lo = sem("a_out_lo")
        ob_out = [sem(f"a_ob_out{i}") for i in range(OB)]
        v_out = [sem(f"a_v_out{i}") for i in range(2)]


        with nc.Block() as block:

            @block.sync
            def _(sp):
                def load(s, b):
                    sp.wait_ge(normed, TK * (2 * s + b - 1))
                    load_tokens(sp, ins, xin, s, b).then_inc(x_in[b], 16)

                def store(s, b):
                    for j in range(NQK):
                        sp.wait_ge(out_lo, NJ * (2 * s + b) + j + 1)
                        dst = scratch["q" if j < 4 else "k"]
                        r0 = b * NH * HD + (j % 4) * P
                        sp.dma_start(dst[:, r0:r0 + P, bass.ds(s * TOK, TOK)].rearrange("l r n -> r l n"),
                                     raw(ob[:, j % OB, :, :])).then_inc(ob_out[j % OB], 16)
                    sp.wait_ge(out_hi, NJ * (2 * s + b + 1))
                    sp.dma_start(scratch["v"][b * NH:(b + 1) * NH, :, bass.ds(s * TK * HD, TK * HD)].rearrange(
                        "g p n -> p g n"), vst[:, b, :, :, :].rearrange("p h k d -> p h (k d)")).then_inc(v_out[b], 16)

                with sp.Fori(0, ST - 1) as s:
                    load(s + 1, 0)
                    store(s, 0)
                    load(s + 1, 1)
                    store(s, 1)
                store(ST - 1, 0)
                store(ST - 1, 1)
                for i in range(OB):
                    sp.wait_ge(ob_out[i], 16 * 2 * TILES)
                for b in range(2):
                    sp.wait_ge(v_out[b], 16 * ST)

            @block.tensor
            def _(pe):
                def turn(s, b, fresh=False):
                    t = 2 * s + b
                    pe.wait_ge(normed, TK * (t + 1))
                    if not fresh:
                        pe.wait_ge(h_hi, DC * t)
                        pe.wait_ge(h_full, DC * t)
                    for c in range(DC):
                        for k in range(TK):
                            last = pe.transpose(pt[:, c, k * P:(k + 1) * P], xn[:, b, k, c * P:(c + 1) * P],
                                                ident[:, :])
                        last.then_inc(turned, 1)

                def results(s, b, j, fresh=False):
                    n = NJ * (2 * s + b) + j
                    if j == 0:
                        pe.wait_ge(h_hi, DC * (2 * s + b + 1))
                        pe.wait_ge(h_lo, DC * (2 * s + b + 1))
                    if not (fresh and j < BANKS):
                        pe.wait_ge(out_hi, n - BANKS + 1)
                        pe.wait_ge(out_lo, n - BANKS + 1)
                    if j < NQK:
                        last = split_product(pe, ps[:, j % BANKS, :], lambda a, c: wqk[:, j, a, c, :],
                                             lambda a, c: ht[:, b, a, c, :], range(DC))
                    else:
                        k = j - NQK
                        last = split_product(pe, ps[:, j % BANKS, :],
                                             lambda a, c: ht[:, b, a, c, k * P:(k + 1) * P],
                                             lambda a, c: wv[:, a, c, :], range(DC))
                    last.then_inc(mm, 1)

                def tile(s, b, nxt, fresh=False):
                    for j in range(NJ):
                        results(s, b, j, fresh)
                        if j == MID and nxt:
                            turn(*nxt)

                turn(0, 0, True)
                tile(0, 0, (0, 1), True)
                tile(0, 1, (1, 0))
                with pe.Fori(1, ST - 1) as s:
                    tile(s, 0, (s, 1))
                    tile(s, 1, (s + 1, 0))
                tile(ST - 1, 0, (ST - 1, 1))
                tile(ST - 1, 1, None)

            @block.scalar
            def _(act):
                def normalise(s, b, fresh=False):
                    t = 2 * s + b
                    if not (fresh and b == 0):
                        take_root(act, chain, rooted, t, dev[:, :])
                    act.wait_ge(stats, t + 1)
                    act.wait_ge(x_in[b], 16 * (s + 1))
                    if not fresh:
                        act.wait_ge(turned, DC * (t - 1))
                    for k in range(TK):
                        act.activation(xn[:, b, k, :], xin[:, b, k, :], ACT.Identity, bias=nmr[:, b, k:k + 1],
                                       scale=rstd[:, b, k:k + 1]).then_inc(normed, 1)

                def high_parts(s, b, fresh=False):
                    t = 2 * s + b
                    if not fresh:
                        act.wait_ge(mm, NJ * (t - 1))
                    for c in range(DC):
                        act.wait_ge(turned, DC * t + c + 1)
                        act.activation(ht[:, b, HI, c, :], pt[:, c, :], ACT.Identity,
                                       bias=shift[:, SA, B * c + b:B * c + b + 1],
                                       scale=scale1[:, CA, B * c + b:B * c + b + 1]).then_inc(h_hi, 1)

                def tile(s, b, nxt, fresh=False):
                    if nxt:
                        normalise(*nxt, fresh and b == 0)
                    for j in range(NJ):
                        n = NJ * (2 * s + b) + j
                        act.wait_ge(mm, n + 1)
                        if j < NQK:
                            if not (fresh and b == 0 and j < OB):
                                act.wait_ge(ob_out[j % OB], 16 * (2 * (2 * s + b) + j // OB))
                            act.activation(ob[:, j % OB, HI, :], ps[:, j % BANKS, :], ACT.Copy).then_inc(out_hi, 1)
                        else:
                            if j == NQK and not fresh:
                                act.wait_ge(v_out[b], 16 * s)
                            act.activation(vst[:, b, :, j - NQK, :],
                                           ps[:, j % BANKS, :].rearrange("p (h d) -> p h d", h=NH),
                                           ACT.Copy).then_inc(out_hi, 1)
                        if j == MID + 1 and nxt:
                            high_parts(*nxt, fresh and b == 0)

                normalise(0, 0, True)
                high_parts(0, 0, True)
                tile(0, 0, (0, 1), True)
                tile(0, 1, (1, 0), True)
                with act.Fori(1, ST - 1) as s:
                    tile(s, 0, (s, 1))
                    tile(s, 1, (s + 1, 0))
                tile(ST - 1, 0, (ST - 1, 1))
                tile(ST - 1, 1, None)

            @block.vector
            def _(dve):
                def measure(s, b, fresh=False):
                    t = 2 * s + b
                    dve.wait_ge(x_in[b], 16 * (s + 1))
                    if not fresh:
                        dve.wait_ge(normed, TK * (t - 1))
                    norm_stats(dve, chain, rooted, t, xin[:, b, :, :], st, mv, dev[:, :], rstd[:, b, :],
                               nmr[:, b, :]).then_inc(stats, 1)

                def low_parts(s, b, fresh=False):
                    t = 2 * s + b
                    for c in range(DC):
                        dve.wait_ge(h_hi, DC * t + c + 1)
                        dve.tensor_scalar(full[:, c, :], pt[:, c, :], scale1[:, CA, B * c + b:B * c + b + 1],
                                          shift[:, SA, B * c + b:B * c + b + 1], ALU.mult,
                                          ALU.add).then_inc(h_full, 1)
                    for c in range(DC):
                        dve.wait_ge(h_full, DC * t + c + 1)
                        dve.tensor_tensor(ht[:, b, LO, c, :], full[:, c, :], ht[:, b, HI, c, :],
                                          ALU.subtract).then_inc(h_lo, 1)

                def tile(s, b, nxt, fresh=False):
                    if nxt:
                        measure(*nxt, fresh and b == 0)
                    for j in range(NJ):
                        n = NJ * (2 * s + b) + j
                        dve.wait_ge(out_hi, n + 1)
                        if j < NQK:
                            dve.tensor_tensor(ob[:, j % OB, LO, :], ps[:, j % BANKS, :], ob[:, j % OB, HI, :],
                                              ALU.subtract).then_inc(out_lo, 1)
                        else:
                            dve.wait_ge(out_lo, n)
                            dve.memset(mark[:, :], 0.0).then_inc(out_lo, 1)
                        if j == MID + 1 and nxt:
                            low_parts(*nxt)

                low_parts(0, 0)
                tile(0, 0, (0, 1), True)
                tile(0, 1, (1, 0), True)
                with dve.Fori(1, ST - 1) as s:
                    tile(s, 0, (s, 1))
                    tile(s, 1, (s + 1, 0))
                tile(ST - 1, 0, (ST - 1, 1))
                tile(ST - 1, 1, None)


GROUPS = ((0, 1, 2, 3), (4, 5, 6, 7), (8, 9, 10, 11, 12))
ADDS = sum(len(g) - 1 for g in GROUPS)
SIDE = (13, 14, 15)
PIECES = QJ
SIDE_ADDS = (len(SIDE) - 1) * PIECES
SIDE_AT = (5, 5, 5, 6, 9, 10, 11, 13)
UNIT_ORDER = (0, 1, 2, "side")
UNITS = len(UNIT_ORDER)
STEPS = (["MqMqMqMqUM", "qMqqMqU", "MUqMqMqqU", "MqMqPMqMqM"] + ["PMqMqMqMqM"] * 4 + ["PMqMqMqMq"] * 6
         + ["PqqqqT", "PMqMqMqMqM"])
LAG = 3
LEAD = 3


def adds_until(kt):
    n = 0
    for g in GROUPS:
        for i, k in enumerate(g):
            n += i > 0
            if k == kt:
                return n + (i == 0)
    raise ValueError(kt)


def attend(nc, keep, scratch):
    ident = keep["ident"]
    SLOTS, RING, KR = 4, 8, 3 * HD
    NM = KT * QJ
    EARLY = STEPS[KT - 1].count("M")
    assert sum(x.count("M") for x in STEPS) == NM and sum(x.count("U") for x in STEPS) == UNITS
    MR = 3
    TURN_BANK = NM % MR
    SCALE = HD ** -0.5
    HALF = S // 2
    LOADS = 16 * 7
    with ExitStack() as ctx:
        def sb(name, shape, dt=F32):
            return ctx.enter_context(nc.sbuf_tensor(name, shape, dt))

        def sem(name):
            return ctx.enter_context(nc.semaphore(name))

        qst = sb("qst", [KR + 2, SLOTS, S], F32R)
        kst = sb("kst", [KR + 2, SLOTS, S], F32R)
        v = sb("v", [P, SLOTS, KT, HD])
        prob = sb("prob", [P, RING, S])
        gsum = sb("gsum", [P, len(GROUPS), S])
        ssum = sb("ssum", [P, S])
        ctxo = sb("ctxo", [P, 2, TOK])
        sumo = sb("sumo", [P, TOK])
        recb = sb("recb", [P, TOK])
        sumc = sb("sumc", [P, S // P])
        recc = sb("recc", [P, S // P])
        mxp = sb("mxp", [P, KT, QJ])
        mx = sb("mx", [P, KT])
        mrow = sb("mrow", [KT, 2, P], F32R)
        ones = sb("ones", [P, HD])
        mark = sb("mark3", [P, 11])
        pexp = ctx.enter_context(nc.psum_tensor("pexp", [P, 2, HALF], F32))
        pmax = ctx.enter_context(nc.psum_tensor("pmax", [P, MR, TOK], F32))
        pctx = ctx.enter_context(nc.psum_tensor("pctx", [P, TOK], F32))

        ones_set = sem("b_ones_set")
        stack_ones = sem("b_stack_ones")
        loaded = [sem(f"b_loaded{i}") for i in range(SLOTS)]
        scores = sem("b_scores")
        exp_done = sem("b_exp_done")
        mm_max = sem("b_mm_max")
        mx_done = sem("b_mx_done")
        mx_all = sem("b_mx_all")
        mx_turned = sem("b_mx_turned")
        m_split = sem("b_m_split")
        m_row = sem("b_m_row")
        pv_done = sem("b_pv_done")
        unit_done = sem("b_unit_done")
        add_done = sem("b_add_done")
        side_done = sem("b_side_done")
        ctx_read = sem("b_ctx_read")
        sum_read = sem("b_sum_read")
        divided = sem("b_divided")
        sum_out = sem("b_sum_out")
        sum_in = sem("b_sum_in")
        inverted = sem("b_inverted")
        rec_out = sem("b_rec_out")
        rec_in = sem("b_rec_in")
        last_inverted = sem("b_last_inverted")
        out_done = [sem(f"b_out_done{i}") for i in range(2)]
        OUTS = 16 * QJ

        def heads(eng, step):
            with eng.Fori(0, HEADS // SLOTS - 1) as i:
                for r in range(SLOTS):
                    step(i * SLOTS + r, i, r)
            i = HEADS // SLOTS - 1
            for r in range(SLOTS):
                step(i * SLOTS + r, i, r)

        def exists(g):
            return not isinstance(g, int) or g < HEADS

        with nc.Block() as block:

            @block.sync
            def _(sp):
                def load(g, slot):
                    rows = bass.ds(g * HD, HD)
                    q, k = scratch["q"], scratch["k"]
                    for r, part in enumerate((HI, LO, HI)):
                        sp.dma_start(raw(qst[r * HD:(r + 1) * HD, slot, :]), q[part, rows, :]).then_inc(loaded[slot], 16)
                    for r, part in enumerate((HI, HI, LO)):
                        sp.dma_start(raw(kst[r * HD:(r + 1) * HD, slot, :]), k[part, rows, :]).then_inc(loaded[slot], 16)
                    sp.dma_start(v[:, slot, :, :].rearrange("p k d -> p (k d)"),
                                 scratch["v"][bass.ds(g, 1)].rearrange("o p n -> (o p) n")).then_inc(loaded[slot], 16)

                def max_row(g, slot):
                    sp.wait_ge(m_split, 2 * (g + 1))
                    for part in (HI, LO):
                        r = KR + part
                        sp.dma_start(raw(qst[r:r + 1, slot, :]).rearrange("o (t n) -> o t n", t=KT),
                                     raw(mrow[:, part, :])).then_inc(m_row, 16)

                def invert(g):
                    sp.wait_ge(sum_read, g + 2)
                    sp.dma_start(scratch["sum"].rearrange("(j n) -> j n", j=QJ), sumo[0:P:HD, :]).then_inc(sum_out, 16)
                    sp.wait_ge(sum_out, 16 * (g + 2))
                    sp.dma_start(sumc[:, :], scratch["sum"].rearrange("(p n) -> p n", p=P)).then_inc(sum_in, 16)
                    sp.wait_ge(inverted, g + 1)
                    sp.dma_start(scratch["rec"].rearrange("(p n) -> p n", p=P), recc[:, :]).then_inc(rec_out, 16)
                    sp.wait_ge(rec_out, 16 * (g + 1))
                    sp.wait_ge(divided, g + 2)
                    for j in range(QJ):
                        sp.dma_start(recb[j * HD:(j + 1) * HD, :], scratch["rec"][j * TOK:(j + 1) * TOK]
                                     .partition_broadcast(HD)).then_inc(rec_in, 16)

                def store(g, par, pair):
                    sp.wait_ge(divided, g + 3)
                    for j in range(QJ):
                        sp.dma_start(scratch["ctx"][par, bass.ds(pair * HD, HD), j * TOK:(j + 1) * TOK],
                                     ctxo[j * HD:(j + 1) * HD, par, :]).then_inc(out_done[par], 16)

                def step(g, i, r):
                    static = isinstance(g, int)
                    par = r % 2
                    if not static or g + 3 < HEADS:
                        sp.wait_ge(pv_done, RING + KT * g)
                        load(g + 3, (r + 3) % SLOTS)
                    if not static or g >= 2:
                        store(g - 2, par, i * 2 + r // 2 - 1)
                    if not static or g >= 1:
                        invert(g - 1)
                    if not static or g + 1 < HEADS:
                        max_row(g + 1, (r + 1) % SLOTS)

                for g in range(3):
                    load(g, g)
                max_row(0, 0)
                for r in range(SLOTS):
                    step(r, 0, r)
                with sp.Fori(1, HEADS // SLOTS - 1) as i:
                    for r in range(SLOTS):
                        step(i * SLOTS + r, i, r)
                i = HEADS // SLOTS - 1
                for r in range(SLOTS):
                    step(i * SLOTS + r, i, r)
                store(HEADS - 2, 0, NH - 1)
                store(HEADS - 1, 1, NH - 1)
                for par in range(2):
                    sp.wait_ge(out_done[par], 16 + OUTS * HEADS // 2)

            @block.tensor
            def _(pe):
                def maximum(g, slot, u, fresh=False):
                    qt, kc = u // QJ, u % QJ
                    if u >= MR:
                        pe.wait_ge(mx_done, g * NM + u - MR + 1)
                    elif not fresh:
                        pe.wait_ge(mx_done, g * NM)
                    if u == TURN_BANK and not fresh:
                        pe.wait_ge(m_split, 2 * g)
                    pe.matmul(pmax[:, u % MR, :], qst[0:KR, slot, qt * P:(qt + 1) * P],
                              kst[0:KR, slot, kc * TOK:(kc + 1) * TOK], start=True, stop=True).then_inc(mm_max, 1)

                def turn_max(g):
                    pe.wait_ge(mx_all, g + 1)
                    pe.transpose(pmax[0:KT, TURN_BANK, 0:P], mx[:, :], ident[:, :]).then_inc(mx_turned, 1)

                def score(g, slot, kt, half, j):
                    if j == 0:
                        if kt == 0 and half == 0:
                            pe.wait_ge(m_row, 32 * (g + 1))
                        pe.wait_ge(exp_done, 2 * KT * g + 2 * kt + half + 1)
                    q0 = half * HALF + j * TOK
                    pe.matmul(pexp[:, half, j * TOK:(j + 1) * TOK], kst[:, slot, kt * P:(kt + 1) * P],
                              qst[:, slot, q0:q0 + TOK], start=True, stop=True).then_inc(scores, 1)

                def weigh(g, slot, kt):
                    pe.wait_ge(exp_done, 2 * KT * g + 2 * kt + 4)
                    if kt == 0:
                        pe.wait_ge(sum_read, g + 1)
                    for j in range(QJ):
                        last = pe.matmul(pctx[j * HD:(j + 1) * HD, :], v[:, slot, kt, :],
                                         prob[:, kt % RING, j * TOK:(j + 1) * TOK], start=(kt == 0), stop=(kt == KT - 1))
                    last.then_inc(pv_done, 1)

                def unit(g, n):
                    k = UNIT_ORDER[n]
                    if n == 0:
                        pe.wait_ge(ctx_read, g + 2)
                    if k == "side":
                        pe.wait_ge(side_done, SIDE_ADDS * (g + 2))
                        src = ssum[:, :]
                    else:
                        pe.wait_ge(add_done, ADDS + ADDS * g + adds_until(GROUPS[k][-1]))
                        src = gsum[:, k, :]
                    for j in range(QJ):
                        last = pe.matmul(pctx[j * HD:(j + 1) * HD, :], ones[:, :], src[:, j * TOK:(j + 1) * TOK],
                                         start=(n == 0), stop=(n == UNITS - 1))
                    last.then_inc(unit_done, 1)

                def run(g, r, kts, ahead, far, closing):
                    u = sum(STEPS[kt].count("M") for kt in range(kts[0])) + EARLY
                    n = 0
                    for kt in kts:
                        q = v = 0
                        for x in STEPS[kt]:
                            if x == "q":
                                score(g, r, kt, q // 2, q % 2)
                                q += 1
                            elif x == "P":
                                weigh(g, r, kt - LAG)
                            elif x == "U" and closing:
                                unit(g - 1, n)
                                n += 1
                            elif x == "T" and ahead:
                                turn_max(g + 1)
                            elif x == "M" and kt == KT - 1 and far:
                                maximum(g + 2, (r + 2) % SLOTS, v)
                                v += 1
                            elif x == "M" and kt < KT - 1 and ahead:
                                maximum(g + 1, (r + 1) % SLOTS, u)
                                u += 1

                def step(g, i, r):
                    if exists(g + 2):
                        pe.wait_ge(loaded[(r + 2) % SLOTS], LOADS * (i + 1 + (r + 2) // SLOTS))
                    run(g, r, range(LEAD, KT), exists(g + 1), exists(g + 2), False)
                    for kt in range(KT - LAG, KT):
                        weigh(g, r, kt)
                    if exists(g + 1):
                        run(g + 1, (r + 1) % SLOTS, range(LEAD), exists(g + 2), False, True)
                    else:
                        for n in range(UNITS):
                            unit(g, n)

                pe.wait_ge(loaded[0], LOADS)
                for u in range(NM):
                    maximum(0, 0, u, True)
                turn_max(0)
                pe.wait_ge(loaded[1], LOADS)
                for u in range(EARLY):
                    maximum(1, 1, u)
                pe.wait_ge(ones_set, 1)
                pe.wait_ge(stack_ones, 1)
                run(0, 0, range(LEAD), True, False, False)
                heads(pe, step)

            @block.scalar
            def _(act):
                def exps(g, kts):
                    for kt in kts:
                        act.wait_ge(pv_done, KT * g + kt + 1)
                        old = (kt - RING) % KT
                        back = 0 if kt >= RING else 1
                        if old in SIDE:
                            act.wait_ge(side_done, SIDE_ADDS * (g + 1 - back) + PIECES * max(SIDE.index(old), 1))
                        else:
                            act.wait_ge(add_done, ADDS + ADDS * g - ADDS * back + adds_until(old))
                        for half in range(2):
                            act.wait_ge(scores, QJ * (KT * g + kt) + 2 * half + 2)
                            act.activation(prob[:, kt % RING, half * HALF:(half + 1) * HALF], pexp[:, half, :],
                                           ACT.Exp, scale=SCALE).then_inc(exp_done, 1)

                def step(g, i, r):
                    par = r % 2
                    exps(g, range(LEAD, KT))
                    act.wait_ge(out_done[par], 16 + OUTS * (2 * i + r // 2))
                    act.wait_ge(pv_done, RING + KT * (g + 1))
                    act.activation(ctxo[:, par, :], pctx[:, :], ACT.Copy).then_inc(ctx_read, 1)
                    if exists(g + 1):
                        exps(g + 1, range(LEAD))
                    act.wait_ge(unit_done, UNITS + UNITS * (g + 1))
                    act.wait_ge(sum_out, 16 + 16 * g)
                    act.activation(sumo[:, :], pctx[:, :], ACT.Copy).then_inc(sum_read, 1)

                exps(0, range(LEAD))
                heads(act, step)

            @block.vector
            def _(dve):
                dve.memset(ones[:, :], 1.0).then_inc(ones_set, 1)
                credits = ((exp_done, 2), (pv_done, RING), (unit_done, UNITS), (add_done, ADDS),
                           (side_done, SIDE_ADDS), (ctx_read, 1),
                           (sum_read, 1), (divided, 2), (sum_out, 16), (out_done[0], 16), (out_done[1], 16))
                for i, (free, n) in enumerate(credits):
                    dve.memset(mark[:, i:i + 1], 0.0).then_inc(free, n)

                def invert(g):
                    dve.wait_ge(sum_in, 16 * (g + 1))
                    dve.wait_ge(rec_out, 16 * g)
                    dve.reciprocal(recc[:, :], sumc[:, :]).then_inc(inverted, 1)

                def side_add(g, n):
                    m, piece = n // PIECES + 1, n % PIECES
                    cols = slice(piece * S // PIECES, (piece + 1) * S // PIECES)
                    if piece == 0:
                        dve.wait_ge(exp_done, 2 * KT * g + 2 * SIDE[m] + 4)
                    if n == 0:
                        dve.wait_ge(unit_done, UNITS * g + UNIT_ORDER.index("side") + 1)
                    if m > 1:
                        dve.wait_ge(side_done, SIDE_ADDS * (g + 1) + n - PIECES + 1)
                    a = prob[:, SIDE[0] % RING, cols] if m == 1 else ssum[:, cols]
                    dve.tensor_tensor(ssum[:, cols], a, prob[:, SIDE[m] % RING, cols], ALU.add).then_inc(side_done, 1)

                def maxima(g, old=None):
                    for u in range(NM):
                        if old is not None:
                            for n, at in enumerate(SIDE_AT):
                                if at == u:
                                    side_add(old, n)
                        if u == NM // 2 and old is not None:
                            invert(old)
                        dve.wait_ge(mm_max, g * NM + u + 1)
                        dve.tensor_reduce(mxp[:, u // QJ, u % QJ:u % QJ + 1], pmax[:, u % MR, :], X,
                                          ALU.max).then_inc(mx_done, 1)
                    dve.wait_ge(mx_done, (g + 1) * NM)
                    dve.tensor_reduce(mx[:, :], mxp[:, :, :], X, ALU.max).then_inc(mx_all, 1)
                    dve.wait_ge(mx_turned, g + 1)
                    dve.wait_ge(m_row, 32 * g)
                    dve.tensor_scalar(mrow[:, HI, :], pmax[0:KT, TURN_BANK, 0:P], -1.0, None, ALU.mult).then_inc(m_split, 1)
                    dve.wait_ge(m_split, 2 * g + 1)
                    dve.scalar_tensor_tensor(out=mrow[:, LO, :], in0=pmax[0:KT, TURN_BANK, 0:P], scalar=-1.0,
                                             in1=mrow[:, HI, :], op0=ALU.mult, op1=ALU.subtract).then_inc(m_split, 1)

                maxima(0)
                maxima(1)
                maxima(2, 0)
                with dve.Fori(3, HEADS) as g:
                    maxima(g, g - 2)
                for n in range(SIDE_ADDS):
                    side_add(HEADS - 2, n)
                invert(HEADS - 2)
                for n in range(SIDE_ADDS):
                    side_add(HEADS - 1, n)
                dve.wait_ge(sum_read, HEADS + 1)
                dve.wait_ge(divided, HEADS + 1)
                dve.reciprocal(recb[:, :], sumo[:, :]).then_inc(last_inverted, 1)

            @block.gpsimd
            def _(pool):
                def head(g):
                    n = 0
                    for k, grp in enumerate(GROUPS):
                        dst = gsum[:, k, :]
                        pool.wait_ge(unit_done, UNITS * g + UNIT_ORDER.index(k) + 1)
                        for m, kt in enumerate(grp[1:]):
                            pool.wait_ge(exp_done, 2 * KT * g + 2 * kt + 4)
                            a = prob[:, grp[0] % RING, :] if m == 0 else dst
                            if m:
                                pool.wait_ge(add_done, ADDS + ADDS * g + n)
                            pool.tensor_tensor(dst, a, prob[:, kt % RING, :], ALU.add).then_inc(add_done, 1)
                            n += 1

                def divide(g, n, par):
                    if isinstance(g, int) and g == HEADS - 1:
                        pool.wait_ge(last_inverted, 1)
                    else:
                        pool.wait_ge(rec_in, 16 * QJ * (g + 1))
                    pool.wait_ge(ctx_read, g + 2)
                    pool.tensor_tensor(ctxo[:, par, :], ctxo[:, par, :], recb[:, :], ALU.mult).then_inc(divided, 1)

                pool.memset(kst[KR:KR + 2, :, :].bitcast(F32), 1.0).then_inc(stack_ones, 1)
                head(0)
                with pool.Fori(0, HEADS // 2 - 1) as n:
                    head(2 * n + 1)
                    divide(2 * n, n, 0)
                    head(2 * n + 2)
                    divide(2 * n + 1, n, 1)
                head(HEADS - 1)
                divide(HEADS - 2, HEADS // 2 - 1, 0)
                divide(HEADS - 1, HEADS // 2 - 1, 1)


def project_out(nc, ins, keep, scratch):
    ident, wp, shift, scale1 = (keep[k] for k in ("ident", "wp", "shift", "scale1"))
    with ExitStack() as ctx:
        def sb(name, shape, dt=F32):
            return ctx.enter_context(nc.sbuf_tensor(name, shape, dt))

        def sem(name):
            return ctx.enter_context(nc.semaphore(name))

        gains = sb("gains", [P, 2, B, D])
        cin = sb("cin", [P, 2, DC, TOK])
        cs = sb("cs", [P, 2, 2, DC, TOK], F32R)
        xin = sb("xin2", [P, 2, TK, D])
        x2 = sb("x2", [P, 2, TK, D])
        xn = sb("xn2", [P, 2, TK, D])
        h2 = sb("h2", [P, 2, DC, TOK])
        st = sb("st2", [P, TK, 6])
        mv = sb("mv2", [P, TK, 2])
        dev = sb("dev2", [P, TK])
        rstd = sb("rstd2", [P, 2, TK])
        nmr = sb("nmr2", [P, 2, TK])
        po = ctx.enter_context(nc.psum_tensor("po", [P, TK, D], F32))
        pt = ctx.enter_context(nc.psum_tensor("pt2", [P, DC, TOK], F32))

        ctx_in = [sem(f"c_ctx_in{i}") for i in range(2)]
        x_in = [sem(f"c_x_in{i}") for i in range(2)]
        gains_in = sem("c_gains_in")
        c_hi = sem("c_ctx_hi")
        c_lo = sem("c_ctx_lo")
        x_bias = sem("c_x_bias")
        mm = sem("c_mm")
        scaled = sem("c_scaled")
        resid = sem("c_resid")
        chain = sem("c_chain")
        rooted = sem("c_rooted")
        stats = sem("c_stats")
        normed = sem("c_normed")
        turned = sem("c_turned")
        h_done = sem("c_h_done")
        x2_out = [sem(f"c_x2_out{i}") for i in range(2)]
        h2_out = [sem(f"c_h2_out{i}") for i in range(2)]


        def tiles(eng, step, first, last):
            with eng.Fori(first // 2, last // 2) as s:
                step(s, 0)
                step(s, 1)

        with nc.Block() as block:

            @block.sync
            def _(sp):
                def load_ctx(s, b, fresh=False):
                    if not fresh:
                        sp.wait_ge(c_lo, DC * (2 * s + b - 1))
                    sp.dma_start(cin[:, b, :, :], scratch["ctx"][b].rearrange("(c p) n -> p c n", p=P)[
                        :, :, bass.ds(s * TOK, TOK)]).then_inc(ctx_in[b], 16)

                def load_x(s, b, fresh=False):
                    if not fresh:
                        sp.wait_ge(resid, TK * (2 * s + b - 1))
                    sp.dma_start(xin[:, b, :, :], ins["x"][b].rearrange("(t k p) d -> t p k d", k=TK, p=P)[
                        bass.ds(s, 1)].rearrange("o p k d -> (o p) k d")).then_inc(x_in[b], 16)

                def store_x2(s, b):
                    t = 2 * s + b
                    sp.wait_ge(resid, TK * (t + 1))
                    sp.dma_start(scratch["x2"][bass.ds(t, 1)].rearrange("o p n -> (o p) n"),
                                 x2[:, b, :, :].rearrange("p k d -> p (k d)")).then_inc(x2_out[b], 16)

                def store_h2(s, b):
                    t = 2 * s + b
                    sp.wait_ge(h_done, DC * (t + 1))
                    sp.dma_start(scratch["h2"][bass.ds(t, 1)].rearrange("o p n -> (o p) n"),
                                 h2[:, b, :, :].rearrange("p c n -> p (c n)")).then_inc(h2_out[b], 16)

                for b in range(2):
                    load_ctx(0, b, True)
                for b in range(2):
                    load_x(0, b, True)
                    if b == 0:
                        sp.dma_start(gains[:, :, :, :].rearrange("p i b n -> p (i b n)"), scratch["gain"][0:2].rearrange(
                            "i b n -> (i b n)").partition_broadcast(P)).then_inc(gains_in, 16)
                for b in range(2):
                    load_ctx(1, b)
                for b in range(2):
                    store_x2(0, b)
                    load_x(1, b)
                with sp.Fori(1, ST - 1) as s:
                    for b in range(2):
                        load_ctx(s + 1, b)
                        store_x2(s, b)
                        load_x(s + 1, b)
                        store_h2(s - 1, b)
                for b in range(2):
                    store_x2(ST - 1, b)
                    store_h2(ST - 2, b)
                for b in range(2):
                    store_h2(ST - 1, b)
                for b in range(2):
                    sp.wait_ge(x2_out[b], 16 + 16 * ST)
                    sp.wait_ge(h2_out[b], 16 + 16 * ST)

            @block.tensor
            def _(pe):
                def project(s, b, first=False):
                    t = 2 * s + b
                    pe.wait_ge(c_hi, DC * (t + 1))
                    pe.wait_ge(c_lo, DC * (t + 1))
                    for k in range(TK):
                        if not first:
                            pe.wait_ge(scaled, TK * t + k + 1 - TK)
                        split_product(pe, po[:, k, :], lambda a, c: cs[:, b, a, c, k * P:(k + 1) * P],
                                      lambda a, c: wp[:, a, c, :], range(DC)).then_inc(mm, 1)

                def turn(s, b, first=False):
                    t = 2 * s + b
                    pe.wait_ge(normed, TK * (t + 1))
                    if not first:
                        pe.wait_ge(h_done, DC * t)
                    for c in range(DC):
                        for k in range(TK):
                            last = pe.transpose(pt[:, c, k * P:(k + 1) * P], xn[:, b, k, c * P:(c + 1) * P], ident[:, :])
                        last.then_inc(turned, 1)

                def step(s, b, first=False):
                    project(s, b)
                    turn(s - 1, b, first)

                project(0, 0, True)
                project(0, 1)
                step(1, 0, True)
                step(1, 1)
                tiles(pe, step, 4, TILES)
                turn(ST - 1, 0)
                turn(ST - 1, 1)

            @block.gpsimd
            def _(pool):
                def step(s, b):
                    pool.wait_ge(x_in[b], 16 * (s + 1))
                    for k in range(TK):
                        pool.tensor_tensor(xin[:, b, k, :], xin[:, b, k, :], gains[:, 1, b, :],
                                           ALU.add).then_inc(x_bias, 1)

                pool.wait_ge(gains_in, 16)
                tiles(pool, step, 0, TILES)

            @block.scalar
            def _(act):
                def ctx_high(s, b, fresh=False):
                    t = 2 * s + b
                    if not fresh:
                        act.wait_ge(mm, TK * (t - 1))
                    act.wait_ge(ctx_in[b], 16 * (s + 1))
                    for c in range(DC):
                        act.activation(cs[:, b, HI, c, :], cin[:, b, c, :], ACT.Copy).then_inc(c_hi, 1)

                def normalise(s, b, fresh=False):
                    t = 2 * s + b
                    take_root(act, chain, rooted, t, dev[:, :])
                    act.wait_ge(stats, t + 1)
                    if not fresh:
                        act.wait_ge(turned, DC * (t - 1))
                    for k in range(TK):
                        act.activation(xn[:, b, k, :], x2[:, b, k, :], ACT.Identity, bias=nmr[:, b, k:k + 1],
                                       scale=rstd[:, b, k:k + 1]).then_inc(normed, 1)

                def high_parts(s, b):
                    t = 2 * s + b
                    act.wait_ge(h2_out[b], 16 + 16 * s)
                    for c in range(DC):
                        act.wait_ge(turned, DC * t + c + 1)
                        act.activation(h2[:, b, c, :], pt[:, c, :], ACT.Identity,
                                       bias=shift[:, SB, B * c + b:B * c + b + 1],
                                       scale=scale1[:, CB, B * c + b:B * c + b + 1]).then_inc(h_done, 1)

                def step(s, b):
                    ctx_high(s + 1, b)
                    high_parts(s - 1, b)
                    normalise(s, b)

                for b in range(2):
                    ctx_high(0, b, True)
                for b in range(2):
                    ctx_high(1, b)
                    normalise(0, b, True)
                tiles(act, step, 2, TILES - 2)
                for b in range(2):
                    high_parts(ST - 2, b)
                    normalise(ST - 1, b)
                for b in range(2):
                    high_parts(ST - 1, b)

            @block.vector
            def _(dve):
                for b in range(2):
                    dve.memset(nmr[:, b, 0:1], 0.0).then_inc(x2_out[b], 16)
                    dve.memset(nmr[:, b, 1:2], 0.0).then_inc(h2_out[b], 16)

                def ctx_low(s, b):
                    t = 2 * s + b
                    for c in range(DC):
                        dve.wait_ge(c_hi, DC * t + c + 1)
                        dve.tensor_tensor(cs[:, b, LO, c, :], cin[:, b, c, :], cs[:, b, HI, c, :],
                                          ALU.subtract).then_inc(c_lo, 1)

                def residual(s, b, fresh=False):
                    t = 2 * s + b
                    dve.wait_ge(x2_out[b], 16 + 16 * s)
                    if not fresh:
                        dve.wait_ge(normed, TK * (t - 1))
                    for k in range(TK):
                        dve.wait_ge(mm, TK * t + k + 1)
                        dve.tensor_tensor(x2[:, b, k, :], po[:, k, :], gains[:, 0, b, :],
                                          ALU.mult).then_inc(scaled, 1)
                    for k in range(TK):
                        dve.wait_ge(scaled, TK * t + k + 1)
                        dve.wait_ge(x_bias, TK * t + k + 1)
                        dve.tensor_tensor(x2[:, b, k, :], x2[:, b, k, :], xin[:, b, k, :],
                                          ALU.add).then_inc(resid, 1)
                    dve.wait_ge(resid, TK * (t + 1))
                    norm_stats(dve, chain, rooted, t, x2[:, b, :, :], st, mv, dev[:, :], rstd[:, b, :],
                               nmr[:, b, :]).then_inc(stats, 1)

                def step(s, b, fresh=False):
                    residual(s, b, fresh)
                    ctx_low(s + 1, b)

                ctx_low(0, 0)
                ctx_low(0, 1)
                dve.wait_ge(gains_in, 16)
                step(0, 0, True)
                step(0, 1, True)
                tiles(dve, step, 2, TILES - 2)
                residual(ST - 1, 0)
                residual(ST - 1, 1)


def feed_forward(nc, ins, keep, scratch, out):
    ident = keep["ident"]
    SPLIT_AT = 11
    W2R = 4
    with ExitStack() as ctx:
        def sb(name, shape, dt=F32):
            return ctx.enter_context(nc.sbuf_tensor(name, shape, dt))

        def sem(name):
            return ctx.enter_context(nc.semaphore(name))

        gain = sb("gain_out", [P, B, D])
        w1 = sb("w1", [P, HC, 2, DC, P], F32R)
        w3 = sb("w3", [P, HC, 2, DC, P], F32R)
        w2 = sb("w2", [P, W2R, 2, D], F32R)
        h2 = sb("h2f", [P, 2, 2, DC, TOK], F32R)
        x2 = sb("x2f", [P, TK, D])
        sil = sb("sil", [P, TOK])
        hid = sb("hid", [P, TOK])
        gs = sb("gs", [P, 2, 2, TOK], F32R)
        fin = sb("fin", [P, 2, D])
        pg = ctx.enter_context(nc.psum_tensor("pg", [P, 2, TOK], F32))
        pl = ctx.enter_context(nc.psum_tensor("pl", [P, 2, TOK], F32))
        po = ctx.enter_context(nc.psum_tensor("pof", [P, TK, D], F32))

        nat_in = [sem(f"f_nat_in{i}") for i in range(2)]
        w_turned = sem("f_w_turned")
        w_hi = sem("f_w_hi")
        w_lo = sem("f_w_lo")
        w2_in = [sem(f"f_w2_in{i}") for i in range(W2R)]
        gain_in = sem("f_gain_in")
        w2_hi = sem("f_w2_hi")
        w2_lo = sem("f_w2_lo")
        h_in = [sem(f"f_h_in{i}") for i in range(2)]
        h_hi = sem("f_h_hi")
        h_lo = sem("f_h_lo")
        x_in = sem("f_x_in")
        gate = sem("f_gate")
        lin = sem("f_lin")
        silu = sem("f_silu")
        prod = sem("f_prod")
        g_hi = sem("f_g_hi")
        g_lo = sem("f_g_lo")
        down = sem("f_down")
        scaled = sem("f_scaled")
        summed = sem("f_summed")
        stored = sem("f_stored")

        with nc.Block() as block:

            @block.sync
            def _(sp):
                def load_h(s, b, fresh=False):
                    if not fresh:
                        sp.wait_ge(lin, HC * (2 * s + b - 1))
                    sp.dma_start(raw(h2[:, b, LO, :, :]).rearrange("p c n -> p (c n)"),
                                 scratch["h2"][bass.ds(2 * s + b, 1)].rearrange("o p n -> (o p) n")
                                 ).then_inc(h_in[b], 16)

                def load_w2(n, h, fresh=False):
                    if not fresh:
                        sp.wait_ge(down, n - W2R + 1)
                    sp.dma_start(raw(w2[:, h % W2R, LO, :]), scratch["w2"][h]).then_inc(w2_in[h % W2R], 16)

                def load_rows(m):
                    if m >= 2:
                        sp.wait_ge(w_turned, 2 * (m - 1))
                    for i, w in enumerate(("w1", "w3")):
                        sp.dma_start(x2[:, 2 * (m % 2) + i, :], ins[w][m * P:(m + 1) * P, :]).then_inc(nat_in[m % 2], 16)

                load_rows(0)
                load_h(0, 0, True)
                load_rows(1)
                load_w2(0, 0, True)
                load_w2(1, 1, True)
                load_rows(2)
                load_w2(2, 2, True)
                load_rows(3)
                load_w2(3, 3, True)
                load_h(0, 1, True)
                sp.dma_start(gain[:, :, :].rearrange("p b n -> p (b n)"), scratch["gain"][2].rearrange(
                    "b n -> (b n)").partition_broadcast(P)).then_inc(gain_in, 16)

                def store(s, b):
                    sp.wait_ge(summed, TK * (2 * s + b + 1))
                    sp.dma_start(out[b].rearrange("(t k p) d -> t p k d", k=TK, p=P)[bass.ds(s, 1)].rearrange(
                        "o p k d -> (o p) k d"), x2[:, :, :]).then_inc(stored, 16)

                def tile(s, b, fresh=False, last=False):
                    t = 2 * s + b
                    for h in range(HC):
                        if not (fresh and h < W2R):
                            load_w2(HC * t + h, h)
                        if h == 2 + W2R and not fresh:
                            store(s - 1 + b, 1 - b)
                        if fresh and h >= W2R:
                            load_rows(h)
                        if h == 3 + W2R and not fresh:
                            sp.wait_ge(stored, 16 * t)
                            load_x2(t)
                        if h == 3 and not fresh and not last:
                            load_h(s + b, 1 - b)

                def load_x2(t):
                    sp.dma_start(x2[:, :, :].rearrange("p k d -> p (k d)"),
                                 scratch["x2"][bass.ds(t, 1)].rearrange("o p n -> (o p) n")).then_inc(x_in, 16)

                tile(0, 0, True)
                sp.wait_ge(w_turned, 2 * HC)
                load_x2(0)
                tile(0, 1)
                with sp.Fori(1, ST - 1) as s:
                    tile(s, 0)
                    tile(s, 1)
                tile(ST - 1, 0)
                tile(ST - 1, 1, last=True)
                store(ST - 1, 1)
                sp.wait_ge(stored, 16 * TILES)

            @block.tensor
            def _(pe):
                def up(t, s, b, h, fresh=False):
                    n = HC * t + h
                    if h == 0:
                        pe.wait_ge(h_hi, t + 1)
                        pe.wait_ge(h_lo, t + 1)
                    if fresh:
                        pe.wait_ge(w_hi, 2 * (h + 1))
                        pe.wait_ge(w_lo, 2 * (h + 1))
                    else:
                        pe.wait_ge(silu, n - 1)
                        pe.wait_ge(prod, n - 1)
                    split_product(pe, pg[:, h % 2, :], lambda a, c: w1[:, h, a, c, :],
                                  lambda a, c: h2[:, b, a, c, :], range(DC)).then_inc(gate, 1)
                    split_product(pe, pl[:, h % 2, :], lambda a, c: w3[:, h, a, c, :],
                                  lambda a, c: h2[:, b, a, c, :], range(DC)).then_inc(lin, 1)

                def turn_rows(m):
                    pe.wait_ge(nat_in[m % 2], 32 * (m // 2 + 1))
                    if m >= 2:
                        pe.wait_ge(silu, m - 1)
                        pe.wait_ge(prod, m - 1)
                    for i, bank in enumerate((pg, pl)):
                        for c in range(DC):
                            last = pe.transpose(bank[:, m % 2, c * P:(c + 1) * P],
                                                x2[:, 2 * (m % 2) + i, c * P:(c + 1) * P], ident[:, :])
                        last.then_inc(w_turned, 1)

                def into_out(t, h, first=False):
                    n = HC * t + h
                    pe.wait_ge(g_hi, n + 1)
                    pe.wait_ge(g_lo, n + 1)
                    pe.wait_ge(w2_lo, n + 1)
                    for k in range(TK):
                        if h == 0 and not first:
                            pe.wait_ge(scaled, TK * t - TK + k + 1)
                        last = split_product(pe, po[:, k, :], lambda a, c: gs[:, h % 2, a, k * P:(k + 1) * P],
                                             lambda a, c: w2[:, h % W2R, a, :], range(1),
                                             start=(h == 0), stop=(h == HC - 1))
                    last.then_inc(down, 1)

                def tile(s, b, fresh=False, last=False):
                    t = 2 * s + b
                    for h in range(1, HC):
                        up(t, s, b, h, fresh)
                        if fresh and h + 1 < HC:
                            turn_rows(h + 1)
                        into_out(t, h - 1, fresh)
                    if not last:
                        up(t + 1, s + b, 1 - b, 0)
                    into_out(t, HC - 1)

                turn_rows(0)
                turn_rows(1)
                up(0, 0, 0, 0, True)
                tile(0, 0, True)
                tile(0, 1)
                with pe.Fori(1, ST - 1) as s:
                    tile(s, 0)
                    tile(s, 1)
                tile(ST - 1, 0)
                tile(ST - 1, 1, last=True)

            @block.scalar
            def _(act):
                def tile(s, b, fresh=False, last=False):
                    t = 2 * s + b
                    for h in range(HC):
                        n = HC * t + h
                        act.wait_ge(gate, n + 1)
                        act.wait_ge(prod, n)
                        act.activation(sil[:, :], pg[:, h % 2, :], ACT.Silu).then_inc(silu, 1)
                        if fresh and 1 <= h < HC - 1:
                            weights_high(h + 1)
                        act.wait_ge(prod, n + 1)
                        if not (fresh and h < 2):
                            act.wait_ge(down, n - 1)
                        act.activation(gs[:, h % 2, HI, :], hid[:, :], ACT.Copy).then_inc(g_hi, 1)
                        if h < HC - 1:
                            w2_high(t, h + 1)
                        elif not last:
                            w2_high(t + 1, 0)
                        if h == SPLIT_AT and not last:
                            high_part(s + b, 1 - b)

                def w2_high(t, h):
                    act.wait_ge(w2_in[h % W2R], 16 * (HC // W2R * t + h // W2R + 1))
                    act.activation(w2[:, h % W2R, HI, :], raw(w2[:, h % W2R, LO, :]), ACT.Copy).then_inc(w2_hi, 1)

                def high_part(s, b):
                    act.wait_ge(h_in[b], 16 * (s + 1))
                    act.activation(h2[:, b, HI, :, :], raw(h2[:, b, LO, :, :]), ACT.Copy).then_inc(h_hi, 1)

                def weights_high(m):
                    for i, (w, bank) in enumerate(((w1, pg), (w3, pl))):
                        act.wait_ge(w_turned, 2 * m + i + 1)
                        act.activation(w[:, m, HI, :, :], bank[:, m % 2, :].rearrange("p (c n) -> p c n", c=DC),
                                       ACT.Copy).then_inc(w_hi, 1)

                weights_high(0)
                high_part(0, 0)
                weights_high(1)
                w2_high(0, 0)
                tile(0, 0, True)
                tile(0, 1)
                with act.Fori(1, ST - 1) as s:
                    tile(s, 0)
                    tile(s, 1)
                tile(ST - 1, 0)
                tile(ST - 1, 1, last=True)

            @block.vector
            def _(dve):
                def finish(s, b):
                    t = 2 * s + b
                    dve.wait_ge(down, HC * (t + 1))
                    dve.wait_ge(x_in, 16 * (t + 1))
                    dve.wait_ge(g_lo, HC * (t + 1))
                    for k in range(TK):
                        dve.tensor_tensor(tmp(k), po[:, k, :], gain[:, b, :], ALU.mult).then_inc(scaled, 1)
                        dve.wait_ge(scaled, TK * t + k + 1)
                        dve.tensor_tensor(x2[:, k, :], tmp(k), x2[:, k, :], ALU.add).then_inc(summed, 1)

                def tmp(k):
                    return fin[:, k % 2, :]

                def w2_low(t, h):
                    dve.wait_ge(w2_hi, HC * t + h + 1)
                    dve.tensor_tensor(w2[:, h % W2R, LO, :], raw(w2[:, h % W2R, LO, :]), w2[:, h % W2R, HI, :],
                                      ALU.subtract).then_inc(w2_lo, 1)

                def low_part(s, b):
                    dve.wait_ge(h_hi, 2 * s + b + 1)
                    dve.tensor_tensor(h2[:, b, LO, :, :], raw(h2[:, b, LO, :, :]), h2[:, b, HI, :, :],
                                      ALU.subtract).then_inc(h_lo, 1)

                def tile(s, b, first=False, last=False):
                    t = 2 * s + b
                    for h in range(HC):
                        n = HC * t + h
                        dve.wait_ge(lin, n + 1)
                        dve.wait_ge(silu, n + 1)
                        dve.wait_ge(g_hi, n)
                        dve.wait_ge(g_lo, n)
                        dve.tensor_tensor(hid[:, :], sil[:, :], pl[:, h % 2, :], ALU.mult).then_inc(prod, 1)
                        if first and 1 <= h < HC - 1:
                            weights_low(h + 1)
                        dve.wait_ge(g_hi, n + 1)
                        dve.tensor_tensor(gs[:, h % 2, LO, :], hid[:, :], gs[:, h % 2, HI, :],
                                          ALU.subtract).then_inc(g_lo, 1)
                        if h < HC - 1:
                            w2_low(t, h + 1)
                        elif not last:
                            w2_low(t + 1, 0)
                        if h == 0 and not first:
                            finish(s - 1 + b, 1 - b)
                        if h == SPLIT_AT and not last:
                            low_part(s + b, 1 - b)

                def weights_low(m):
                    for i, (w, bank) in enumerate(((w1, pg), (w3, pl))):
                        dve.wait_ge(w_hi, 2 * m + i + 1)
                        dve.tensor_tensor(w[:, m, LO, :, :], bank[:, m % 2, :].rearrange("p (c n) -> p c n", c=DC),
                                          w[:, m, HI, :, :], ALU.subtract).then_inc(w_lo, 1)

                weights_low(0)
                low_part(0, 0)
                weights_low(1)
                w2_low(0, 0)
                dve.wait_ge(gain_in, 16)
                tile(0, 0, True)
                tile(0, 1)
                with dve.Fori(1, ST - 1) as s:
                    tile(s, 0)
                    tile(s, 1)
                tile(ST - 1, 0)
                tile(ST - 1, 1, last=True)
                finish(ST - 1, 1)


def program(nc, x, wqkv, wproj, bproj, w1, w2, w3, c, wmod, identity, hadamard, out):
    ins = dict(x=x, wqkv=wqkv, wproj=wproj, bproj=bproj, w1=w1, w2=w2, w3=w3, c=c, wmod=wmod,
               identity=identity, hadamard=hadamard)

    def dram(name, shape, dt=F32):
        return nc.dram_tensor(name, shape, dt, kind="Internal").ap()

    scratch = {
        "q": dram("q_scratch", [2, HEADS * HD, S]),
        "k": dram("k_scratch", [2, HEADS * HD, S]),
        "v": dram("v_scratch", [HEADS, P, KT * HD]),
        "ctx": dram("ctx_scratch", [B, D, S]),
        "sum": dram("sum_scratch", [S]),
        "rec": dram("rec_scratch", [S]),
        "w2": dram("w2_scratch", [HC, P, D]),
        "gain": dram("gain_scratch", [3, B, D]),
        "h2": dram("h2_scratch", [TILES, P, DC * TOK]),
        "x2": dram("x2_scratch", [TILES, P, TK * D]),
    }
    with ExitStack() as whole:
        keep = {}

        def sb(stack, name, shape, dt=F32):
            keep[name] = stack.enter_context(nc.sbuf_tensor(name, shape, dt))

        sb(whole, "ident", [P, P])
        with ExitStack() as most:
            sb(most, "wp", [P, 2, DC, D], F32R)
            sb(most, "shift", [P, 4, DC * B])
            sb(most, "scale1", [P, 4, DC * B])
            with ExitStack() as early:
                sb(early, "wqk", [P, 8, 2, DC, P], F32R)
                sb(early, "wv", [P, 2, DC, D], F32R)
                sb(early, "xin", [P, 2, TK, D])
                sb(early, "st", [P, TK, 6])
                sb(early, "mv", [P, TK, 2])
                sb(early, "dev", [P, TK])
                sb(early, "rstd", [P, 2, TK])
                sb(early, "nmr", [P, 2, TK])
                keep["x_in"] = [early.enter_context(nc.semaphore(f"a_x_in{i}")) for i in range(2)]
                for name in ("chain", "rooted", "stats"):
                    keep[name] = early.enter_context(nc.semaphore("a_" + name))
                prepare(nc, ins, keep, scratch)
                project_qkv(nc, ins, keep, scratch)
            attend(nc, keep, scratch)
            project_out(nc, ins, keep, scratch)
        feed_forward(nc, ins, keep, scratch, out)


_INS = ["L0_attn_query", "L0_attn_Wqkv", "L0_attn_Wproj", "L0_attn_bproj", "L0_ffn_W1", "L0_ffn_W2", "L0_ffn_W3",
        "L0_c", "L0_wmod"]


def kernel(**inputs):
    import numpy as _np
    import concourse.bacc as _bacc
    from concourse import mybir as _mybir
    from concourse.bass_utils import run_bass_kernel_spmd as _run

    nc = _bacc.Bacc("TRN2", target_bir_lowering=False, num_devices=1)
    arrays, args = {}, []
    given = [(n, inputs[n]) for n in _INS]
    n = _np.arange(128)
    bits = _np.array([[bin(i & j).count("1") & 1 for j in range(128)] for i in range(128)])
    given += [("identity", _np.eye(128, dtype=_np.float32)), ("hadamard", (1 - 2 * bits).astype(_np.float32))]
    for name, a in given:
        a = _np.ascontiguousarray(a)
        arrays[f"in_{name}_dram"] = a
        args.append(nc.dram_tensor(f"in_{name}_dram", a.shape, _mybir.dt.from_np(a.dtype), kind="ExternalInput").ap())
    out = nc.dram_tensor("out_0_dram", (2, 2048, 512), _mybir.dt.float32, kind="ExternalOutput").ap()
    program(nc, *args, out)
    r = _run(nc, [arrays], core_ids=[0])
    return r.results[0]["out_0_dram"]
```
